# Optimizing a Trainium2 kernel written in Bass

```python
import numpy as np
import jax
import jax.numpy as jnp

def _softmax(x, axis=-1):
    return jax.nn.softmax(x, axis=axis)

def _gelu(x):
    return jax.nn.gelu(x, approximate=True)

def _silu(x):
    return jax.nn.silu(x)

def _sigmoid(x):
    return jax.nn.sigmoid(x)

def _layernorm(x, axis=-1, eps=1e-05):
    m = jnp.mean(x, axis=axis, keepdims=True)
    v = jnp.var(x, axis=axis, keepdims=True)
    return (x - m) / jnp.sqrt(v + eps)

def _scatter_add(tgt, idx, src, axis=0):
    return tgt.at[idx].add(src)

def _segment_sum(src, seg, n):
    return jax.ops.segment_sum(src, seg, n)
kernel_name = 'mk_hybrid_d1_jaxref_r8_3af3a9'

def setup_inputs(seed: int=0):
    np.random.seed(seed)
    _w = jnp.asarray

    def _L0_attn_a_setup():
        import jax, jax.numpy as jnp
        import numpy as np
        D_MODEL = 128
        N_HEADS = 16
        HEAD_DIM = D_MODEL // N_HEADS
        KV_LATENT = 32
        LN_EPS = 1e-05

        def apply_rope(x):
            b, h, t, d = x.shape
            half = d // 2
            pos = jnp.arange(t, dtype=x.dtype)[:, None]
            inv_freq = 1.0 / 10000.0 ** (jnp.arange(half, dtype=x.dtype) / half)
            angles = pos * inv_freq[None, :]
            sin = jnp.sin(angles)[None, None]
            cos = jnp.cos(angles)[None, None]
            x1, x2 = (x[..., :half], x[..., half:])
            return jnp.concatenate([x1 * cos - x2 * sin, x1 * sin + x2 * cos], axis=-1)
        key = jax.random.key(seed)
        ks = jax.random.split(key, 6)
        d, L = (D_MODEL, KV_LATENT)
        s = 1.0 / np.sqrt(d)
        sl = 1.0 / np.sqrt(L)
        return {'x': jax.random.normal(ks[0], (2, 256, d), dtype=jnp.float32), 'W_q': jax.random.uniform(ks[1], (d, d), jnp.float32, -s, s), 'W_dkv': jax.random.uniform(ks[2], (d, L), jnp.float32, -s, s), 'W_uk': jax.random.uniform(ks[3], (L, d), jnp.float32, -sl, sl), 'W_uv': jax.random.uniform(ks[4], (L, d), jnp.float32, -sl, sl), 'W_o': jax.random.uniform(ks[5], (d, d), jnp.float32, -s, s), 'ln_gamma': jnp.ones((L,), jnp.float32), 'ln_beta': jnp.zeros((L,), jnp.float32)}
    _L0_attn_a_in = _L0_attn_a_setup()

    def _L0_attn_b_setup():
        import jax, jax.numpy as jnp
        import numpy as np
        N_POWER_ITERS = 10

        def _spectral_normalize(W):
            u = jnp.ones((W.shape[0],), W.dtype) / jnp.sqrt(jnp.asarray(W.shape[0], W.dtype))

            def body(u, _):
                v = W.T @ u
                v = v / (jnp.linalg.norm(v) + 1e-12)
                u = W @ v
                u = u / (jnp.linalg.norm(u) + 1e-12)
                return (u, None)
            u, _ = jax.lax.scan(body, u, None, length=N_POWER_ITERS)
            u = jax.lax.stop_gradient(u)
            v = W.T @ u
            v = jax.lax.stop_gradient(v / (jnp.linalg.norm(v) + 1e-12))
            sigma = u @ (W @ v)
            return W / sigma

        def _reference_tuple_inner(x, W_A, W_B, W_C):
            A = _spectral_normalize(W_A)
            Bw = _spectral_normalize(W_B)
            C = _spectral_normalize(W_C)
            xb = jnp.einsum('bti,hi->bth', x, Bw)
            h0 = jnp.zeros((x.shape[0], A.shape[0]), x.dtype)

            def step(h, xb_t):
                h = h @ A.T + xb_t
                return (h, h)
            _, hs = jax.lax.scan(step, h0, jnp.swapaxes(xb, 0, 1))
            hs = jnp.swapaxes(hs, 0, 1)
            ys = jnp.einsum('bth,oh->bto', hs, C)
            return (ys, hs)
        key = jax.random.key(seed)
        k1, k2, k3, k4 = jax.random.split(key, 4)
        B, T, D_in, H, D_out = (32, 128, 128, 128, 128)
        x = jax.random.normal(k1, (B, T, D_in), dtype=jnp.float32)
        W_A = jax.random.normal(k2, (H, H), dtype=jnp.float32) * (1.0 / np.sqrt(H))
        W_B = jax.random.normal(k3, (H, D_in), dtype=jnp.float32) * (1.0 / np.sqrt(D_in))
        W_C = jax.random.normal(k4, (D_out, H), dtype=jnp.float32) * (1.0 / np.sqrt(H))
        return {'x': x, 'W_A': W_A, 'W_B': W_B, 'W_C': W_C}
    _L0_attn_b_in = _L0_attn_b_setup()

    def _L0_ffn_setup():
        import jax, jax.numpy as jnp
        import numpy as np
        DIM = 128
        INTER = 176
        N_EXPERTS = 16
        TOPK = 2
        N_SHARED = 2
        SHARED_INTER = N_SHARED * INTER
        ROUTE_SCALE = 1.0
        key = jax.random.key(seed)
        ks = jax.random.split(key, 16)
        s = 0.02
        return {'x': jax.random.normal(ks[0], (2, 256, DIM), dtype=jnp.float32), 'gate_w': jax.random.normal(ks[1], (DIM, N_EXPERTS), dtype=jnp.float32) * s, 'gate_b': jnp.zeros((N_EXPERTS,), dtype=jnp.float32), 'w1': jax.random.normal(ks[2], (N_EXPERTS, DIM, INTER), dtype=jnp.float32) * s, 'b1': jnp.zeros((N_EXPERTS, INTER), dtype=jnp.float32), 'w3': jax.random.normal(ks[3], (N_EXPERTS, DIM, INTER), dtype=jnp.float32) * s, 'b3': jnp.zeros((N_EXPERTS, INTER), dtype=jnp.float32), 'w2': jax.random.normal(ks[4], (N_EXPERTS, INTER, DIM), dtype=jnp.float32) * s, 'b2': jnp.zeros((N_EXPERTS, DIM), dtype=jnp.float32), 'sw1': jax.random.normal(ks[5], (DIM, SHARED_INTER), dtype=jnp.float32) * s, 'sb1': jax.random.normal(ks[6], (SHARED_INTER,), dtype=jnp.float32) * s, 'sw3': jax.random.normal(ks[7], (DIM, SHARED_INTER), dtype=jnp.float32) * s, 'sb3': jax.random.normal(ks[8], (SHARED_INTER,), dtype=jnp.float32) * s, 'sw2': jax.random.normal(ks[9], (SHARED_INTER, DIM), dtype=jnp.float32) * s, 'sb2': jax.random.normal(ks[10], (DIM,), dtype=jnp.float32) * s}
    _L0_ffn_in = _L0_ffn_setup()
    _d = {'L0_attn_a_x': _L0_attn_a_in['x'], 'L0_attn_a_W_q': _L0_attn_a_in['W_q'], 'L0_attn_a_W_dkv': _L0_attn_a_in['W_dkv'], 'L0_attn_a_W_uk': _L0_attn_a_in['W_uk'], 'L0_attn_a_W_uv': _L0_attn_a_in['W_uv'], 'L0_attn_a_W_o': _L0_attn_a_in['W_o'], 'L0_attn_a_ln_gamma': _L0_attn_a_in['ln_gamma'], 'L0_attn_a_ln_beta': _L0_attn_a_in['ln_beta'], 'L0_attn_b_W_A': _L0_attn_b_in['W_A'], 'L0_attn_b_W_B': _L0_attn_b_in['W_B'], 'L0_attn_b_W_C': _L0_attn_b_in['W_C'], 'L0_ffn_gate_w': _L0_ffn_in['gate_w'], 'L0_ffn_gate_b': _L0_ffn_in['gate_b'], 'L0_ffn_w1': _L0_ffn_in['w1'], 'L0_ffn_b1': _L0_ffn_in['b1'], 'L0_ffn_w3': _L0_ffn_in['w3'], 'L0_ffn_b3': _L0_ffn_in['b3'], 'L0_ffn_w2': _L0_ffn_in['w2'], 'L0_ffn_b2': _L0_ffn_in['b2'], 'L0_ffn_sw1': _L0_ffn_in['sw1'], 'L0_ffn_sb1': _L0_ffn_in['sb1'], 'L0_ffn_sw3': _L0_ffn_in['sw3'], 'L0_ffn_sb3': _L0_ffn_in['sb3'], 'L0_ffn_sw2': _L0_ffn_in['sw2'], 'L0_ffn_sb2': _L0_ffn_in['sb2']}
    _x0 = _d['L0_attn_a_x']
    _d['L0_attn_a_x'] = jax.random.normal(jax.random.fold_in(jax.random.key(seed), 1), (4, 1024, 128), dtype=_x0.dtype)
    del _x0
    return _d

def reference(L0_attn_a_x, L0_attn_a_W_q, L0_attn_a_W_dkv, L0_attn_a_W_uk, L0_attn_a_W_uv, L0_attn_a_W_o, L0_attn_a_ln_gamma, L0_attn_a_ln_beta, L0_attn_b_W_A, L0_attn_b_W_B, L0_attn_b_W_C, L0_ffn_gate_w, L0_ffn_gate_b, L0_ffn_w1, L0_ffn_b1, L0_ffn_w3, L0_ffn_b3, L0_ffn_w2, L0_ffn_b2, L0_ffn_sw1, L0_ffn_sb1, L0_ffn_sw3, L0_ffn_sb3, L0_ffn_sw2, L0_ffn_sb2):

    def _L0_attn_a_ref(x, W_q, W_dkv, W_uk, W_uv, W_o, ln_gamma, ln_beta):
        import jax, jax.numpy as jnp
        import numpy as np
        D_MODEL = 128
        N_HEADS = 16
        HEAD_DIM = D_MODEL // N_HEADS
        KV_LATENT = 32
        LN_EPS = 1e-05

        def apply_rope(x):
            b, h, t, d = x.shape
            half = d // 2
            pos = jnp.arange(t, dtype=x.dtype)[:, None]
            inv_freq = 1.0 / 10000.0 ** (jnp.arange(half, dtype=x.dtype) / half)
            angles = pos * inv_freq[None, :]
            sin = jnp.sin(angles)[None, None]
            cos = jnp.cos(angles)[None, None]
            x1, x2 = (x[..., :half], x[..., half:])
            return jnp.concatenate([x1 * cos - x2 * sin, x1 * sin + x2 * cos], axis=-1)
        b, t, _ = x.shape
        q = (x @ W_q).reshape(b, t, N_HEADS, HEAD_DIM).transpose(0, 2, 1, 3)
        lat = x @ W_dkv
        mu = jnp.mean(lat, axis=-1, keepdims=True)
        var = jnp.mean(jnp.square(lat - mu), axis=-1, keepdims=True)
        lat = (lat - mu) * jax.lax.rsqrt(var + LN_EPS) * ln_gamma + ln_beta
        k = (lat @ W_uk).reshape(b, t, N_HEADS, HEAD_DIM).transpose(0, 2, 1, 3)
        v = (lat @ W_uv).reshape(b, t, N_HEADS, HEAD_DIM).transpose(0, 2, 1, 3)
        q = apply_rope(q)
        k = apply_rope(k)
        scores = jnp.einsum('bhqd,bhkd->bhqk', q, k) / jnp.sqrt(jnp.float32(HEAD_DIM))
        causal = jnp.tril(jnp.ones((t, t), dtype=bool))
        scores = jnp.where(causal[None, None], scores, -jnp.inf)
        attn = jax.nn.softmax(scores, axis=-1)
        out = jnp.einsum('bhqk,bhkd->bhqd', attn, v)
        out = out.transpose(0, 2, 1, 3).reshape(b, t, D_MODEL)
        return out @ W_o

    def _L0_attn_b_ref(x, W_A, W_B, W_C):
        import jax, jax.numpy as jnp
        import numpy as np
        N_POWER_ITERS = 10

        def _spectral_normalize(W):
            u = jnp.ones((W.shape[0],), W.dtype) / jnp.sqrt(jnp.asarray(W.shape[0], W.dtype))

            def body(u, _):
                v = W.T @ u
                v = v / (jnp.linalg.norm(v) + 1e-12)
                u = W @ v
                u = u / (jnp.linalg.norm(u) + 1e-12)
                return (u, None)
            u, _ = jax.lax.scan(body, u, None, length=N_POWER_ITERS)
            u = jax.lax.stop_gradient(u)
            v = W.T @ u
            v = jax.lax.stop_gradient(v / (jnp.linalg.norm(v) + 1e-12))
            sigma = u @ (W @ v)
            return W / sigma

        def _reference_tuple_inner(x, W_A, W_B, W_C):
            A = _spectral_normalize(W_A)
            Bw = _spectral_normalize(W_B)
            C = _spectral_normalize(W_C)
            xb = jnp.einsum('bti,hi->bth', x, Bw)
            h0 = jnp.zeros((x.shape[0], A.shape[0]), x.dtype)

            def step(h, xb_t):
                h = h @ A.T + xb_t
                return (h, h)
            _, hs = jax.lax.scan(step, h0, jnp.swapaxes(xb, 0, 1))
            hs = jnp.swapaxes(hs, 0, 1)
            ys = jnp.einsum('bth,oh->bto', hs, C)
            return (ys, hs)
        return _reference_tuple_inner(x, W_A, W_B, W_C)[0]

    def _L0_ffn_ref(x, gate_w, gate_b, w1, b1, w3, b3, w2, b2, sw1, sb1, sw3, sb3, sw2, sb2):
        import jax, jax.numpy as jnp
        import numpy as np
        DIM = 128
        INTER = 176
        N_EXPERTS = 16
        TOPK = 2
        N_SHARED = 2
        SHARED_INTER = N_SHARED * INTER
        ROUTE_SCALE = 1.0
        shape = x.shape
        xf = x.reshape(-1, DIM)
        logits = xf @ gate_w + gate_b
        scores = jax.nn.softmax(logits.astype(jnp.float32), axis=-1)
        top_vals, top_idx = jax.lax.top_k(scores, TOPK)
        weights = (top_vals * ROUTE_SCALE).astype(x.dtype)
        cw = (jax.nn.one_hot(top_idx, N_EXPERTS, dtype=x.dtype) * weights[..., None]).sum(axis=1)
        h = jnp.einsum('td,edh->teh', xf, w1) + b1
        g = jnp.einsum('td,edh->teh', xf, w3) + b3
        a = jax.nn.silu(h) * g
        y = jnp.einsum('teh,ehd,te->td', a, w2, cw) + cw @ b2
        z = jax.nn.silu(xf @ sw1 + sb1) * (xf @ sw3 + sb3) @ sw2 + sb2
        return (y + z).reshape(shape)
    x = L0_attn_a_x
    x = x + _L0_attn_a_ref(_layernorm(x, axis=-1), L0_attn_a_W_q, L0_attn_a_W_dkv, L0_attn_a_W_uk, L0_attn_a_W_uv, L0_attn_a_W_o, L0_attn_a_ln_gamma, L0_attn_a_ln_beta)
    x = x + _L0_ffn_ref(_layernorm(x, axis=-1), L0_ffn_gate_w, L0_ffn_gate_b, L0_ffn_w1, L0_ffn_b1, L0_ffn_w3, L0_ffn_b3, L0_ffn_w2, L0_ffn_b2, L0_ffn_sw1, L0_ffn_sb1, L0_ffn_sw3, L0_ffn_sb3, L0_ffn_sw2, L0_ffn_sb2)
    x = x + _L0_attn_b_ref(_layernorm(x, axis=-1), L0_attn_b_W_A, L0_attn_b_W_B, L0_attn_b_W_C)
    x = x + _L0_ffn_ref(_layernorm(x, axis=-1), L0_ffn_gate_w, L0_ffn_gate_b, L0_ffn_w1, L0_ffn_b1, L0_ffn_w3, L0_ffn_b3, L0_ffn_w2, L0_ffn_b2, L0_ffn_sw1, L0_ffn_sb1, L0_ffn_sw3, L0_ffn_sb3, L0_ffn_sw2, L0_ffn_sb2)
    return x

_drawn_inputs = setup_inputs


def setup_inputs(seed=0):
    import zlib

    import numpy as np

    out = dict(_drawn_inputs(seed))
    spreads = {'L0_attn_a_ln_gamma': (1.0, 0.6),
     'L0_attn_a_ln_beta': (0.0, 0.271),
     'L0_ffn_gate_b': (0.0, 0.498),
     'L0_ffn_b1': (0.0, 0.8),
     'L0_ffn_b3': (0.0, 0.8),
     'L0_ffn_b2': (0.0, 0.347)}
    factors = {'L0_attn_a_W_q': 3.219,
     'L0_attn_a_W_uk': 3.181,
     'L0_ffn_gate_w': 2.693,
     'L0_ffn_w1': 8.0,
     'L0_ffn_w3': 8.0,
     'L0_ffn_w2': 8.0,
     'L0_ffn_sw1': 3.115,
     'L0_ffn_sb1': 8.0,
     'L0_ffn_sw3': 3.109,
     'L0_ffn_sb3': 8.0,
     'L0_ffn_sw2': 3.082}
    for name, (base, spread) in spreads.items():
        noise = np.random.default_rng([zlib.crc32(name.encode()), seed]).standard_normal(out[name].shape)
        drawn = base * np.exp(spread * noise) if base else spread * noise
        out[name] = jnp.asarray(drawn.astype(out[name].dtype))
    for name, factor in factors.items():
        out[name] = (out[name] * factor).astype(out[name].dtype)
    return out
```

```python
from contextlib import ExitStack

import numpy as np
import concourse.bass as bass
from concourse import mybir

F32 = mybir.dt.float32
BF16 = mybir.dt.bfloat16
I32 = mybir.dt.int32
U32 = mybir.dt.uint32
ALU = mybir.AluOpType
ACT = mybir.ActivationFunctionType
AX_X = mybir.AxisListType.X

P = 128
B, T, D = 4, 1024, 128
NT = T // P
TILES = B * NT
H, HD = 16, 8
HALF = HD // 2
LAT = 32
EPS = 1e-5
SCALE = 1.0 / float(np.sqrt(np.float32(HD)))
PARTS = 3
POWER_ITERS = 10
HALF_STEPS = 2 * POWER_ITERS + 1

E, TOPK = 16, 2
F = 176
FH = F - P
SF = 2 * F
SLOT_TILES = B * T * TOPK // P + E
SLOTS = SLOT_TILES * P
ROW = D + 1


def semaphores(nc, ctx, phase, names):
    made = {n: nc.alloc_semaphore(f"{phase}_{n}") for n in names.split()}

    def give_back():
        nc.clear_and_free_semaphores(list(made.values()))
        nc.all_engine_barrier()

    ctx.callback(give_back)
    return made


class Keep:
    pass


def chained(engine, sem):
    done = [0]

    def link(ins):
        done[0] += 1
        ins.then_inc(sem, 1)
        engine.wait_ge(sem, done[0])

    return link


def load_and_project(nc, ctx, dram, keep):
    def sb(name, shape, dt=F32):
        return ctx.enter_context(nc.sbuf_tensor(name, shape, dt))

    x = keep.x
    xn = sb("a_xn", [P, TILES, D])
    xnT = sb("a_xnT", [P, TILES, P])
    stats = sb("a_stats", [P, TILES, 6])
    mv = sb("a_mv", [P, TILES, 2])
    std = sb("a_std", [P, TILES])
    rstd = sb("a_rstd", [P, TILES])
    lstats = sb("a_lstats", [P, TILES, 6])
    lmv = sb("a_lmv", [P, TILES, 2])
    lstd = sb("a_lstd", [P, TILES])
    lrstd = sb("a_lrstd", [P, TILES])
    w_in = sb("a_w_in", [P, D + LAT])
    w_kv = sb("a_w_kv", [P, 2 * D])
    gamma = sb("a_gamma", [P, LAT])
    beta = sb("a_beta", [P, LAT])
    cos = sb("a_cos", [P, NT, HALF])
    sin = sb("a_sin", [P, NT, HALF])
    q = sb("a_q", [P, TILES, D + LAT])
    k = sb("a_k", [P, TILES, D])
    tmp_q = sb("a_tmp_q", [P, NT, H, HALF])
    tmp_k = sb("a_tmp_k", [P, NT, H, HALF])
    lat = sb("a_lat", [P, TILES, P])
    latn = sb("a_latn", [P, NT, LAT])
    latT = sb("a_latT", [P, 2, NT * P])
    parts = sb("a_parts", [P, 2, PARTS, T], BF16)
    w_ssm = sb("a_w_ssm", [P, 3, P])
    w_ssmT = sb("a_w_ssmT", [P, 3, P])
    uv = sb("a_uv", [P, 3])
    raw = sb("a_raw", [P, 3])
    sq = sb("a_sq", [P, 3])
    norm = sb("a_norm", [P, 3])
    inv = sb("a_inv", [P, 3])
    qr, kr = xn, lat
    rest = xnT
    ps_t = ctx.enter_context(nc.psum_tensor("a_ps_t", [P, T], F32))
    ps_p = ctx.enter_context(nc.psum_tensor("a_ps_p", [P, NT, 256], F32))
    ps_w = ctx.enter_context(nc.psum_tensor("a_ps_w", [P, 512], F32))
    ps_s = ctx.enter_context(nc.psum_tensor("a_ps_s", [P, 512], F32))
    s = semaphores(nc, ctx, "project", "x_in0 x_in1 x_in2 x_in3 consts w_in w_kv ssm zeroed eps mv std xn xnT_ps xnT "
             "proj q_sb lmv lstd lat_sb latT_ps latT kv k_sb v_sb qr kr chain_v chain_p chain_s "
             "qkT part_h rest_m part_m part_l pw_mv pw_raw pw_sq pw_ss pw_std pw_uv wT_ps wT sigma sent0 sent1")
    sent = [s["sent0"], s["sent1"]]
    x_in = [s["x_in0"], s["x_in1"], s["x_in2"], s["x_in3"]]
    block = ctx.enter_context(nc.Block())

    def tiles(b):
        return slice(b * NT, (b + 1) * NT)

    def rope(engine, link, src, dst, tmp, b, done):
        i = src[:, tiles(b), 0:D].rearrange("p t (h s d) -> p t h s d", s=2, d=HALF)
        o = dst[:, tiles(b), :].rearrange("p t (s d h) -> p t h s d", s=2, d=HALF)
        c = cos[:, :, :].unsqueeze(2).to_broadcast([P, NT, H, HALF])
        n = sin[:, :, :].unsqueeze(2).to_broadcast([P, NT, H, HALF])
        link(engine.tensor_tensor(o[:, :, :, 0, :], i[:, :, :, 0, :], c, ALU.mult))
        link(engine.tensor_tensor(tmp[:, :, :, :], i[:, :, :, 1, :], n, ALU.mult))
        link(engine.tensor_tensor(o[:, :, :, 0, :], o[:, :, :, 0, :], tmp[:, :, :, :], ALU.subtract))
        link(engine.tensor_tensor(o[:, :, :, 1, :], i[:, :, :, 0, :], n, ALU.mult))
        link(engine.tensor_tensor(tmp[:, :, :, :], i[:, :, :, 1, :], c, ALU.mult))
        engine.tensor_tensor(o[:, :, :, 1, :], o[:, :, :, 1, :], tmp[:, :, :, :], ALU.add).then_inc(done, 1)
        engine.wait_ge(done, b + 1)

    @block.sync
    def _(sp):
        sp.dma_start(keep.ident[:, :], dram["ident"]).then_inc(s["consts"], 16)
        for b in range(B):
            sp.dma_start(x[:, tiles(b), :], dram["x"][b].rearrange("(t p) d -> p t d", p=P)).then_inc(x_in[b], 16)
        sp.dma_start(w_in[:, 0:D], dram["w_q"]).then_inc(s["w_in"], 16)
        sp.dma_start(w_in[:, D:D + LAT], dram["w_dkv"]).then_inc(s["w_in"], 16)
        for i, w in enumerate((dram["w_a"], dram["w_b"], dram["w_c"])):
            sp.dma_start(w_ssm[:, i, :], w).then_inc(s["ssm"], 16)
        sp.dma_start(w_kv[0:LAT, 0:D], dram["w_uk"]).then_inc(s["w_kv"], 16)
        sp.dma_start(w_kv[0:LAT, D:2 * D], dram["w_uv"]).then_inc(s["w_kv"], 16)
        sp.dma_start(cos[:, :, :], dram["cos"]).then_inc(s["consts"], 16)
        sp.dma_start(sin[:, :, :], dram["sin"]).then_inc(s["consts"], 16)
        sp.dma_start(gamma[:, :], dram["ln_gamma"].partition_broadcast(P)).then_inc(s["consts"], 16)
        sp.dma_start(beta[:, :], dram["ln_beta"].partition_broadcast(P)).then_inc(s["consts"], 16)
        n = 0
        for b in range(B):
            for out in (keep.q_parts, keep.k_parts):
                sp.wait_ge(s["part_l"], n + 1)
                sp.dma_start(out[:, :, b * T:(b + 1) * T].rearrange("i r t -> r i t"), parts[:, n % 2, :, :]).then_inc(sent[n % 2], 16)
                n += 1
        for done in sent:
            sp.wait_ge(done, 16 * B)

    @block.gpsimd
    def _(pool):
        link = chained(pool, s["chain_p"])
        nc.gpsimd.memset(keep.eps[:, :], EPS).then_inc(s["eps"], 1)
        pool.wait_ge(s["eps"], 1)
        for g in range(1, P // LAT):
            nc.gpsimd.memset(w_kv[g * LAT:(g + 1) * LAT, :], 0.0).then_inc(s["zeroed"], 1)
            pool.wait_ge(s["zeroed"], g)
        nc.gpsimd.memset(lat[:, :, :], 0.0).then_inc(s["zeroed"], 1)
        pool.wait_ge(s["consts"], 80)
        for b in range(B):
            pool.wait_ge(s["k_sb"], b + 1)
            rope(nc.gpsimd, link, k, kr, tmp_k, b, s["kr"])

    def stage_slots():
        n = 0
        while True:
            yield n if n < HALF_STEPS + 1 else None
            n += 1

    @block.tensor
    def _(pe):
        slots = stage_slots()

        def power():
            n = next(slots)
            if n is None:
                return
            w = w_ssm if n % 2 == 0 else w_ssmT
            pe.wait_ge(s["pw_uv"], n + 1)
            for i in range(3):
                mm = nc.tensor.matmul(ps_w[:, i:i + 1], w[:, i, :], uv[:, i:i + 1], start=True, stop=True)
            mm.then_inc(s["pw_mv"], 1)
            pe.wait_ge(s["pw_sq"], n + 1)
            nc.tensor.matmul(ps_s[:, 0:3], keep.ones[:, :], sq[:, :], start=True, stop=True).then_inc(s["pw_ss"], 1)

        pe.wait_ge(s["consts"], 80)
        pe.wait_ge(s["ssm"], 48)
        for i in range(3):
            mm = nc.tensor.transpose(ps_w[:, 128 + i * P:128 + (i + 1) * P], w_ssm[:, i, :], keep.ident[:, :])
        mm.then_inc(s["wT_ps"], 1)
        for b in range(B):
            pe.wait_ge(s["xn"], b + 1)
            if b:
                pe.wait_ge(s["xnT"], b)
            for t in range(NT):
                mm = nc.tensor.transpose(ps_t[:, t * P:(t + 1) * P], xn[:, b * NT + t, :], keep.ident[:, :])
            mm.then_inc(s["xnT_ps"], 1)
            power()
        pe.wait_ge(s["w_in"], 32)
        for b in range(B):
            pe.wait_ge(s["xnT"], b + 1)
            if b:
                pe.wait_ge(s["q_sb"], b)
            for t in range(NT):
                mm = nc.tensor.matmul(ps_p[:, t, 0:D + LAT], xnT[:, b * NT + t, :], w_in[:, :], start=True, stop=True)
            mm.then_inc(s["proj"], 1)
            power()
        pe.wait_ge(s["w_kv"], 32)
        pe.wait_ge(s["zeroed"], P // LAT)
        for b in range(B):
            pe.wait_ge(s["lat_sb"], b + 1)
            if b == 0:
                pe.wait_ge(s["xnT"], B)
            else:
                pe.wait_ge(s["latT"], b)
            for t in range(NT):
                mm = nc.tensor.transpose(ps_t[:, t * P:(t + 1) * P], lat[:, b * NT + t, :], keep.ident[:, :])
            mm.then_inc(s["latT_ps"], 1)
            power()
            pe.wait_ge(s["latT"], b + 1)
            if b == 0:
                pe.wait_ge(s["q_sb"], B)
            else:
                pe.wait_ge(s["k_sb"], b)
                pe.wait_ge(s["v_sb"], b)
            for t in range(NT):
                mm = nc.tensor.matmul(ps_p[:, t, :], latT[:, b % 2, t * P:(t + 1) * P], w_kv[:, :], start=True, stop=True)
            mm.then_inc(s["kv"], 1)
            power()
        n = 0
        for b in range(B):
            for src, ready in ((qr, s["qr"]), (kr, s["kr"])):
                pe.wait_ge(ready, b + 1)
                if n == 0:
                    pe.wait_ge(s["latT"], B)
                else:
                    pe.wait_ge(s["rest_m"], n)
                for t in range(NT):
                    mm = nc.tensor.transpose(ps_t[:, t * P:(t + 1) * P], src[:, b * NT + t, :], keep.ident[:, :])
                mm.then_inc(s["qkT"], 1)
                power()
                n += 1

    @block.scalar
    def _(act):
        slots = stage_slots()

        def power():
            n = next(slots)
            if n is None:
                return
            if n < HALF_STEPS:
                act.wait_ge(s["pw_ss"], n + 1)
                nc.scalar.activation(norm[:, :], ps_s[:, 0:3], ACT.Sqrt).then_inc(s["pw_std"], 1)

        act.wait_ge(s["eps"], 1)
        act.wait_ge(s["wT_ps"], 1)
        nc.scalar.copy(w_ssmT[:, :, :], ps_w[:, 128:512].rearrange("p (i o) -> p i o", i=3)).then_inc(s["wT"], 1)
        for b in range(B):
            act.wait_ge(s["mv"], b + 1)
            nc.scalar.activation(std[:, tiles(b)], mv[:, tiles(b), 1], ACT.Sqrt, bias=keep.eps[:, 0:1]).then_inc(s["std"], 1)
        for b in range(B):
            act.wait_ge(s["xnT_ps"], b + 1)
            nc.scalar.copy(xnT[:, tiles(b), :], ps_t[:, :].rearrange("p (t c) -> p t c", t=NT)).then_inc(s["xnT"], 1)
            power()
        for b in range(B):
            act.wait_ge(s["proj"], b + 1)
            nc.scalar.copy(q[:, tiles(b), :], ps_p[:, :, 0:D + LAT]).then_inc(s["q_sb"], 1)
            act.wait_ge(s["lmv"], b + 1)
            nc.scalar.activation(lstd[:, tiles(b)], lmv[:, tiles(b), 1], ACT.Sqrt, bias=keep.eps[:, 0:1]).then_inc(s["lstd"], 1)
            power()
        for b in range(B):
            act.wait_ge(s["latT_ps"], b + 1)
            if b >= 2:
                act.wait_ge(s["kv"], b - 1)
            nc.scalar.copy(latT[:, b % 2, :], ps_t[:, :]).then_inc(s["latT"], 1)
            power()
            act.wait_ge(s["kv"], b + 1)
            nc.scalar.copy(k[:, tiles(b), :], ps_p[:, :, 0:D]).then_inc(s["k_sb"], 1)
            power()
        n = 0
        for b in range(B):
            for _ in range(2):
                act.wait_ge(s["qkT"], n + 1)
                if n >= 2:
                    act.wait_ge(sent[n % 2], 16 * (n // 2))
                nc.scalar.copy(parts[:, n % 2, 0, :], ps_t[:, :]).then_inc(s["part_h"], 1)
                act.wait_ge(s["rest_m"], n + 1)
                nc.scalar.copy(parts[:, n % 2, 1, :], rest[:, tiles(n % 4), :].rearrange("p t c -> p (t c)")).then_inc(s["part_m"], 1)
                power()
                n += 1

    @block.vector
    def _(dve):
        link = chained(dve, s["chain_v"])
        slots = stage_slots()

        def power():
            n = next(slots)
            if n is None:
                return
            dve.wait_ge(s["pw_mv"], n + 1)
            if n < HALF_STEPS:
                link(nc.vector.tensor_copy(raw[:, :], ps_w[:, 0:3]))
                nc.vector.tensor_tensor(sq[:, :], raw[:, :], raw[:, :], ALU.mult).then_inc(s["pw_sq"], 1)
                dve.wait_ge(s["pw_std"], n + 1)
                link(nc.vector.tensor_scalar(inv[:, :], norm[:, :], 1e-12, None, ALU.add))
                link(nc.vector.reciprocal(inv[:, :], inv[:, :]))
                if n == HALF_STEPS - 2:
                    nc.vector.tensor_tensor(keep.u_last[:, :], raw[:, :], inv[:, :], ALU.mult)
                nc.vector.tensor_tensor(uv[:, :], raw[:, :], inv[:, :], ALU.mult).then_inc(s["pw_uv"], 1)
            else:
                nc.vector.tensor_tensor(sq[:, :], ps_w[:, 0:3], keep.u_last[:, :], ALU.mult).then_inc(s["pw_sq"], 1)
                dve.wait_ge(s["pw_ss"], n + 1)
                link(nc.vector.tensor_copy(norm[:, :], ps_s[:, 0:3]))
                link(nc.vector.reciprocal(inv[:, :], norm[:, :]))
                nc.vector.tensor_scalar(keep.a_nat[:, :], w_ssm[:, 0, :], inv[:, 0:1], None, ALU.mult)
                for i, out in enumerate((keep.a_T, keep.b_T, keep.c_T)):
                    last = nc.vector.tensor_scalar(out[:, :], w_ssmT[:, i, :], inv[:, i:i + 1], None, ALU.mult)
                last.then_inc(s["sigma"], 1)

        nc.vector.memset(keep.ones[:, :], 1.0)
        link(nc.vector.memset(raw[:, :], 1.0))
        dve.wait_ge(s["wT"], 1)
        nc.vector.tensor_scalar(uv[:, :], raw[:, :], float(1.0 / np.sqrt(np.float32(P))), None, ALU.mult).then_inc(s["pw_uv"], 1)
        for b in range(B):
            dve.wait_ge(x_in[b], 16)
            for t in range(b * NT, (b + 1) * NT):
                last = nc.vector.bn_stats(stats[:, t, :], x[:, t, :])
            link(last)
            for t in range(b * NT, (b + 1) * NT):
                last = nc.vector.bn_aggr(mv[:, t, :], stats[:, t, :])
            last.then_inc(s["mv"], 1)
        for b in range(B):
            dve.wait_ge(s["std"], b + 1)
            link(nc.vector.reciprocal(rstd[:, tiles(b)], std[:, tiles(b)]))
            for t in range(b * NT, (b + 1) * NT):
                last = nc.vector.tensor_scalar(xn[:, t, :], x[:, t, :], mv[:, t, 0:1], rstd[:, t:t + 1],
                                               ALU.subtract, ALU.mult)
            last.then_inc(s["xn"], 1)
            power()
        dve.wait_ge(s["consts"], 80)
        dve.wait_ge(s["zeroed"], P // LAT)
        for b in range(B):
            dve.wait_ge(s["q_sb"], b + 1)
            for t in range(b * NT, (b + 1) * NT):
                last = nc.vector.bn_stats(lstats[:, t, :], q[:, t, D:D + LAT])
            link(last)
            for t in range(b * NT, (b + 1) * NT):
                last = nc.vector.bn_aggr(lmv[:, t, :], lstats[:, t, :])
            last.then_inc(s["lmv"], 1)
            dve.wait_ge(s["lstd"], b + 1)
            link(nc.vector.reciprocal(lrstd[:, tiles(b)], lstd[:, tiles(b)]))
            for t in range(NT):
                g = b * NT + t
                last = nc.vector.tensor_scalar(latn[:, t, :], q[:, g, D:D + LAT], lmv[:, g, 0:1],
                                               lrstd[:, g:g + 1], ALU.subtract, ALU.mult)
            link(last)
            link(nc.vector.tensor_tensor(latn[:, :, :], latn[:, :, :], gamma[:, :].unsqueeze(1).to_broadcast([P, NT, LAT]), ALU.mult))
            nc.vector.tensor_tensor(lat[:, tiles(b), 0:LAT], latn[:, :, :],
                                    beta[:, :].unsqueeze(1).to_broadcast([P, NT, LAT]), ALU.add).then_inc(s["lat_sb"], 1)
            power()
        for b in range(B):
            power()
            dve.wait_ge(s["q_sb"], b + 1)
            rope(nc.vector, link, q, qr, tmp_q, b, s["qr"])
            dve.wait_ge(s["k_sb"], b + 1)
            v_out = keep.v[:, tiles(b), :, 0:HD]
            nc.vector.tensor_copy(v_out, ps_p[:, :, D:2 * D].rearrange("p t (h d) -> p t h d", h=H)).then_inc(s["v_sb"], 1)
            power()
        nc.vector.memset(keep.v[:, :, :, HD:HD + 1], 1.0)
        n = 0
        for b in range(B):
            for _ in range(2):
                r = rest[:, tiles(n % 4), :].rearrange("p t c -> p (t c)")
                dve.wait_ge(s["part_h"], n + 1)
                nc.vector.tensor_tensor(r, ps_t[:, :], parts[:, n % 2, 0, :], ALU.subtract).then_inc(s["rest_m"], 1)
                dve.wait_ge(s["part_m"], n + 1)
                nc.vector.tensor_tensor(parts[:, n % 2, 2, :], r, parts[:, n % 2, 1, :], ALU.subtract).then_inc(s["part_l"], 1)
                power()
                n += 1
        dve.wait_ge(s["part_l"], 2 * B)
        dve.wait_ge(s["sigma"], 1)


G = 4
UNITS = B * H // G
RING = 3
PAIRS = PARTS * PARTS
KROWS = PAIRS * HD
SROWS = KROWS + PARTS
HALFQ = 512
LAST_MAX_STEP = 8


def unit_steps():
    return [(hf, kb, max(kb * P, hf * HALFQ), (hf + 1) * HALFQ - max(kb * P, hf * HALFQ))
            for hf in range(T // HALFQ) for kb in range((hf + 1) * HALFQ // P)]


def max_tasks():
    return [(j, qt, c, min(HALFQ, (qt + 1) * P - c)) for j in range(G) for qt in range(NT)
            for c in range(0, (qt + 1) * P, HALFQ)]


def spread_tasks():
    steps, tasks = unit_steps(), max_tasks()
    whole, all_cols = sum(w for *_, w in steps[:LAST_MAX_STEP + 1]), sum(n for *_, n in tasks)
    out, at, cols, done = [], 0, 0, 0
    for i, (*_, w) in enumerate(steps):
        done += w
        first = at
        while at < len(tasks) and (i >= LAST_MAX_STEP or cols * whole < done * all_cols):
            cols += tasks[at][3]
            at += 1
        out.append(range(first, at))
    return out


def attention(nc, ctx, dram, keep):
    def sb(name, shape, dt=F32):
        return ctx.enter_context(nc.sbuf_tensor(name, shape, dt))

    q_stack = [sb(f"b_q_stack{r}", [SROWS, G, T], BF16) for r in range(RING)]
    k_stack = [sb(f"b_k_stack{r}", [SROWS, G, T], BF16) for r in range(RING)]
    ones_row = sb("b_ones_row", [PARTS, G * T], BF16)
    ident_b = sb("b_ident_b", [P, P], BF16)
    maskneg = sb("b_maskneg", [P, P], BF16)
    probs = sb("b_probs", [P, 3, G, HALFQ])
    mx = sb("b_mx", [P, 2, G * NT])
    neg = sb("b_neg", [P, G * NT])
    neg_parts = sb("b_neg_parts", [P, PARTS, G * NT], BF16)
    neg_rows = sb("b_neg_rows", [PARTS * G * NT, P], BF16)
    o_sb = sb("b_o_sb", [P, 2, HALFQ])
    rz = sb("b_rz", [P, HALFQ // P, G])
    ps_s = ctx.enter_context(nc.psum_tensor("b_ps_s", [P, 2, 2, HALFQ], F32))
    ps_m = ctx.enter_context(nc.psum_tensor("b_ps_m", [P, 2, HALFQ], F32))
    ps_o = ctx.enter_context(nc.psum_tensor("b_ps_o", [P, 2, HALFQ], F32))
    s = semaphores(nc, ctx, "attend", "ones masks ones0 ones1 ones2 stack0 stack1 stack2 neg_sb0 neg_sb1 neg_sb2 ps_zero scores exp mask pv "
             "cand reduced mx_chain neg_ready negT neg_rows o_sb oT attn chain_v")
    stacked = [s["stack0"], s["stack1"], s["stack2"]]
    ones_in = [s["ones0"], s["ones1"], s["ones2"]]
    neg_in = [s["neg_sb0"], s["neg_sb1"], s["neg_sb2"]]
    steps, tasks, spread = unit_steps(), max_tasks(), spread_tasks()
    NS = len(steps)
    NTASK = len(tasks)
    diag = [kb * P >= hf * HALFQ for hf, kb, _, _ in steps]
    half_end = [NS // 3 - 1, NS - 1]
    block = ctx.enter_context(nc.Block())

    def masks_until(i):
        return i // NS * sum(diag) + sum(diag[:i % NS + 1])

    @block.sync
    def _(sp):
        sp.wait_ge(s["ones"], 1)
        for r in range(RING):
            sp.dma_start(k_stack[r][KROWS:SROWS, :, :], ones_row[:, :].rearrange("r (h t) -> r h t", h=G)).then_inc(ones_in[r], 16)

        def stacks(u):
            b, g, r = u // G, u % G, u % RING
            if u >= RING:
                sp.wait_ge(s["scores"], 2 * NS * (u - RING + 1))
            q_src, k_src = (x.rearrange("i (d h) t -> (i d) h t", h=H)[:, g * G:(g + 1) * G, b * T:(b + 1) * T]
                            for x in (keep.q_parts, keep.k_parts))
            for i in range(PARTS):
                at = i * PARTS * HD
                sp.dma_start(k_stack[r][at:at + PARTS * HD, :, :], k_src).then_inc(stacked[r], 16)
                for j in range(PARTS):
                    sp.dma_start(q_stack[r][at + j * HD:at + (j + 1) * HD, :, :], q_src[i * HD:(i + 1) * HD]).then_inc(stacked[r], 16)

        def maxima(u):
            sp.wait_ge(s["neg_rows"], u + 1)
            for i in range(PARTS):
                n = G * NT
                sp.dma_start(q_stack[u % RING][KROWS + i:KROWS + i + 1, :, :].rearrange("r h (t c) -> r (h t) c", c=P),
                             neg_rows[i * n:(i + 1) * n, :]).then_inc(neg_in[u % RING], 16)

        stacks(0)
        for u in range(UNITS):
            if u + 1 < UNITS:
                stacks(u + 1)
            maxima(u)

    STACK_DMAS = PARTS + PAIRS

    @block.gpsimd
    def _(pool):
        nc.gpsimd.memset(maskneg[:, :], 0.0).then_inc(s["mx_chain"], 1)
        pool.wait_ge(s["mx_chain"], 1)
        nc.gpsimd.affine_select(out=maskneg[:, :], in_=maskneg[:, :], compare_op=ALU.is_ge, fill=-1e30, base=0,
                                pattern=[[-1, P]], channel_multiplier=1).then_inc(s["masks"], 1)
        n = 0
        for i in range(UNITS * NS):
            if not diag[i % NS]:
                continue
            pool.wait_ge(s["exp"], 2 * i + 2)
            blk = probs[:, i % 3, :, 0:P]
            nc.gpsimd.affine_select(out=blk, in_=blk, compare_op=ALU.is_ge, fill=0.0, base=0,
                                    pattern=[[0, G], [1, P]], channel_multiplier=-1).then_inc(s["mask"], 1)

    @block.scalar
    def _(act):
        def take_outputs(n):
            act.wait_ge(s["pv"], n // 2 * NS + half_end[n % 2] + 1)
            if n >= 2:
                act.wait_ge(s["oT"], n - 1)
            nc.scalar.copy(o_sb[:, n % 2, :], ps_o[:, n % 2, :]).then_inc(s["o_sb"], 1)

        for i in range(UNITS * NS):
            u, k = divmod(i, NS)
            w = steps[k][3]
            if i >= 3:
                act.wait_ge(s["pv"], i - 2)
            for hp in range(2):
                act.wait_ge(s["scores"], 2 * i + hp + 1)
                nc.scalar.activation(probs[:, i % 3, 2 * hp:2 * hp + 2, 0:w], ps_s[:, hp, :, 0:w], ACT.Exp,
                                     scale=SCALE).then_inc(s["exp"], 1)
            if k == half_end[0] + 2:
                take_outputs(2 * u)
            if k == 1 and u:
                take_outputs(2 * u - 1)
        take_outputs(2 * UNITS - 1)

    @block.tensor
    def _(pe):
        def maximum_scores(u, which):
            r = u % RING
            for n in which:
                j, qt, c, keys = tasks[n]
                at = u * NTASK + n
                if at >= 2:
                    pe.wait_ge(s["reduced"], at - 1)
                out = ps_m[:, at % 2, 0:keys]
                on_diagonal = c + keys == (qt + 1) * P
                mm = nc.tensor.matmul(out, q_stack[r][0:KROWS, j, qt * P:(qt + 1) * P],
                                      k_stack[r][0:KROWS, j, c:c + keys], start=True, stop=not on_diagonal,
                                      skip_group_check=True)
                if on_diagonal:
                    mm = nc.tensor.matmul(out[:, keys - P:keys], ident_b[:, :], maskneg[:, :], start=False, stop=True,
                                          skip_group_check=True)
                mm.then_inc(s["cand"], 1)

        def maximum_rows(u):
            pe.wait_ge(s["neg_ready"], u + 1)
            nc.tensor.transpose(ps_m[0:PARTS * G * NT, 0, 0:P // 2].bitcast(BF16), neg_parts[:, :, :].rearrange("p i n -> p (i n)"),
                                ident_b[:, :]).then_inc(s["negT"], 1)

        def weighted_values(i):
            u, k = divmod(i, NS)
            hf, kb, lo, w = steps[k]
            b, g = u // G, u % G
            pe.wait_ge(s["exp"], 2 * i + 2)
            if diag[k]:
                pe.wait_ge(s["mask"], masks_until(i))
            if kb == 0:
                if u:
                    pe.wait_ge(s["attn"], 2 * u - 1 + hf)
                else:
                    pe.wait_ge(s["ps_zero"], 1)
            for j in range(G):
                mm = nc.tensor.matmul(ps_o[32 * j:32 * j + HD + 1, hf, lo - hf * HALFQ:HALFQ],
                                      keep.v[:, b * NT + kb, g * G + j, :], probs[:, i % 3, j, 0:w],
                                      start=(kb == 0), stop=(k in half_end), skip_group_check=True)
            mm.then_inc(s["pv"], 1)

        def turn_outputs(n):
            pe.wait_ge(s["o_sb"], n + 1)
            for t in range(HALFQ // P):
                mm = nc.tensor.transpose(ps_o[:, n % 2, t * P:(t + 1) * P], o_sb[:, n % 2, t * P:(t + 1) * P], keep.ident[:, :])
            mm.then_inc(s["oT"], 1)

        def stacks_ready(u):
            pe.wait_ge(stacked[u % RING], 16 * STACK_DMAS * (u // RING + 1))

        pe.wait_ge(s["masks"], 2)
        for r in range(RING):
            pe.wait_ge(ones_in[r], 16)
        stacks_ready(0)
        maximum_scores(0, range(NTASK))
        maximum_rows(0)
        for i in range(UNITS * NS):
            u, k = divmod(i, NS)
            hf, kb, lo, w = steps[k]
            r = u % RING
            if k == 0:
                pe.wait_ge(neg_in[r], 16 * PARTS * (u // RING + 1))
                if u + 1 < UNITS:
                    stacks_ready(u + 1)
            for hp in range(2):
                if i:
                    pe.wait_ge(s["exp"], 2 * i + hp - 1)
                for jj in range(2):
                    j = 2 * hp + jj
                    mm = nc.tensor.matmul(ps_s[:, hp, jj, 0:w], k_stack[r][0:SROWS, j, kb * P:(kb + 1) * P],
                                          q_stack[r][0:SROWS, j, lo:lo + w], start=True, stop=True)
                mm.then_inc(s["scores"], 1)
            if u + 1 < UNITS:
                maximum_scores(u + 1, spread[k])
                if k == LAST_MAX_STEP + 1:
                    maximum_rows(u + 1)
            if i:
                weighted_values(i - 1)
            if k == half_end[0] + 2:
                turn_outputs(2 * u)
            if k == 1 and u:
                turn_outputs(2 * u - 1)
        weighted_values(UNITS * NS - 1)
        turn_outputs(2 * UNITS - 1)

    @block.vector
    def _(dve):
        link = chained(dve, s["chain_v"])
        nc.vector.memset(ones_row[:, :], 1.0).then_inc(s["ones"], 1)
        nc.vector.memset(mx[:, :, :], -1e30)
        nc.vector.memset(ps_o[:, :, :], 0.0).then_inc(s["ps_zero"], 1)
        nc.vector.tensor_copy(ident_b[:, :], keep.ident[:, :]).then_inc(s["masks"], 1)

        def reduce(u, which):
            for n in which:
                j, qt, c, keys = tasks[n]
                at = u * NTASK + n
                dve.wait_ge(s["cand"], at + 1)
                nc.vector.tensor_reduce(mx[:, c // HALFQ, j * NT + qt:j * NT + qt + 1], ps_m[:, at % 2, 0:keys],
                                        AX_X, ALU.max).then_inc(s["reduced"], 1)

        def negate(u):
            dve.wait_ge(s["reduced"], (u + 1) * NTASK)
            if u:
                dve.wait_ge(neg_in[(u - 1) % RING], 16 * PARTS * ((u - 1) // RING + 1))
            link(nc.vector.tensor_tensor(neg[:, :], mx[:, 0, :], mx[:, 1, :], ALU.max))
            link(nc.vector.tensor_scalar(neg[:, :], neg[:, :], -1.0, None, ALU.mult))
            link(nc.vector.tensor_copy(neg_parts[:, 0, :], neg[:, :]))
            for i in range(1, PARTS):
                link(nc.vector.tensor_tensor(neg[:, :], neg[:, :], neg_parts[:, i - 1, :], ALU.subtract))
                if i < PARTS - 1:
                    link(nc.vector.tensor_copy(neg_parts[:, i, :], neg[:, :]))
                else:
                    nc.vector.tensor_copy(neg_parts[:, i, :], neg[:, :]).then_inc(s["neg_ready"], 1)
            dve.wait_ge(s["negT"], u + 1)
            nc.vector.tensor_copy(neg_rows[:, :], ps_m[0:PARTS * G * NT, 0, 0:P // 2].bitcast(BF16)).then_inc(s["neg_rows"], 1)

        def normalize(n):
            u, hf = divmod(n, 2)
            b, g = divmod(u, G)
            dve.wait_ge(s["oT"], n + 1)
            if n:
                dve.wait_ge(s["attn"], n)
            o = ps_o[:, hf, :].rearrange("p (t j c) -> p t j c", t=HALFQ // P, j=G)
            link(nc.vector.reciprocal(rz[:, :, :], o[:, :, :, HD]))
            first = b * NT + hf * HALFQ // P
            out = keep.attn[:, first:first + HALFQ // P, g * G * HD:(g + 1) * G * HD]
            nc.vector.tensor_tensor(out.rearrange("p t (j d) -> p t j d", j=G), o[:, :, :, 0:HD],
                                    rz[:, :, :].unsqueeze(3).to_broadcast([P, HALFQ // P, G, HD]), ALU.mult).then_inc(s["attn"], 1)

        reduce(0, range(NTASK))
        negate(0)
        for u in range(UNITS):
            for k in range(NS):
                if u + 1 < UNITS:
                    reduce(u + 1, spread[k])
                    if k == LAST_MAX_STEP:
                        negate(u + 1)
                if k == half_end[0] + 2:
                    normalize(2 * u)
                if k == 1 and u:
                    normalize(2 * u - 1)
        normalize(2 * UNITS - 1)


LEVELS = T.bit_length() - 1
GROUP = 4


def project_out(nc, ctx, dram, keep):
    def sb(name, shape, dt=F32):
        return ctx.enter_context(nc.sbuf_tensor(name, shape, dt))

    w_o = sb("c_w_o", [P, D])
    attnT = sb("c_attnT", [P, 2, GROUP * P])
    a_pow = sb("c_a_pow", [P, 2, P])
    ps_t = ctx.enter_context(nc.psum_tensor("c_ps_t", [P, 2, GROUP * P], F32))
    ps_y = ctx.enter_context(nc.psum_tensor("c_ps_y", [P, 2, GROUP * P], F32))
    ps_a = ctx.enter_context(nc.psum_tensor("c_ps_a", [P, 512], F32))
    s = semaphores(nc, ctx, "out", "w_o turned copied projected added squared power")
    groups = TILES // GROUP
    block = ctx.enter_context(nc.Block())

    @block.sync
    def _(sp):
        sp.dma_start(w_o[:, :], dram["w_o"]).then_inc(s["w_o"], 16)

    @block.tensor
    def _(pe):
        def square(level):
            pe.wait_ge(s["power"], level)
            natural = a_pow[:, level % 2, :]
            nc.tensor.matmul(ps_a[:, 0:P], natural, keep.a_powT[:, level - 1, :], start=True, stop=True)
            nc.tensor.matmul(ps_a[:, P:2 * P], keep.a_powT[:, level - 1, :], natural, start=True, stop=True).then_inc(s["squared"], 1)

        pe.wait_ge(s["w_o"], 16)
        level = 1
        for g in range(groups + 1):
            if g < groups:
                if g >= 2:
                    pe.wait_ge(s["copied"], g - 1)
                for t in range(GROUP):
                    mm = nc.tensor.transpose(ps_t[:, g % 2, t * P:(t + 1) * P], keep.attn[:, g * GROUP + t, :], keep.ident[:, :])
                mm.then_inc(s["turned"], 1)
            if g:
                pe.wait_ge(s["copied"], g)
                if g >= 3:
                    pe.wait_ge(s["added"], g - 2)
                for t in range(GROUP):
                    mm = nc.tensor.matmul(ps_y[:, (g - 1) % 2, t * P:(t + 1) * P],
                                          attnT[:, (g - 1) % 2, t * P:(t + 1) * P], w_o[:, :], start=True, stop=True)
                mm.then_inc(s["projected"], 1)
            square(level)
            level += 1
        while level < LEVELS:
            square(level)
            level += 1

    @block.scalar
    def _(act):
        for g in range(groups):
            act.wait_ge(s["turned"], g + 1)
            if g >= 2:
                act.wait_ge(s["projected"], g - 1)
            nc.scalar.copy(attnT[:, g % 2, :], ps_t[:, g % 2, :]).then_inc(s["copied"], 1)

    @block.vector
    def _(dve):
        nc.vector.tensor_copy(a_pow[:, 1, :], keep.a_nat[:, :])
        nc.vector.tensor_copy(keep.a_powT[:, 0, :], keep.a_T[:, :]).then_inc(s["power"], 1)
        level = 1

        def take_power(level):
            dve.wait_ge(s["squared"], level)
            nc.vector.tensor_copy(keep.a_powT[:, level, :], ps_a[:, 0:P])
            nc.vector.tensor_copy(a_pow[:, (level + 1) % 2, :], ps_a[:, P:2 * P]).then_inc(s["power"], 1)

        for g in range(groups + 1):
            if g:
                dve.wait_ge(s["projected"], g)
                xs = keep.x[:, (g - 1) * GROUP:g * GROUP, :]
                nc.vector.tensor_tensor(xs, ps_y[:, (g - 1) % 2, :].rearrange("p (t d) -> p t d", t=GROUP), xs,
                                        ALU.add).then_inc(s["added"], 1)
            take_power(level)
            level += 1
        while level < LEVELS:
            take_power(level)
            level += 1


class Norm:

    def __init__(self, nc, ctx, keep, tag, out, outT):
        def sb(name, shape, dt=F32):
            return ctx.enter_context(nc.sbuf_tensor(tag + name, shape, dt))
        self.nc, self.keep, self.out, self.outT = nc, keep, out, outT
        self.stats, self.mv = sb("stats", [P, TILES, 6]), sb("mv", [P, TILES, 2])
        self.std, self.rstd = sb("std", [P, TILES]), sb("rstd", [P, TILES])
        self.s = semaphores(nc, ctx, tag + "norm", "mv std rstd xn turned xnT")

    def vector_stats(self, dve, link, b):
        for t in range(b * NT, (b + 1) * NT):
            last = dve.bn_stats(self.stats[:, t, :], self.keep.x[:, t, :])
        link(last)
        for t in range(b * NT, (b + 1) * NT):
            last = dve.bn_aggr(self.mv[:, t, :], self.stats[:, t, :])
        last.then_inc(self.s["mv"], 1)

    def scalar_std(self, act, b):
        at = slice(b * NT, (b + 1) * NT)
        act.wait_ge(self.s["mv"], b + 1)
        act.activation(self.std[:, at], self.mv[:, at, 1], ACT.Sqrt, bias=self.keep.eps[:, 0:1]).then_inc(self.s["std"], 1)

    def vector_scale(self, dve, link, b):
        dve.wait_ge(self.s["std"], b + 1)
        link(dve.reciprocal(self.rstd[:, b * NT:(b + 1) * NT], self.std[:, b * NT:(b + 1) * NT]))
        for t in range(b * NT, (b + 1) * NT):
            last = dve.tensor_scalar(self.out[:, t, 0:D], self.keep.x[:, t, :], self.mv[:, t, 0:1],
                                     self.rstd[:, t:t + 1], ALU.subtract, ALU.mult)
        last.then_inc(self.s["xn"], 1)

    def tensor_turn(self, pe, bank, b):
        pe.wait_ge(self.s["xn"], b + 1)
        if b >= 2:
            pe.wait_ge(self.s["xnT"], b - 1)
        for t in range(NT):
            mm = pe.transpose(bank[:, t * P:(t + 1) * P], self.out[:, b * NT + t, 0:D], self.keep.ident[:, :])
        mm.then_inc(self.s["turned"], 1)

    def scalar_copy(self, act, bank, b):
        act.wait_ge(self.s["turned"], b + 1)
        act.copy(self.outT[:, b * T:(b + 1) * T], bank[:, :]).then_inc(self.s["xnT"], 1)


def load_expert_weights(nc, ctx, dram, keep):
    def sb(name, shape, dt=F32):
        return ctx.enter_context(nc.sbuf_tensor(name, shape, dt))

    keep.w13 = sb("w13", [P, E, 2, F])
    keep.b13 = sb("b13", [P, E, 2, F])
    keep.w2 = sb("w2", [P, E, 2, D])
    keep.sw1, keep.sw3 = sb("sw1", [P, SF]), sb("sw3", [P, SF])
    keep.sbias = sb("sbias", [P, 2, 3])
    keep.sw2 = sb("sw2", [P, 3, D])
    keep.gate_w = sb("gate_w", [P, E])
    keep.gate_b = sb("gate_b", [P, E])
    keep.before = sb("before", [P, P])
    keep.expert_no = sb("expert_no", [P, E])
    keep.tile_no = sb("tile_no", [P, SLOT_TILES])
    keep.token_id = sb("token_id", [P, TOPK, TILES])
    s = semaphores(nc, ctx, "load", "loaded w2_zero sw2_zero")
    keep.loaded = s["loaded"]
    n = [0]

    def load(sp, out, src):
        sp.dma_start(out, src).then_inc(s["loaded"], 16)
        n[0] += 16

    with nc.Block() as block:

        @block.gpsimd
        def _(pool):
            nc.gpsimd.memset(keep.w2[:, :, 1, :], 0.0).then_inc(s["w2_zero"], 1)

        @block.sync
        def _(sp):
            load(sp, keep.gate_w[:, :], dram["gate_w"])
            load(sp, keep.gate_b[:, :], dram["gate_b"].partition_broadcast(P))
            load(sp, keep.before[:, :], dram["before"])
            load(sp, keep.expert_no[:, :], dram["expert_no"].partition_broadcast(P))
            load(sp, keep.tile_no[:, :], dram["tile_no"].partition_broadcast(P))
            load(sp, keep.token_id[:, :, :], dram["token_id"])
            load(sp, keep.sw1[:, :], dram["sw1"])
            load(sp, keep.sw3[:, :], dram["sw3"])
            for i, v in enumerate((dram["sb1"], dram["sb3"])):
                for c in range(3):
                    rows = min(P, SF - c * P)
                    load(sp, keep.sbias[0:rows, i, c:c + 1], v[c * P:c * P + rows].unsqueeze(1))
            for c in range(3):
                rows = min(P, SF - c * P)
                load(sp, keep.sw2[0:rows, c, :], dram["sw2"][c * P:c * P + rows, :])
            load(sp, keep.sw2[SF - 2 * P:SF - 2 * P + 1, 2, :], dram["sb2"].unsqueeze(0))
            load(sp, keep.w13[:, :, 0, :], dram["w1"].rearrange("e d f -> d e f"))
            load(sp, keep.w13[:, :, 1, :], dram["w3"].rearrange("e d f -> d e f"))
            load(sp, keep.b13[:, :, 0, :], dram["b1"].partition_broadcast(P))
            load(sp, keep.b13[:, :, 1, :], dram["b3"].partition_broadcast(P))
            load(sp, keep.w2[:, :, 0, :], dram["w2"][:, 0:P, :].rearrange("e f d -> f e d"))
            sp.wait_ge(s["w2_zero"], 1)
            load(sp, keep.w2[0:FH, :, 1, :], dram["w2"][:, P:F, :].rearrange("e f d -> f e d"))
            load(sp, keep.w2[FH:FH + 1, :, 1, :], dram["b2"].unsqueeze(0))
            sp.wait_ge(s["loaded"], n[0])
    keep.loaded_all = n[0]


def route(nc, ctx, dram, keep, tag):
    def sb(name, shape, dt=F32):
        return ctx.enter_context(nc.sbuf_tensor(tag + name, shape, dt))

    logits = sb("logits", [P, TILES, E])
    scores = sb("scores", [P, TILES, E])
    top = sb("top", [P, TILES])
    total = sb("total", [P, TILES])
    best = sb("best", [P, TILES, 8])
    where = sb("where", [P, TILES, 8], U32)
    where_f = sb("where_f", [P, TOPK, TILES])
    chosen = sb("chosen", [P, TOPK, TILES, E])
    either = sb("either", [P, TILES, E])
    tile_sum = sb("tile_sum", [P, TILES, E])
    run = [sb(f"run{i}", [P, TILES, E]) for i in range(2)]
    place = sb("place", [P, TILES, E])
    slot_f = sb("slot_f", [P, TOPK, TILES])
    whole = sb("whole", [P, E])
    whole_i = sb("whole_i", [P, E], I32)
    end = [sb(f"end{i}", [P, E]) for i in range(2)]
    passed = sb("passed", [P, SLOT_TILES, E])
    expert_f = sb("expert_f", [P, SLOT_TILES])
    ps_t = ctx.enter_context(nc.psum_tensor(tag + "ps_t", [P, 2, T], F32))
    ps_g = ctx.enter_context(nc.psum_tensor(tag + "ps_g", [P, TILES, E], F32))
    ps_c = ctx.enter_context(nc.psum_tensor(tag + "ps_c", [P, TILES, E], F32))
    ps_n = ctx.enter_context(nc.psum_tensor(tag + "ps_n", [P, TILES, E], F32))
    norm = Norm(nc, ctx, keep, tag, keep.rows[:, 0], keep.xnT)
    s = semaphores(nc, ctx, tag + "route", "gate less exp either counts chain")
    block = ctx.enter_context(nc.Block())

    @block.tensor
    def _(pe):
        for b in range(B):
            norm.tensor_turn(nc.tensor, ps_t[:, b % 2, :], b)
        pe.wait_ge(norm.s["xnT"], B)
        for t in range(TILES):
            mm = nc.tensor.matmul(ps_g[:, t, :], keep.xnT[:, t * P:(t + 1) * P], keep.gate_w[:, :], start=True, stop=True)
        mm.then_inc(s["gate"], 1)
        pe.wait_ge(s["either"], 1)
        flat = either[:, :, :].rearrange("p t e -> p (t e)")
        nc.tensor.matmul(ps_c[:, :, :].rearrange("p t e -> p (t e)"), keep.before[:, :], flat, start=True, stop=True)
        nc.tensor.matmul(ps_n[:, :, :].rearrange("p t e -> p (t e)"), keep.ones[:, :], flat, start=True, stop=True).then_inc(s["counts"], 1)

    @block.scalar
    def _(act):
        for b in range(B):
            norm.scalar_std(nc.scalar, b)
        for b in range(B):
            norm.scalar_copy(nc.scalar, ps_t[:, b % 2, :], b)
            at = slice(b * NT, (b + 1) * NT)
            nc.scalar.copy(keep.rows[:, 1, at, 0:D], keep.rows[:, 0, at, 0:D])
        act.wait_ge(s["less"], 1)
        nc.scalar.activation(scores[:, :, :], logits[:, :, :], ACT.Exp).then_inc(s["exp"], 1)

    @block.vector
    def _(dve):
        link = chained(dve, s["chain"])
        v = nc.vector
        for b in range(B):
            norm.vector_stats(v, link, b)
            if b:
                norm.vector_scale(v, link, b - 1)
        norm.vector_scale(v, link, B - 1)
        for k in range(TOPK):
            v.tensor_copy(keep.rows[:, k, :, D].bitcast(I32), keep.token_id[:, k, :].bitcast(I32))
        dve.wait_ge(s["gate"], 1)
        link(v.tensor_tensor(logits[:, :, :], ps_g[:, :, :], keep.gate_b[:, :].unsqueeze(1).to_broadcast([P, TILES, E]), ALU.add))
        link(v.tensor_reduce(top[:, :], logits[:, :, :], AX_X, ALU.max))
        v.tensor_tensor(logits[:, :, :], logits[:, :, :], top[:, :].unsqueeze(2).to_broadcast([P, TILES, E]),
                        ALU.subtract).then_inc(s["less"], 1)
        dve.wait_ge(s["exp"], 1)
        link(v.tensor_reduce(total[:, :], scores[:, :, :], AX_X, ALU.add))
        link(v.reciprocal(total[:, :], total[:, :]))
        link(v.tensor_tensor(scores[:, :, :], scores[:, :, :], total[:, :].unsqueeze(2).to_broadcast([P, TILES, E]), ALU.mult))
        for t in range(TILES):
            last = v.max(best[:, t, :], scores[:, t, :])
        link(last)
        for t in range(TILES):
            last = v.max_index(where[:, t, :], best[:, t, :], scores[:, t, :])
        link(last)
        for k in range(TOPK):
            v.tensor_copy(keep.weight[:, k, :], best[:, :, k])
            last = v.tensor_copy(where_f[:, k, :], where[:, :, k])
        link(last)
        numbers = keep.expert_no[:, :].unsqueeze(1).to_broadcast([P, TILES, E])
        for k in range(TOPK):
            last = v.tensor_tensor(chosen[:, k], where_f[:, k, :].unsqueeze(2).to_broadcast([P, TILES, E]), numbers, ALU.is_equal)
        link(last)
        v.tensor_tensor(either[:, :, :], chosen[:, 0], chosen[:, 1], ALU.add).then_inc(s["either"], 1)
        dve.wait_ge(s["counts"], 1)
        link(v.tensor_copy(tile_sum[:, :, :], ps_n[:, :, :]))
        src, step, i = tile_sum, 1, 0
        while step < TILES:
            v.tensor_copy(run[i][:, 0:step, :], src[:, 0:step, :])
            link(v.tensor_tensor(run[i][:, step:, :], src[:, step:, :], src[:, 0:TILES - step, :], ALU.add))
            src, step, i = run[i], 2 * step, 1 - i
        incl = src
        link(v.tensor_scalar(whole[:, :], incl[:, TILES - 1, :], float(P - 1), None, ALU.add))
        link(v.tensor_copy(whole_i[:, :], whole[:, :]))
        link(v.tensor_scalar(whole_i[:, :], whole_i[:, :], P.bit_length() - 1, None, ALU.arith_shift_right))
        link(v.tensor_copy(whole[:, :], whole_i[:, :]))
        src2, step, j = whole, 1, 0
        while step < E:
            v.tensor_copy(end[j][:, 0:step], src2[:, 0:step])
            link(v.tensor_tensor(end[j][:, step:], src2[:, step:], src2[:, 0:E - step], ALU.add))
            src2, step, j = end[j], 2 * step, 1 - j
        ends = src2
        v.tensor_tensor(passed[:, :, :], keep.tile_no[:, :].unsqueeze(2).to_broadcast([P, SLOT_TILES, E]),
                        ends[:, :].unsqueeze(1).to_broadcast([P, SLOT_TILES, E]), ALU.is_ge)
        link(v.tensor_tensor(whole[:, :], ends[:, :], whole[:, :], ALU.subtract))
        link(v.tensor_scalar(whole[:, :], whole[:, :], float(P), None, ALU.mult))
        link(v.tensor_reduce(expert_f[:, :], passed[:, :, :], AX_X, ALU.add))
        link(v.tensor_scalar(expert_f[:, :], expert_f[:, :], float(E - 1), None, ALU.min))
        v.tensor_copy(keep.expert[:, :], expert_f[:, :])
        link(v.tensor_tensor(place[:, :, :], incl[:, :, :], tile_sum[:, :, :], ALU.subtract))
        link(v.tensor_tensor(place[:, :, :], ps_c[:, :, :], place[:, :, :], ALU.add))
        link(v.tensor_tensor(place[:, :, :], place[:, :, :], whole[:, :].unsqueeze(1).to_broadcast([P, TILES, E]), ALU.add))
        for k in range(TOPK):
            last = v.tensor_tensor(chosen[:, k], chosen[:, k], place[:, :, :], ALU.mult)
        link(last)
        for k in range(TOPK):
            last = v.tensor_reduce(slot_f[:, k, :], chosen[:, k], AX_X, ALU.add)
        link(last)
        link(v.tensor_copy(keep.slot[:, :, :], slot_f[:, :, :]))


XS_RING = 8
Y_RING = 4


def experts(nc, ctx, dram, keep, tag, slots_dram, parted_dram, out):
    def sb(name, shape, dt=F32):
        return ctx.enter_context(nc.sbuf_tensor(tag + name, shape, dt))

    sil = sb("sil", [P, 2, 3, HALFQ])
    up = sb("up", [P, 2, 3, HALFQ])
    xs = sb("xs", [P, XS_RING, ROW])
    xsT = sb("xsT", [P, 2, P])
    hg = sb("hg", [P, 2, 2 * F])
    act_h = sb("act_h", [P, 2, F])
    a = sb("a", [P, 2, 2 * P])
    aT = sb("aT", [P, 2, 2 * P])
    y = sb("y", [P, Y_RING, D])
    back = sb("back", [P, 2, NT, TOPK * D])
    ps = ctx.enter_context(nc.psum_tensor(tag + "ps", [P, 8, 512], F32))
    s = semaphores(nc, ctx, tag + "expert", "scattered hidden sil up out added chain xs0 xs1 xs2 xs3 xs4 xs5 xs6 xs7 xT_ps xT h hg act_h a a_ready aT_ps aT "
             "y_ps y sent0 sent1 sent2 sent3 back0 back1 combined")
    xs_in = [s["xs0"], s["xs1"], s["xs2"], s["xs3"], s["xs4"], s["xs5"], s["xs6"], s["xs7"]]
    sent = [s["sent0"], s["sent1"], s["sent2"], s["sent3"]]
    back_in = [s["back0"], s["back1"]]
    CH = [min(P, SF - c * P) for c in range(3)]
    QUADS = B * T // HALFQ
    N = SLOT_TILES
    block = ctx.enter_context(nc.Block())

    def ps_shared(q, c, which):
        return ps[:, 2 * ((3 * q + c) % 3) + which, :]

    @block.sync
    def _(sp):
        def store(b):
            if out is not None:
                sp.dma_start(out[b].rearrange("(t p) d -> p t d", p=P), keep.x[:, b * NT:(b + 1) * NT, :]).then_inc(keep.stored, 16)

        sp.wait_ge(s["scattered"], 16 * TOPK * TILES)
        for i in range(N):
            r = i % XS_RING
            if i >= XS_RING:
                j = i - XS_RING
                sp.wait_ge(sent[j % Y_RING], 16 * (j // Y_RING + 1))
            sp.dma_start(xs[:, r, :], slots_dram[i * P:(i + 1) * P, :]).then_inc(xs_in[r], 16)
        for j in range(Y_RING):
            sp.wait_ge(sent[j], 16 * (N // Y_RING))
        for b in range(B):
            if b >= 2:
                sp.wait_ge(s["combined"], b - 1)
                store(b - 2)
            src = parted_dram[b * T * TOPK:(b + 1) * T * TOPK, :].rearrange("(t p k) d -> p t (k d)", p=P, k=TOPK)
            sp.dma_start(back[:, b % 2, :, :], src).then_inc(back_in[b % 2], 16)
        for b in (B - 2, B - 1):
            sp.wait_ge(s["combined"], b + 1)
            store(b)
        if out is not None:
            sp.wait_ge(keep.stored, 16 * B)

    @block.gpsimd
    def _(pool):
        for t in range(TILES):
            for k in range(TOPK):
                nc.gpsimd.indirect_dma_start(out=slots_dram, out_offset=bass.IndirectOffsetOnAxis(ap=keep.slot[:, k, t:t + 1], axis=0),
                                             in_=keep.rows[:, k, t, :], in_offset=None).then_inc(s["scattered"], 16)
        for i in range(N):
            pool.wait_ge(s["y"], i + 1)
            where = xs[:, i % XS_RING, D:D + 1].bitcast(I32)
            nc.gpsimd.indirect_dma_start(out=parted_dram, out_offset=bass.IndirectOffsetOnAxis(ap=where, axis=0),
                                         in_=y[:, i % Y_RING, :], in_offset=None).then_inc(sent[i % Y_RING], 16)

    @block.tensor
    def _(pe):
        def shared_up(q):
            for c in range(3):
                n = 3 * q + c
                if n >= 3:
                    pe.wait_ge(s["up"], n - 2)
                for which, w in enumerate((keep.sw1, keep.sw3)):
                    mm = nc.tensor.matmul(ps[0:CH[c], 2 * (n % 3) + which, :], w[:, c * P:c * P + CH[c]],
                                          keep.xnT[:, q * HALFQ:(q + 1) * HALFQ], start=True, stop=True)
                mm.then_inc(s["hidden"], 1)

        def shared_down(q):
            pe.wait_ge(s["up"], 3 * q + 3)
            if q >= 2:
                pe.wait_ge(s["added"], q - 1)
            for t in range(HALFQ // P):
                for c in range(3):
                    rows = CH[c] + (c == 2)
                    mm = nc.tensor.matmul(ps[:, 6 + q % 2, t * P:(t + 1) * P], up[0:rows, q % 2, c, t * P:(t + 1) * P],
                                          keep.sw2[0:rows, c, :], start=(c == 0), stop=(c == 2))
            mm.then_inc(s["out"], 1)

        for q in range(QUADS):
            shared_up(q)
            if q:
                shared_down(q - 1)
        shared_down(QUADS - 1)
        pe.wait_ge(s["added"], QUADS)

        for i in range(N + 4):
            if i < N:
                pe.wait_ge(xs_in[i % XS_RING], 16 * (i // XS_RING + 1))
                if i >= 2:
                    pe.wait_ge(s["xT"], i - 1)
                nc.tensor.transpose(ps[:, i % 2, 0:P], xs[:, i % XS_RING, 0:D], keep.ident[:, :]).then_inc(s["xT_ps"], 1)
            if 1 <= i <= N:
                j = i - 1
                e = nc.tensor.value_load(keep.expert[0:1, j:j + 1], min_val=0, max_val=E - 1)
                pe.wait_ge(s["xT"], j + 1)
                if j >= 2:
                    pe.wait_ge(s["hg"], j - 1)
                w = keep.w13[:, :, :, :].rearrange("p e i f -> p (e i f)")[:, bass.ds(e * (2 * F), 2 * F)]
                nc.tensor.matmul(ps[:, 2 + j % 2, 0:2 * F], xsT[:, j % 2, :], w, start=True, stop=True).then_inc(s["h"], 1)
            if 3 <= i < N + 3:
                j = i - 3
                pe.wait_ge(s["a"], j + 1)
                if j >= 2:
                    pe.wait_ge(s["aT"], j - 1)
                for c in range(2):
                    mm = nc.tensor.transpose(ps[:, 4 + j % 2, c * P:(c + 1) * P], a[:, j % 2, c * P:(c + 1) * P], keep.ident[:, :])
                mm.then_inc(s["aT_ps"], 1)
            if 4 <= i:
                j = i - 4
                e = nc.tensor.value_load(keep.expert[0:1, j:j + 1], min_val=0, max_val=E - 1)
                pe.wait_ge(s["aT"], j + 1)
                if j >= 2:
                    pe.wait_ge(s["y"], j - 1)
                for c in range(2):
                    w = keep.w2[:, :, :, :].rearrange("p e c d -> p (e c d)")[:, bass.ds(e * (2 * D) + c * D, D)]
                    mm = nc.tensor.matmul(ps[:, 6 + j % 2, 0:D], aT[:, j % 2, c * P:(c + 1) * P], w, start=(c == 0), stop=(c == 1))
                mm.then_inc(s["y_ps"], 1)

    @block.scalar
    def _(act):
        for q in range(QUADS):
            for c in range(3):
                n = 3 * q + c
                act.wait_ge(s["hidden"], n + 1)
                if q >= 2:
                    act.wait_ge(s["up"], n - 5)
                nc.scalar.activation(sil[0:CH[c], q % 2, c, :], ps[0:CH[c], 2 * (n % 3), :], ACT.Silu,
                                     bias=keep.sbias[0:CH[c], 0, c:c + 1]).then_inc(s["sil"], 1)
        for i in range(N + 3):
            if i < N:
                act.wait_ge(s["xT_ps"], i + 1)
                if i >= 2:
                    act.wait_ge(s["h"], i - 1)
                nc.scalar.copy(xsT[:, i % 2, :], ps[:, i % 2, 0:P]).then_inc(s["xT"], 1)
            if 1 <= i <= N:
                j = i - 1
                act.wait_ge(s["hg"], j + 1)
                if j >= 2:
                    act.wait_ge(s["a"], j - 1)
                nc.scalar.activation(act_h[:, j % 2, :], hg[:, j % 2, 0:F], ACT.Silu).then_inc(s["act_h"], 1)
            if 3 <= i:
                j = i - 3
                act.wait_ge(s["aT_ps"], j + 1)
                if j >= 2:
                    act.wait_ge(s["y_ps"], j - 1)
                nc.scalar.copy(aT[:, j % 2, :], ps[:, 4 + j % 2, 0:2 * P]).then_inc(s["aT"], 1)

    @block.vector
    def _(dve):
        v = nc.vector
        link = chained(dve, s["chain"])
        for h in range(2):
            v.memset(up[SF - 2 * P:SF - 2 * P + 1, h, 2, :], 1.0)
        v.memset(a[:, :, F + 1:2 * P], 0.0)
        v.memset(a[:, :, F:F + 1], 1.0)

        def shared_add(q):
            dve.wait_ge(s["out"], q + 1)
            xq = keep.x[:, q * GROUP:(q + 1) * GROUP, :]
            v.tensor_tensor(xq, ps[:, 6 + q % 2, :].rearrange("p (t d) -> p t d", t=GROUP), xq, ALU.add).then_inc(s["added"], 1)

        for q in range(QUADS):
            for c in range(3):
                n = 3 * q + c
                dve.wait_ge(s["sil"], n + 1)
                if q >= 2 and c == 0:
                    dve.wait_ge(s["out"], q - 1)
                v.scalar_tensor_tensor(out=up[0:CH[c], q % 2, c, :], in0=ps[0:CH[c], 2 * (n % 3) + 1, :],
                                       scalar=keep.sbias[0:CH[c], 1, c:c + 1], in1=sil[0:CH[c], q % 2, c, :],
                                       op0=ALU.add, op1=ALU.mult).then_inc(s["up"], 1)
            if q:
                shared_add(q - 1)
        shared_add(QUADS - 1)
        for i in range(N + 3):
            if i < N:
                e = v.value_load(keep.expert[0:1, i:i + 1], min_val=0, max_val=E - 1)
                dve.wait_ge(s["h"], i + 1)
                if i >= 2:
                    dve.wait_ge(s["a"], i - 1)
                bias = keep.b13[:, :, :, :].rearrange("p e i f -> p (e i f)")[:, bass.ds(e * (2 * F), 2 * F)]
                v.tensor_tensor(hg[:, i % 2, :], ps[:, 2 + i % 2, 0:2 * F], bias, ALU.add).then_inc(s["hg"], 1)
            if 1 <= i <= N:
                j = i - 1
                dve.wait_ge(s["act_h"], j + 1)
                if j >= 2:
                    dve.wait_ge(s["aT_ps"], j - 1)
                v.tensor_tensor(a[:, j % 2, 0:F], act_h[:, j % 2, :], hg[:, j % 2, F:2 * F], ALU.mult).then_inc(s["a"], 1)
            if 3 <= i:
                j = i - 3
                dve.wait_ge(s["y_ps"], j + 1)
                if j >= Y_RING:
                    dve.wait_ge(sent[j % Y_RING], 16 * (j // Y_RING))
                v.tensor_copy(y[:, j % Y_RING, :], ps[:, 6 + j % 2, 0:D]).then_inc(s["y"], 1)
        for b in range(B):
            dve.wait_ge(back_in[b % 2], 16 * (b // 2 + 1))
            for k in range(TOPK):
                for t in range(NT):
                    g = b * NT + t
                    last = v.scalar_tensor_tensor(out=keep.x[:, g, :], in0=back[:, b % 2, t, k * D:(k + 1) * D],
                                                  scalar=keep.weight[:, k, g:g + 1], in1=keep.x[:, g, :],
                                                  op0=ALU.mult, op1=ALU.add)
                if k == 0:
                    link(last)
            last.then_inc(s["combined"], 1)


def feed_forward(nc, ctx, dram, keep, tag, slots_dram, parted_dram, out=None):
    def sb(name, shape, dt=F32):
        return ctx.enter_context(nc.sbuf_tensor(tag + name, shape, dt))

    keep.rows = sb("rows", [P, TOPK, TILES, ROW])
    keep.xnT = sb("xnT", [P, B * T])
    keep.weight = sb("weight", [P, TOPK, TILES])
    keep.slot = sb("slot", [P, TOPK, TILES], I32)
    keep.expert = sb("expert", [P, SLOT_TILES], I32)
    with ExitStack() as c:
        route(nc, c, dram, keep, tag + "r_")
    with ExitStack() as c:
        experts(nc, c, dram, keep, tag + "e_", slots_dram, parted_dram, out)


def state_space(nc, ctx, dram, keep):
    def sb(name, shape, dt=F32):
        return ctx.enter_context(nc.sbuf_tensor(name, shape, dt))

    xn = sb("s_xn", [P, TILES, D])
    xnT = sb("s_xnT", [P, B * T])
    hs = sb("s_hs", [P, B, T])
    ps_t = ctx.enter_context(nc.psum_tensor("s_ps_t", [P, 2, T], F32))
    ps = ctx.enter_context(nc.psum_tensor("s_ps", [P, 4, 512], F32))
    norm = Norm(nc, ctx, keep, "s_", xn, xnT)
    s = semaphores(nc, ctx, "scan", "chain driven taken moved merged projected added")
    block = ctx.enter_context(nc.Block())

    def moves():
        out = []
        for up in (True, False):
            for level in (range(LEVELS) if up else reversed(range(LEVELS - 1))):
                c = 2 << level
                m = T // c
                cols = m if up else m - 1
                per = min(B, 512 // (m if m <= 512 else 512))
                tree = hs[:, :, :].rearrange("p b (m c) -> p b m c", c=c)
                for b in range(0, B, per):
                    if up:
                        src, dst = tree[:, b:b + per, :, c // 2 - 1], tree[:, b:b + per, :, c - 1]
                    else:
                        src, dst = tree[:, b:b + per, 0:cols, c - 1], tree[:, b:b + per, 1:m, c // 2 - 1]
                    out.append((level, b, per, cols, src, dst))
        return out

    plan = moves()
    needs, last_of = [], [0] * B
    for n, (_, b, per, *_) in enumerate(plan):
        needs.append(max(last_of[b:b + per]))
        for i in range(b, b + per):
            last_of[i] = n + 1

    def result(n):
        _, _, per, cols, _, _ = plan[n]
        return ps[:, n % 4, 0:per * cols].rearrange("p (b m) -> p b m", b=per)

    @block.tensor
    def _(pe):
        for b in range(B):
            norm.tensor_turn(nc.tensor, ps_t[:, b % 2, :], b)
        for n in range(B * T // 512):
            if n % 2 == 0:
                pe.wait_ge(norm.s["xnT"], n // 2 + 1)
            if n >= 4:
                pe.wait_ge(s["taken"], n - 3)
            nc.tensor.matmul(ps[:, n % 4, :], keep.b_T[:, :], xnT[:, n * 512:(n + 1) * 512], start=True, stop=True).then_inc(s["driven"], 1)
        pe.wait_ge(s["taken"], B * T // 512)
        for n, (level, b, per, cols, src, _) in enumerate(plan):
            need = max(needs[n], n - 3)
            if need > 0:
                pe.wait_ge(s["merged"], need)
            nc.tensor.matmul(result(n), keep.a_powT[:, level, :], src, start=True, stop=True).then_inc(s["moved"], 1)
        pe.wait_ge(s["merged"], len(plan))
        flat = hs[:, :, :].rearrange("p b t -> p (b t)")
        for g in range(TILES // GROUP):
            if g >= 4:
                pe.wait_ge(s["added"], g - 3)
            for t in range(GROUP):
                at = (g * GROUP + t) * P
                mm = nc.tensor.matmul(ps[:, g % 4, t * P:(t + 1) * P], flat[:, at:at + P], keep.c_T[:, :], start=True, stop=True)
            mm.then_inc(s["projected"], 1)

    @block.scalar
    def _(act):
        for b in range(B):
            norm.scalar_std(nc.scalar, b)
        for b in range(B):
            norm.scalar_copy(nc.scalar, ps_t[:, b % 2, :], b)
        flat = hs[:, :, :].rearrange("p b t -> p (b t)")
        for n in range(B * T // 512):
            act.wait_ge(s["driven"], n + 1)
            nc.scalar.copy(flat[:, n * 512:(n + 1) * 512], ps[:, n % 4, :]).then_inc(s["taken"], 1)

    @block.vector
    def _(dve):
        link = chained(dve, s["chain"])
        v = nc.vector
        for b in range(B):
            norm.vector_stats(v, link, b)
            if b:
                norm.vector_scale(v, link, b - 1)
        norm.vector_scale(v, link, B - 1)
        dve.wait_ge(s["taken"], B * T // 512)
        for n, (*_, dst) in enumerate(plan):
            dve.wait_ge(s["moved"], n + 1)
            if needs[n] > 0:
                dve.wait_ge(s["merged"], needs[n])
            v.tensor_tensor(dst, result(n), dst, ALU.add).then_inc(s["merged"], 1)
        for g in range(TILES // GROUP):
            dve.wait_ge(s["projected"], g + 1)
            xs = keep.x[:, g * GROUP:(g + 1) * GROUP, :]
            v.tensor_tensor(xs, ps[:, g % 4, :].rearrange("p (t d) -> p t d", t=GROUP), xs, ALU.add).then_inc(s["added"], 1)


def hybrid_kernel(nc, inp, out):
    dram = inp
    keep = Keep()
    with ExitStack() as ctx:
        def sb(name, shape, dt=F32):
            return ctx.enter_context(nc.sbuf_tensor(name, shape, dt))
        keep.x = sb("x", [P, TILES, D])
        keep.ident = sb("ident", [P, P])
        keep.ones = sb("ones", [P, P])
        keep.eps = sb("eps", [P, 1])
        keep.u_last = sb("u_last", [P, 3])
        keep.a_nat, keep.a_T = sb("a_nat", [P, P]), sb("a_T", [P, P])
        keep.b_T, keep.c_T = sb("b_T", [P, P]), sb("c_T", [P, P])
        keep.a_powT = sb("a_powT", [P, LEVELS, P])
        slots = [nc.dram_tensor(f"slots{i}", [SLOTS, ROW], F32).ap() for i in range(2)]
        parted = [nc.dram_tensor(f"parted{i}", [B * T * TOPK + SLOTS, D], F32).ap() for i in range(2)]
        keep.stored = ctx.enter_context(nc.semaphore("stored"))
        keep.q_parts = nc.dram_tensor("q_parts", [PARTS, P, B * T], BF16).ap()
        keep.k_parts = nc.dram_tensor("k_parts", [PARTS, P, B * T], BF16).ap()
        with ExitStack() as attn_ctx:
            keep.attn = attn_ctx.enter_context(nc.sbuf_tensor("attn", [P, TILES, D], F32))
            keep.v = attn_ctx.enter_context(nc.sbuf_tensor("v", [P, TILES, H, HD + 1], F32))
            with ExitStack() as c:
                load_and_project(nc, c, dram, keep)
            with ExitStack() as c:
                attention(nc, c, dram, keep)
            with ExitStack() as c:
                project_out(nc, c, dram, keep)
        with ExitStack() as c:
            clear_slots(nc, c, dram, slots)
        load_expert_weights(nc, ctx, dram, keep)
        with ExitStack() as c:
            feed_forward(nc, c, dram, keep, "f1", slots[0], parted[0])
        with ExitStack() as c:
            state_space(nc, c, dram, keep)
        with ExitStack() as c:
            feed_forward(nc, c, dram, keep, "f2", slots[1], parted[1], out)


def clear_slots(nc, ctx, dram, slots):
    s = ctx.enter_context(nc.semaphore("cleared"))
    block = ctx.enter_context(nc.Block())

    @block.sync
    def _(sp):
        for d in slots:
            sp.dma_start(d.rearrange("(a b) c -> a (b c)", a=P), dram["slot_rows"].rearrange("(a b) c -> a (b c)", a=P)).then_inc(s, 16)
        sp.wait_ge(s, 32)

NAMES = {
    "x": "L0_attn_a_x", "w_q": "L0_attn_a_W_q", "w_dkv": "L0_attn_a_W_dkv", "w_uk": "L0_attn_a_W_uk",
    "w_uv": "L0_attn_a_W_uv", "w_o": "L0_attn_a_W_o", "ln_gamma": "L0_attn_a_ln_gamma", "ln_beta": "L0_attn_a_ln_beta",
    "w_a": "L0_attn_b_W_A", "w_b": "L0_attn_b_W_B", "w_c": "L0_attn_b_W_C",
    "gate_w": "L0_ffn_gate_w", "gate_b": "L0_ffn_gate_b", "w1": "L0_ffn_w1", "b1": "L0_ffn_b1", "w3": "L0_ffn_w3",
    "b3": "L0_ffn_b3", "w2": "L0_ffn_w2", "b2": "L0_ffn_b2", "sw1": "L0_ffn_sw1", "sb1": "L0_ffn_sb1",
    "sw3": "L0_ffn_sw3", "sb3": "L0_ffn_sb3", "sw2": "L0_ffn_sw2", "sb2": "L0_ffn_sb2",
}


def shape_constants():
    f = np.float32
    inv_freq = (f(1.0) / f(10000.0) ** (np.arange(HALF, dtype=f) / f(HALF))).astype(f)
    angles = (np.arange(T, dtype=f)[:, None] * inv_freq[None, :]).astype(f)
    rows = np.zeros((SLOTS, ROW), f)
    rows[:, D] = (np.arange(SLOTS, dtype=np.int32) + B * T * TOPK).view(f)
    tokens = np.arange(TILES)[None, :] * P + np.arange(P)[:, None]
    token_id = np.ascontiguousarray(np.stack([tokens * TOPK + k for k in range(TOPK)], axis=1).astype(np.int32))
    return {
        "cos": np.ascontiguousarray(np.cos(angles).astype(f).reshape(NT, P, HALF).transpose(1, 0, 2)),
        "sin": np.ascontiguousarray(np.sin(angles).astype(f).reshape(NT, P, HALF).transpose(1, 0, 2)),
        "ident": np.eye(P, dtype=f),
        "before": np.triu(np.ones((P, P), f), 1),
        "expert_no": np.arange(E, dtype=f),
        "tile_no": np.arange(SLOT_TILES, dtype=f),
        "token_id": token_id.view(f),
        "slot_rows": rows,
    }


def kernel(**inputs):
    import concourse.bacc as bacc
    from concourse.bass_utils import run_bass_kernel_spmd

    nc = bacc.Bacc("TRN2", target_bir_lowering=False, num_devices=1)
    arrays, inp = {}, {}
    held = {short: np.ascontiguousarray(inputs[name]) for short, name in NAMES.items()}
    for short, a in {**held, **shape_constants()}.items():
        arrays[f"in_{short}"] = a
        inp[short] = nc.dram_tensor(f"in_{short}", a.shape, mybir.dt.from_np(a.dtype), kind="ExternalInput").ap()
    out = nc.dram_tensor("out", (B, T, D), F32, kind="ExternalOutput").ap()
    hybrid_kernel(nc, inp, out)
    r = run_bass_kernel_spmd(nc, [arrays], core_ids=[0])
    return r.results[0]["out"]
```

```python
from contextlib import ExitStack

import numpy as np
import concourse.bass as bass
from concourse import mybir

F32 = mybir.dt.float32
BF16 = mybir.dt.bfloat16
I32 = mybir.dt.int32
U32 = mybir.dt.uint32
ALU = mybir.AluOpType
ACT = mybir.ActivationFunctionType
AX_X = mybir.AxisListType.X

P = 128
B, T, D = 4, 1024, 128
NT = T // P
TILES = B * NT
H, HD = 16, 8
HALF = HD // 2
LAT = 32
EPS = 1e-5
SCALE = 1.0 / float(np.sqrt(np.float32(HD)))
PARTS = 3
HT = NT // 2
HALVES = 2 * B
Q_TURN, K_TURN = 4, 8
POWER_ITERS = 10
HALF_STEPS = 2 * POWER_ITERS + 1
ROWS3 = 3 * 32

E, TOPK = 16, 2
F = 176
FH = F - P
SF = 2 * F
SLOT_TILES = B * T * TOPK // P + E
SLOTS = SLOT_TILES * P
ROW = D + 1


def semaphores(nc, ctx, phase, names):
    made = {n: nc.alloc_semaphore(f"{phase}_{n}") for n in names.split()}

    def give_back():
        nc.clear_and_free_semaphores(list(made.values()))
        nc.all_engine_barrier()

    ctx.callback(give_back)
    return made


class Keep:
    pass


def chained(engine, sem):
    done = [0]

    def link(ins):
        done[0] += 1
        ins.then_inc(sem, 1)
        engine.wait_ge(sem, done[0])

    return link


def load_and_project(nc, ctx, dram, keep):
    def sb(name, shape, dt=F32):
        return ctx.enter_context(nc.sbuf_tensor(name, shape, dt))

    x = keep.x
    xn = sb("a_xn", [P, TILES, D])
    xnT = sb("a_xnT", [P, TILES, P])
    stats = sb("a_stats", [P, TILES, 6])
    mv = sb("a_mv", [P, TILES, 2])
    std = sb("a_std", [P, TILES])
    rstd = sb("a_rstd", [P, TILES])
    lstats = sb("a_lstats", [P, TILES, 6])
    lmv = sb("a_lmv", [P, TILES, 2])
    lstd = sb("a_lstd", [P, TILES])
    lrstd = sb("a_lrstd", [P, TILES])
    w_in = sb("a_w_in", [P, D + LAT])
    w_kv = sb("a_w_kv", [P, 2 * D])
    gamma = sb("a_gamma", [P, LAT])
    beta = sb("a_beta", [P, LAT])
    cos = sb("a_cos", [P, NT, HALF])
    sin = sb("a_sin", [P, NT, HALF])
    q = keep.w13[:, :, :, :].rearrange("p e i f -> p (e i f)")[:, 0:TILES * (D + LAT)].rearrange("p (t c) -> p t c", c=D + LAT)
    k = keep.b13[:, :, :, :].rearrange("p e i f -> p (e i f)")[:, 0:TILES * D].rearrange("p (t c) -> p t c", c=D)
    tmp_q = sb("a_tmp_q", [P, HT, H, HALF])
    tmp_k = sb("a_tmp_k", [P, HT, H, HALF])
    lat = sb("a_lat", [P, TILES, P])
    latn = sb("a_latn", [P, HT, LAT])
    latT = sb("a_latT", [P, 2, HT * P])
    parts = sb("a_parts", [P, 2, 2, PARTS, HT * P], BF16)
    w_ssm = sb("a_w_ssm", [P, 3, P])
    w_ssmT = sb("a_w_ssmT", [P, 3, P])
    uv = sb("a_uv", [P, 3])
    squares = sb("a_squares", [ROWS3, P])
    unit = sb("a_unit", [ROWS3, P])
    u_last = sb("a_u_last", [ROWS3, P])
    sq_sum = sb("a_sq_sum", [ROWS3, 1])
    norm = sb("a_norm", [ROWS3, 1])
    inv = sb("a_inv", [ROWS3, 1])
    pick = sb("a_pick", [ROWS3, 3])
    sigma = sb("a_sigma", [P, 3])
    qr, kr = xn, lat
    rest = xnT
    ps_t = ctx.enter_context(nc.psum_tensor("a_ps_t", [P, 2, HT * P], F32))
    ps_p = ctx.enter_context(nc.psum_tensor("a_ps_p", [P, 2, HT, 256], F32))
    ps_w = ctx.enter_context(nc.psum_tensor("a_ps_w", [P, 512], F32))
    ps_s = ctx.enter_context(nc.psum_tensor("a_ps_s", [P, 512], F32))
    s = semaphores(nc, ctx, "project", "x_in0 x_in1 x_in2 x_in3 ident tables w_in w_kv ssm zeroed eps mv std xn xnT_ps xnT "
             "proj q_sb lmv lstd lat_sb latT_ps latT kv k_sb v_sb qr kr chain_v chain_p "
             "qT kT q_h k_h q_rest k_rest q_m k_m q_l k_l pw_mv pw_ss pw_std pw_unit pw_turned pw_uv wT_ps wT scaled "
             "sent_q0 sent_q1 sent_k0 sent_k1")
    x_in = [s["x_in0"], s["x_in1"], s["x_in2"], s["x_in3"]]
    sent = [[s["sent_q0"], s["sent_q1"]], [s["sent_k0"], s["sent_k1"]]]
    block = ctx.enter_context(nc.Block())

    def tiles(h):
        return slice(h * HT, (h + 1) * HT)

    def live(h):
        return 0 <= h < HALVES

    def rope(engine, link, src, dst, tmp, h, done):
        at = slice(h * HT % NT, h * HT % NT + HT)
        i = src[:, tiles(h), 0:D].rearrange("p t (h s d) -> p t h s d", s=2, d=HALF)
        o = dst[:, tiles(h), :].rearrange("p t (s d h) -> p t h s d", s=2, d=HALF)
        c = cos[:, at, :].unsqueeze(2).to_broadcast([P, HT, H, HALF])
        n = sin[:, at, :].unsqueeze(2).to_broadcast([P, HT, H, HALF])
        link(engine.tensor_tensor(o[:, :, :, 0, :], i[:, :, :, 0, :], c, ALU.mult))
        link(engine.tensor_tensor(tmp[:, :, :, :], i[:, :, :, 1, :], n, ALU.mult))
        link(engine.tensor_tensor(o[:, :, :, 0, :], o[:, :, :, 0, :], tmp[:, :, :, :], ALU.subtract))
        link(engine.tensor_tensor(o[:, :, :, 1, :], i[:, :, :, 0, :], n, ALU.mult))
        link(engine.tensor_tensor(tmp[:, :, :, :], i[:, :, :, 1, :], c, ALU.mult))
        engine.tensor_tensor(o[:, :, :, 1, :], o[:, :, :, 1, :], tmp[:, :, :, :], ALU.add).then_inc(done, 1)
        engine.wait_ge(done, h + 1)

    @block.sync
    def _(sp):
        def load_x(b):
            sp.dma_start(x[:, b * NT:(b + 1) * NT, :], dram["x"][b].rearrange("(t p) d -> p t d", p=P)).then_inc(x_in[b], 16)

        load_x(0)
        sp.dma_start(keep.ident[:, :], dram["ident"]).then_inc(s["ident"], 16)
        for i, w in enumerate((dram["w_a"], dram["w_b"], dram["w_c"])):
            sp.dma_start(w_ssm[:, i, :], w).then_inc(s["ssm"], 16)
        sp.dma_start(w_in[:, 0:D], dram["w_q"]).then_inc(s["w_in"], 16)
        sp.dma_start(w_in[:, D:D + LAT], dram["w_dkv"]).then_inc(s["w_in"], 16)
        load_x(1)
        sp.dma_start(cos[:, :, :], dram["cos"]).then_inc(s["tables"], 16)
        sp.dma_start(sin[:, :, :], dram["sin"]).then_inc(s["tables"], 16)
        sp.dma_start(gamma[:, :], dram["ln_gamma"].partition_broadcast(P)).then_inc(s["tables"], 16)
        sp.dma_start(beta[:, :], dram["ln_beta"].partition_broadcast(P)).then_inc(s["tables"], 16)
        sp.dma_start(w_kv[0:LAT, 0:D], dram["w_uk"]).then_inc(s["w_kv"], 16)
        sp.dma_start(w_kv[0:LAT, D:2 * D], dram["w_uv"]).then_inc(s["w_kv"], 16)
        load_x(2)
        load_x(3)
        for h in range(HALVES + 2):
            for n, (out, ready, j) in enumerate(((keep.q_parts, s["q_l"], h), (keep.k_parts, s["k_l"], h - 2))):
                if live(j):
                    sp.wait_ge(ready, j + 1)
                    at = slice(j * HT * P, (j + 1) * HT * P)
                    sp.dma_start(out[:, :, at].rearrange("i r t -> r i t"), parts[:, n, j % 2, :, :]).then_inc(sent[n][j % 2], 16)
        for done in sent[0] + sent[1]:
            sp.wait_ge(done, 16 * HALVES // 2)

    @block.gpsimd
    def _(pool):
        link = chained(pool, s["chain_p"])
        nc.gpsimd.memset(keep.eps[:, :], EPS).then_inc(s["eps"], 1)
        pool.wait_ge(s["eps"], 1)
        for g in range(1, P // LAT):
            nc.gpsimd.memset(w_kv[g * LAT:(g + 1) * LAT, :], 0.0).then_inc(s["zeroed"], 1)
            pool.wait_ge(s["zeroed"], g)
        nc.gpsimd.memset(lat[:, :, :], 0.0).then_inc(s["zeroed"], 1)
        pool.wait_ge(s["tables"], 64)

        def last_part(n, j, middle, done):
            pool.wait_ge(middle, j + 1)
            r = rest[:, tiles(j), :].rearrange("p t c -> p (t c)")
            nc.gpsimd.tensor_tensor(parts[:, n, j % 2, 2, :], r, parts[:, n, j % 2, 1, :], ALU.subtract).then_inc(done, 1)
            pool.wait_ge(done, j + 1)

        for h in range(HALVES + 2):
            if live(h):
                last_part(0, h, s["q_m"], s["q_l"])
                pool.wait_ge(s["k_sb"], h + 1)
                rope(nc.gpsimd, link, k, kr, tmp_k, h, s["kr"])
            if live(h - 2):
                last_part(1, h - 2, s["k_m"], s["k_l"])

    @block.tensor
    def _(pe):
        def vectors(n):
            if n > HALF_STEPS:
                return
            w = w_ssm if n % 2 == 0 else w_ssmT
            pe.wait_ge(s["pw_uv"], n + 1)
            for i in range(3):
                mm = nc.tensor.matmul(ps_w[32 * i:32 * i + 1, 0:P], uv[:, i:i + 1], w[:, i, :], start=True, stop=True)
            mm.then_inc(s["pw_mv"], 1)

        def turn_vectors(n):
            if n > HALF_STEPS:
                return
            pe.wait_ge(s["pw_unit"], n + 1)
            if n < HALF_STEPS:
                nc.tensor.transpose(ps_s[:, 0:ROWS3], unit[:, :], keep.ident[0:ROWS3, 0:ROWS3]).then_inc(s["pw_turned"], 1)
            else:
                nc.tensor.matmul(ps_s[:, 0:3], unit[:, :], pick[:, :], start=True, stop=True).then_inc(s["pw_turned"], 1)

        def turn(src, h, bank, done):
            for t in range(HT):
                mm = nc.tensor.transpose(ps_t[:, bank, t * P:(t + 1) * P], src[:, h * HT + t, :], keep.ident[:, :])
            mm.then_inc(done, 1)

        pe.wait_ge(s["ident"], 16)
        pe.wait_ge(s["ssm"], 48)
        for i in range(3):
            mm = nc.tensor.transpose(ps_s[:, i * P:(i + 1) * P], w_ssm[:, i, :], keep.ident[:, :])
        mm.then_inc(s["wT_ps"], 1)
        for i in range(HALVES + K_TURN):
            vectors(2 * i)
            if live(i):
                pe.wait_ge(s["xn"], i + 1)
                if i:
                    pe.wait_ge(s["xnT"], i)
                if live(i - Q_TURN - 1):
                    pe.wait_ge(s["q_rest"], i - Q_TURN)
                turn(xn, i, 0, s["xnT_ps"])
            if live(i - 1):
                j = i - 1
                if j == 0:
                    pe.wait_ge(s["w_in"], 32)
                pe.wait_ge(s["xnT"], j + 1)
                if j:
                    pe.wait_ge(s["q_sb"], j)
                for t in range(HT):
                    mm = nc.tensor.matmul(ps_p[:, 0, t, 0:D + LAT], xnT[:, j * HT + t, :], w_in[:, :], start=True, stop=True)
                mm.then_inc(s["proj"], 1)
            turn_vectors(2 * i)
            vectors(2 * i + 1)
            if live(i - Q_TURN):
                j = i - Q_TURN
                pe.wait_ge(s["lat_sb"], j + 1)
                if j:
                    pe.wait_ge(s["latT"], j)
                if live(i - K_TURN - 1):
                    pe.wait_ge(s["k_rest"], i - K_TURN)
                turn(lat, j, 1, s["latT_ps"])
            if live(i - Q_TURN - 1):
                j = i - Q_TURN - 1
                if j == 0:
                    pe.wait_ge(s["w_kv"], 32)
                    pe.wait_ge(s["zeroed"], P // LAT)
                pe.wait_ge(s["latT"], j + 1)
                if j:
                    pe.wait_ge(s["v_sb"], j)
                for t in range(HT):
                    mm = nc.tensor.matmul(ps_p[:, 1, t, :], latT[:, j % 2, t * P:(t + 1) * P], w_kv[:, :], start=True, stop=True)
                mm.then_inc(s["kv"], 1)
            turn_vectors(2 * i + 1)
            if live(i - Q_TURN):
                j = i - Q_TURN
                pe.wait_ge(s["qr"], j + 1)
                pe.wait_ge(s["xnT"], min(i + 1, HALVES))
                if j:
                    pe.wait_ge(s["q_rest"], j)
                turn(qr, j, 0, s["qT"])
            if live(i - K_TURN):
                j = i - K_TURN
                pe.wait_ge(s["kr"], j + 1)
                pe.wait_ge(s["latT"], min(i - Q_TURN + 1, HALVES))
                if j:
                    pe.wait_ge(s["k_rest"], j)
                turn(kr, j, 1, s["kT"])

    @block.scalar
    def _(act):
        def length(n):
            if n >= HALF_STEPS:
                return
            act.wait_ge(s["pw_mv"], n + 1)
            nc.scalar.activation(squares[:, :], ps_w[0:ROWS3, 0:P], ACT.Square, accum_out=sq_sum[:, :]).then_inc(s["pw_ss"], 1)
            act.wait_ge(s["pw_ss"], n + 1)
            nc.scalar.activation(norm[:, :], sq_sum[:, :], ACT.Sqrt).then_inc(s["pw_std"], 1)

        def columns(n):
            if n >= HALF_STEPS:
                return
            act.wait_ge(s["pw_turned"], n + 1)
            nc.scalar.copy(uv[:, :], ps_s[:, 0:ROWS3].rearrange("p (i c) -> p i c", c=LAT)[:, :, 0]).then_inc(s["pw_uv"], 1)

        def first_part(n, j, turned, done):
            act.wait_ge(turned, j + 1)
            if j >= 2:
                act.wait_ge(sent[n][j % 2], 16 * (j // 2))
            nc.scalar.copy(parts[:, n, j % 2, 0, :], ps_t[:, n, :]).then_inc(done, 1)

        def middle_part(n, j, ready, done):
            act.wait_ge(ready, j + 1)
            nc.scalar.copy(parts[:, n, j % 2, 1, :], rest[:, tiles(j), :].rearrange("p t c -> p (t c)")).then_inc(done, 1)

        act.wait_ge(s["eps"], 1)

        def deviation(h):
            act.wait_ge(s["mv"], h + 1)
            nc.scalar.activation(std[:, tiles(h)], mv[:, tiles(h), 1], ACT.Sqrt, bias=keep.eps[:, 0:1]).then_inc(s["std"], 1)

        deviation(0)
        act.wait_ge(s["wT_ps"], 1)
        nc.scalar.copy(w_ssmT[:, :, :], ps_s[:, 0:3 * P].rearrange("p (i o) -> p i o", i=3)).then_inc(s["wT"], 1)
        for i in range(HALVES + K_TURN):
            if live(i + 1):
                deviation(i + 1)
            length(2 * i)
            if live(i):
                act.wait_ge(s["xnT_ps"], i + 1)
                nc.scalar.copy(xnT[:, tiles(i), :], ps_t[:, 0, :].rearrange("p (t c) -> p t c", t=HT)).then_inc(s["xnT"], 1)
            if live(i - 1):
                act.wait_ge(s["proj"], i)
                nc.scalar.copy(q[:, tiles(i - 1), :], ps_p[:, 0, :, 0:D + LAT]).then_inc(s["q_sb"], 1)
            columns(2 * i)
            length(2 * i + 1)
            if live(i - 2):
                act.wait_ge(s["lmv"], i - 1)
                nc.scalar.activation(lstd[:, tiles(i - 2)], lmv[:, tiles(i - 2), 1], ACT.Sqrt, bias=keep.eps[:, 0:1]).then_inc(s["lstd"], 1)
            if live(i - Q_TURN):
                j = i - Q_TURN
                act.wait_ge(s["latT_ps"], j + 1)
                if j >= 2:
                    act.wait_ge(s["kv"], j - 1)
                nc.scalar.copy(latT[:, j % 2, :], ps_t[:, 1, :]).then_inc(s["latT"], 1)
            if live(i - Q_TURN - 1):
                j = i - Q_TURN - 1
                act.wait_ge(s["kv"], j + 1)
                nc.scalar.copy(k[:, tiles(j), :], ps_p[:, 1, :, 0:D]).then_inc(s["k_sb"], 1)
                nc.scalar.copy(keep.v[:, tiles(j), :, 0:HD], ps_p[:, 1, :, D:2 * D].rearrange("p t (h d) -> p t h d", h=H)).then_inc(s["v_sb"], 1)
            columns(2 * i + 1)
            if live(i - Q_TURN):
                first_part(0, i - Q_TURN, s["qT"], s["q_h"])
            if live(i - K_TURN):
                act.wait_ge(s["q_l"], i - K_TURN + 1)
                first_part(1, i - K_TURN, s["kT"], s["k_h"])
            if live(i - Q_TURN):
                middle_part(0, i - Q_TURN, s["q_rest"], s["q_m"])
            if live(i - K_TURN):
                middle_part(1, i - K_TURN, s["k_rest"], s["k_m"])

    @block.vector
    def _(dve):
        link = chained(dve, s["chain_v"])
        v = nc.vector

        def statistics(h):
            dve.wait_ge(x_in[h * HT // NT], 16)
            for t in range(h * HT, (h + 1) * HT):
                last = v.bn_stats(stats[:, t, :], x[:, t, :])
            link(last)
            for t in range(h * HT, (h + 1) * HT):
                last = v.bn_aggr(mv[:, t, :], stats[:, t, :])
            last.then_inc(s["mv"], 1)

        def units(n):
            if n > HALF_STEPS:
                return
            if n < HALF_STEPS:
                dve.wait_ge(s["pw_std"], n + 1)
                link(v.tensor_scalar(inv[:, :], norm[:, :], 1e-12, None, ALU.add))
                link(v.reciprocal(inv[:, :], inv[:, :]))
                if n == HALF_STEPS - 2:
                    v.tensor_scalar(u_last[:, :], ps_w[0:ROWS3, 0:P], inv[:, 0:1], None, ALU.mult)
                v.tensor_scalar(unit[:, :], ps_w[0:ROWS3, 0:P], inv[:, 0:1], None, ALU.mult).then_inc(s["pw_unit"], 1)
                return
            dve.wait_ge(s["pw_mv"], n + 1)
            link(v.tensor_copy(unit[:, :], ps_w[0:ROWS3, 0:P]))
            link(v.tensor_tensor_reduce(squares[:, :], unit[:, :], u_last[:, :], 1.0, 0.0, ALU.mult, ALU.add, sq_sum[:, :]))
            link(v.tensor_scalar(unit[:, :], keep.ones[0:ROWS3, :], sq_sum[:, 0:1], None, ALU.mult))
            v.tensor_copy(pick[:, :], keep.ident[0:ROWS3, 0:ROWS3].rearrange("p (i c) -> p i c", c=LAT)[:, :, 0]).then_inc(s["pw_unit"], 1)
            dve.wait_ge(s["pw_turned"], n + 1)
            link(v.tensor_copy(sigma[:, :], ps_s[:, 0:3]))
            link(v.reciprocal(sigma[:, :], sigma[:, :]))
            v.tensor_scalar(keep.a_nat[:, :], w_ssm[:, 0, :], sigma[:, 0:1], None, ALU.mult)
            v.tensor_scalar(keep.a_T[:, :], w_ssmT[:, 0, :], sigma[:, 0:1], None, ALU.mult)
            v.tensor_scalar(keep.b_T[:, :], w_ssmT[:, 1, :], sigma[:, 1:2], None, ALU.mult)
            v.tensor_scalar(keep.c_T[:, :], w_ssmT[:, 2, :], sigma[:, 2:3], None, ALU.mult).then_inc(s["scaled"], 1)

        def take_rest(n, j, first, done):
            dve.wait_ge(first, j + 1)
            r = rest[:, tiles(j), :].rearrange("p t c -> p (t c)")
            v.tensor_tensor(r, ps_t[:, n, :], parts[:, n, j % 2, 0, :], ALU.subtract).then_inc(done, 1)

        v.memset(keep.ones[:, :], 1.0)
        v.memset(keep.v[:, :, :, HD:HD + 1], 1.0)
        v.memset(uv[:, :], float(1.0 / np.sqrt(np.float32(P))))
        link(v.memset(ps_w[:, 0:P], 0.0))
        statistics(0)
        dve.wait_ge(s["wT"], 1)
        v.memset(squares[:, :], 0.0).then_inc(s["pw_uv"], 1)
        for i in range(HALVES + K_TURN):
            if live(i + 1):
                statistics(i + 1)
            if live(i):
                dve.wait_ge(s["std"], i + 1)
                link(v.reciprocal(rstd[:, tiles(i)], std[:, tiles(i)]))
                for t in range(i * HT, (i + 1) * HT):
                    last = v.tensor_scalar(xn[:, t, :], x[:, t, :], mv[:, t, 0:1], rstd[:, t:t + 1], ALU.subtract, ALU.mult)
                last.then_inc(s["xn"], 1)
            units(2 * i)
            if live(i - 2):
                j = i - 2
                dve.wait_ge(s["q_sb"], j + 1)
                for t in range(j * HT, (j + 1) * HT):
                    last = v.bn_stats(lstats[:, t, :], q[:, t, D:D + LAT])
                link(last)
                for t in range(j * HT, (j + 1) * HT):
                    last = v.bn_aggr(lmv[:, t, :], lstats[:, t, :])
                last.then_inc(s["lmv"], 1)
            if live(i - 3):
                j = i - 3
                if j == 0:
                    dve.wait_ge(s["tables"], 64)
                    dve.wait_ge(s["zeroed"], P // LAT)
                dve.wait_ge(s["lstd"], j + 1)
                link(v.reciprocal(lrstd[:, tiles(j)], lstd[:, tiles(j)]))
                wide = [P, HT, LAT]
                link(v.tensor_tensor(latn[:, :, :], q[:, tiles(j), D:D + LAT], lmv[:, tiles(j), 0].unsqueeze(2).to_broadcast(wide), ALU.subtract))
                link(v.tensor_tensor(latn[:, :, :], latn[:, :, :], lrstd[:, tiles(j)].unsqueeze(2).to_broadcast(wide), ALU.mult))
                link(v.tensor_tensor(latn[:, :, :], latn[:, :, :], gamma[:, :].unsqueeze(1).to_broadcast(wide), ALU.mult))
                v.tensor_tensor(lat[:, tiles(j), 0:LAT], latn[:, :, :], beta[:, :].unsqueeze(1).to_broadcast(wide),
                                ALU.add).then_inc(s["lat_sb"], 1)
            units(2 * i + 1)
            if live(i - 3):
                rope(v, link, q, qr, tmp_q, i - 3, s["qr"])
            if live(i - Q_TURN):
                take_rest(0, i - Q_TURN, s["q_h"], s["q_rest"])
            if live(i - K_TURN):
                take_rest(1, i - K_TURN, s["k_h"], s["k_rest"])
        dve.wait_ge(s["scaled"], 1)


def place_weights(nc, ctx, keep):
    def sb(name, shape, dt=F32):
        return ctx.enter_context(nc.sbuf_tensor(name, shape, dt))

    keep.w13 = sb("w13", [P, E, 2, F])
    keep.b13 = sb("b13", [P, E, 2, F])
    keep.w2 = sb("w2", [P, E, 2, D])
    keep.sw1, keep.sw3 = sb("sw1", [P, SF]), sb("sw3", [P, SF])
    keep.sbias = sb("sbias", [P, 2, 3])
    keep.sw2 = sb("sw2", [P, 3, D])
    keep.gate_w = sb("gate_w", [P, E])
    keep.gate_b = sb("gate_b", [P, E])
    keep.before = sb("before", [P, P])
    keep.expert_no = sb("expert_no", [P, E])
    keep.tile_no = sb("tile_no", [P, SLOT_TILES])
    keep.token_id = sb("token_id", [P, TOPK, TILES])


def background_loads(dram, keep, slots):
    rows = [(c, min(P, SF - c * P)) for c in range(3)]
    half = E // 2
    out = [(keep.gate_w[:, :], dram["gate_w"]),
           (keep.gate_b[:, :], dram["gate_b"].partition_broadcast(P)),
           (keep.before[:, :], dram["before"]),
           (keep.expert_no[:, :], dram["expert_no"].partition_broadcast(P)),
           (keep.tile_no[:, :], dram["tile_no"].partition_broadcast(P)),
           (keep.token_id[:, :, :], dram["token_id"]),
           (keep.sw1[:, :], dram["sw1"]),
           (keep.sw3[:, :], dram["sw3"])]
    out += [(keep.sbias[0:n, i, c:c + 1], v[c * P:c * P + n].unsqueeze(1))
            for i, v in enumerate((dram["sb1"], dram["sb3"])) for c, n in rows]
    out += [(keep.sw2[0:n, c, :], dram["sw2"][c * P:c * P + n, :]) for c, n in rows]
    out += [(keep.sw2[SF - 2 * P:SF - 2 * P + 1, 2, :], dram["sb2"].unsqueeze(0))]
    for e in (slice(0, half), slice(half, E)):
        out += [(keep.w13[:, e, 0, :], dram["w1"][e].rearrange("e d f -> d e f")),
                (keep.w13[:, e, 1, :], dram["w3"][e].rearrange("e d f -> d e f")),
                (keep.b13[:, e, 0, :], dram["b1"][e].partition_broadcast(P)),
                (keep.b13[:, e, 1, :], dram["b3"][e].partition_broadcast(P)),
                (keep.w2[:, e, 0, :], dram["w2"][e, 0:P, :].rearrange("e f d -> f e d")),
                (keep.w2[0:FH, e, 1, :], dram["w2"][e, P:F, :].rearrange("e f d -> f e d")),
                (keep.w2[FH:FH + 1, e, 1, :], dram["b2"][e].unsqueeze(0))]
    piece = SLOTS // 4
    for d in slots:
        out += [(d[n:n + piece].rearrange("(a b) c -> a (b c)", a=P),
                 dram["slot_rows"][n:n + piece].rearrange("(a b) c -> a (b c)", a=P)) for n in range(0, SLOTS, piece)]
    return out


G = 4
UNITS = B * H // G
RING = 3
PAIRS = PARTS * PARTS
KROWS = PAIRS * HD
SROWS = KROWS + PARTS
HALFQ = 512
LEAD = 1.25
ROWS_LATER = 5
LAG = 2


def unit_steps():
    return [(hf, kb, max(kb * P, hf * HALFQ), (hf + 1) * HALFQ - max(kb * P, hf * HALFQ))
            for hf in range(T // HALFQ) for kb in range((hf + 1) * HALFQ // P)]


def max_tasks():
    return [(j, qt, c, min(HALFQ, (qt + 1) * P - c)) for j in range(G) for qt in range(NT)
            for c in range(0, (qt + 1) * P, HALFQ)]


def maxima_stream():
    tasks = len(max_tasks())
    out = []
    for u in range(UNITS):
        for n in range(tasks):
            out.append((u, n))
            if u and n == ROWS_LATER:
                out.append((u - 1, None))
    return out + [(UNITS - 1, None)]


def spread_stream():
    stream, steps = maxima_stream(), unit_steps()
    width, per_unit = sum(w for *_, w in steps), len(stream) / UNITS
    out, at = [], 0
    for i in range(-1, UNITS * len(steps)):
        u, k = divmod(i + 1, len(steps))
        goal = min(len(stream), int(per_unit * (LEAD + u + sum(w for *_, w in steps[:k]) / width)))
        out.append(range(at, goal))
        at = goal
    return out


def attention(nc, ctx, dram, keep, slots):
    def sb(name, shape, dt=F32):
        return ctx.enter_context(nc.sbuf_tensor(name, shape, dt))

    q_stack = [sb(f"b_q_stack{r}", [SROWS, G, T], BF16) for r in range(RING)]
    k_stack = [sb(f"b_k_stack{r}", [SROWS, G, T], BF16) for r in range(RING)]
    ones_row = sb("b_ones_row", [PARTS, T], BF16)
    ident_b = sb("b_ident_b", [P, P], BF16)
    maskneg = sb("b_maskneg", [P, P], BF16)
    probs = sb("b_probs", [P, 3, G, HALFQ])
    mx = sb("b_mx", [P, 2, 2, G * NT])
    top = sb("b_top", [P, 2, G * NT])
    max_parts = sb("b_max_parts", [P, PARTS, G * NT], BF16)
    max_rows = sb("b_max_rows", [PARTS * G * NT, P], BF16)
    o_sb = sb("b_o_sb", [P, 2, HALFQ])
    rz = sb("b_rz", [P, HALFQ // P, G])
    ps_s = ctx.enter_context(nc.psum_tensor("b_ps_s", [P, 2, 2, HALFQ], F32))
    ps_m = ctx.enter_context(nc.psum_tensor("b_ps_m", [P, 2, HALFQ], F32))
    ps_o = ctx.enter_context(nc.psum_tensor("b_ps_o", [P, 2, HALFQ], F32))
    s = semaphores(nc, ctx, "attend", "ones masks ones0 ones1 ones2 stack0 stack1 stack2 max_in0 max_in1 max_in2 ps_zero scores exp mask pv "
             "cand reduced mx_chain top max_ready w2_zero loaded o_sb oT attn chain_v")
    stacked = [s["stack0"], s["stack1"], s["stack2"]]
    ones_in = [s["ones0"], s["ones1"], s["ones2"]]
    max_in = [s["max_in0"], s["max_in1"], s["max_in2"]]
    steps, tasks, stream, spread = unit_steps(), max_tasks(), maxima_stream(), spread_stream()
    NS = len(steps)
    NTASK = len(tasks)
    diag = [kb * P >= hf * HALFQ for hf, kb, _, _ in steps]
    loads = background_loads(dram, keep, slots)
    half_end = [NS // 3 - 1, NS - 1]
    turn_of_rows = {u: at for at, (u, n) in enumerate(stream) if n is None}
    last_turn = {u: at for at, (u, n) in enumerate(stream) if n == NTASK - 1}

    def taken_from(i):
        u, k = divmod(i, NS)
        if k == half_end[0] + LAG:
            return 2 * u
        if k == LAG - 1 and u:
            return 2 * u - 1
        return None
    block = ctx.enter_context(nc.Block())

    def masks_until(i):
        return i // NS * sum(diag) + sum(diag[:i % NS + 1])

    @block.sync
    def _(sp):
        sp.wait_ge(s["ones"], 1)
        for r in range(RING):
            for h in range(G):
                sp.dma_start(k_stack[r][KROWS:SROWS, h, :], ones_row[:, :]).then_inc(ones_in[r], 16)

        def stacks(u):
            b, g, r = u // G, u % G, u % RING
            if u >= RING:
                sp.wait_ge(s["scores"], 2 * NS * (u - RING + 1))
            q_src, k_src = (x.rearrange("i (d h) t -> (i d) h t", h=H)[:, g * G:(g + 1) * G, b * T:(b + 1) * T]
                            for x in (keep.q_parts, keep.k_parts))
            for i in range(PARTS):
                at = i * PARTS * HD
                sp.dma_start(k_stack[r][at:at + PARTS * HD, :, :], k_src).then_inc(stacked[r], 16)
                for j in range(PARTS):
                    sp.dma_start(q_stack[r][at + j * HD:at + (j + 1) * HD, :, :], q_src[i * HD:(i + 1) * HD]).then_inc(stacked[r], 16)

        def maxima(u):
            sp.wait_ge(s["reduced"], turn_of_rows[u] + 1)
            for i in range(PARTS):
                n = G * NT
                sp.dma_start(q_stack[u % RING][KROWS + i:KROWS + i + 1, :, :].rearrange("r h (t c) -> r (h t) c", c=P),
                             max_rows[i * n:(i + 1) * n, :]).then_inc(max_in[u % RING], 16)

        stacks(0)
        for u in range(UNITS):
            if u + 1 < UNITS:
                stacks(u + 1)
            maxima(u)
            for to, src in loads[u::UNITS]:
                if u == 0:
                    sp.wait_ge(s["w2_zero"], 1)
                sp.dma_start(to, src).then_inc(s["loaded"], 16)
        sp.wait_ge(s["loaded"], 16 * len(loads))

    STACK_DMAS = PARTS + PAIRS

    @block.gpsimd
    def _(pool):
        nc.gpsimd.memset(keep.w2[:, :, 1, :], 0.0).then_inc(s["w2_zero"], 1)
        pool.wait_ge(s["w2_zero"], 1)
        nc.gpsimd.memset(maskneg[:, :], 0.0).then_inc(s["mx_chain"], 1)
        pool.wait_ge(s["mx_chain"], 1)
        nc.gpsimd.affine_select(out=maskneg[:, :], in_=maskneg[:, :], compare_op=ALU.is_ge, fill=-1e30, base=0,
                                pattern=[[-1, P]], channel_multiplier=1).then_inc(s["masks"], 1)

        def split_maxima(u):
            pool.wait_ge(s["top"], u + 1)
            if u:
                pool.wait_ge(s["reduced"], turn_of_rows[u - 1] + 1)
            steps_before = 1 + 2 * (PARTS - 1) * u
            left = top[:, u % 2, :]
            for part in range(PARTS - 1):
                nc.gpsimd.tensor_copy(max_parts[:, part, :], left).then_inc(s["mx_chain"], 1)
                pool.wait_ge(s["mx_chain"], steps_before + 2 * part + 1)
                nc.gpsimd.tensor_tensor(left, left, max_parts[:, part, :], ALU.subtract).then_inc(s["mx_chain"], 1)
                pool.wait_ge(s["mx_chain"], steps_before + 2 * part + 2)
            nc.gpsimd.tensor_copy(max_parts[:, PARTS - 1, :], left).then_inc(s["max_ready"], 1)
            pool.wait_ge(s["max_ready"], u + 1)

        for i in range(-1, UNITS * NS):
            for at in spread[i + 1]:
                if stream[at][1] == NTASK - 1:
                    split_maxima(stream[at][0])
            if i < 0 or not diag[i % NS]:
                continue
            pool.wait_ge(s["exp"], 2 * i + 2)
            blk = probs[:, i % 3, :, 0:P]
            nc.gpsimd.affine_select(out=blk, in_=blk, compare_op=ALU.is_ge, fill=0.0, base=0,
                                    pattern=[[0, G], [1, P]], channel_multiplier=-1).then_inc(s["mask"], 1)

    @block.scalar
    def _(act):
        def take_outputs(n):
            act.wait_ge(s["pv"], n // 2 * NS + half_end[n % 2] + 1)
            if n >= 2:
                act.wait_ge(s["oT"], n - 1)
            nc.scalar.copy(o_sb[:, n % 2, :], ps_o[:, n % 2, :]).then_inc(s["o_sb"], 1)

        for i in range(UNITS * NS):
            u, k = divmod(i, NS)
            w = steps[k][3]
            if i >= 3:
                act.wait_ge(s["pv"], i - 2)
            for hp in range(2):
                act.wait_ge(s["scores"], 2 * i + hp + 1)
                nc.scalar.activation(probs[:, i % 3, 2 * hp:2 * hp + 2, 0:w], ps_s[:, hp, :, 0:w], ACT.Exp,
                                     scale=SCALE).then_inc(s["exp"], 1)
            if taken_from(i) is not None:
                take_outputs(taken_from(i))
        take_outputs(2 * UNITS - 1)

    @block.tensor
    def _(pe):
        def maximum_scores(turns):
            for at in turns:
                u, n = stream[at]
                r = u % RING
                if at >= 2:
                    pe.wait_ge(s["reduced"], at - 1)
                if n is None:
                    pe.wait_ge(s["max_ready"], u + 1)
                    nc.tensor.transpose(ps_m[0:PARTS * G * NT, at % 2, 0:P // 2].bitcast(BF16),
                                        max_parts[:, :, :].rearrange("p i n -> p (i n)"), ident_b[:, :]).then_inc(s["cand"], 1)
                    continue
                if n == 0:
                    pe.wait_ge(stacked[r], 16 * STACK_DMAS * (u // RING + 1))
                j, qt, c, keys = tasks[n]
                out = ps_m[:, at % 2, 0:keys]
                on_diagonal = c + keys == (qt + 1) * P
                mm = nc.tensor.matmul(out, q_stack[r][0:KROWS, j, qt * P:(qt + 1) * P],
                                      k_stack[r][0:KROWS, j, c:c + keys], start=True, stop=not on_diagonal,
                                      skip_group_check=True)
                if on_diagonal:
                    mm = nc.tensor.matmul(out[:, keys - P:keys], ident_b[:, :], maskneg[:, :], start=False, stop=True,
                                          skip_group_check=True)
                mm.then_inc(s["cand"], 1)

        def weighted_values(i):
            u, k = divmod(i, NS)
            hf, kb, lo, w = steps[k]
            b, g = u // G, u % G
            pe.wait_ge(s["exp"], 2 * i + 2)
            if diag[k]:
                pe.wait_ge(s["mask"], masks_until(i))
            if kb == 0:
                if u:
                    pe.wait_ge(s["attn"], 2 * u - 1 + hf)
                else:
                    pe.wait_ge(s["ps_zero"], 1)
            for j in range(G):
                mm = nc.tensor.matmul(ps_o[32 * j:32 * j + HD + 1, hf, lo - hf * HALFQ:HALFQ],
                                      keep.v[:, b * NT + kb, g * G + j, :], probs[:, i % 3, j, 0:w],
                                      start=(kb == 0), stop=(k in half_end), skip_group_check=True)
            mm.then_inc(s["pv"], 1)

        def turn_outputs(n):
            pe.wait_ge(s["o_sb"], n + 1)
            for t in range(HALFQ // P):
                mm = nc.tensor.transpose(ps_o[:, n % 2, t * P:(t + 1) * P], o_sb[:, n % 2, t * P:(t + 1) * P], keep.ident[:, :])
            mm.then_inc(s["oT"], 1)

        pe.wait_ge(s["masks"], 2)
        for r in range(RING):
            pe.wait_ge(ones_in[r], 16 * G)
        maximum_scores(spread[0])
        for i in range(UNITS * NS):
            u, k = divmod(i, NS)
            hf, kb, lo, w = steps[k]
            r = u % RING
            if k == 0:
                pe.wait_ge(max_in[r], 16 * PARTS * (u // RING + 1))
            ahead = spread[i + 1]
            cut = [ahead[n * len(ahead) // 4:(n + 1) * len(ahead) // 4] for n in range(4)]
            for hp in range(2):
                if i:
                    pe.wait_ge(s["exp"], 2 * i + hp - 1)
                for jj in range(2):
                    j = 2 * hp + jj
                    mm = nc.tensor.matmul(ps_s[:, hp, jj, 0:w], k_stack[r][0:SROWS, j, kb * P:(kb + 1) * P],
                                          q_stack[r][0:SROWS, j, lo:lo + w], start=True, stop=True)
                mm.then_inc(s["scores"], 1)
                maximum_scores(cut[hp])
            if i >= LAG:
                weighted_values(i - LAG)
            maximum_scores(cut[2])
            if i and taken_from(i - 1) is not None:
                turn_outputs(taken_from(i - 1))
            maximum_scores(cut[3])
        for i in range(UNITS * NS - LAG, UNITS * NS):
            weighted_values(i)
        turn_outputs(2 * UNITS - 1)

    @block.vector
    def _(dve):
        link = chained(dve, s["chain_v"])
        nc.vector.memset(ones_row[:, :], -1.0).then_inc(s["ones"], 1)
        nc.vector.memset(mx[:, :, :, :], -1e30)
        nc.vector.memset(ps_o[:, :, :], 0.0).then_inc(s["ps_zero"], 1)
        nc.vector.tensor_copy(ident_b[:, :], keep.ident[:, :]).then_inc(s["masks"], 1)

        def reduce(turns):
            for at in turns:
                u, n = stream[at]
                dve.wait_ge(s["cand"], at + 1)
                if n is None:
                    if u:
                        before = u - 1
                        dve.wait_ge(max_in[before % RING], 16 * PARTS * (before // RING + 1))
                    nc.vector.tensor_copy(max_rows[:, :], ps_m[0:PARTS * G * NT, at % 2, 0:P // 2].bitcast(BF16)).then_inc(s["reduced"], 1)
                    continue
                j, qt, c, keys = tasks[n]
                nc.vector.tensor_reduce(mx[:, u % 2, c // HALFQ, j * NT + qt:j * NT + qt + 1], ps_m[:, at % 2, 0:keys],
                                        AX_X, ALU.max).then_inc(s["reduced"], 1)
                if n == NTASK - 1:
                    dve.wait_ge(s["reduced"], at + 1)
                    if u >= 2:
                        dve.wait_ge(s["max_ready"], u - 1)
                    nc.vector.tensor_tensor(top[:, u % 2, :], mx[:, u % 2, 0, :], mx[:, u % 2, 1, :], ALU.max).then_inc(s["top"], 1)

        def normalize(n):
            u, hf = divmod(n, 2)
            b, g = divmod(u, G)
            dve.wait_ge(s["oT"], n + 1)
            if n:
                dve.wait_ge(s["attn"], n)
            o = ps_o[:, hf, :].rearrange("p (t j c) -> p t j c", t=HALFQ // P, j=G)
            link(nc.vector.reciprocal(rz[:, :, :], o[:, :, :, HD]))
            first = b * NT + hf * HALFQ // P
            out = keep.attn[:, first:first + HALFQ // P, g * G * HD:(g + 1) * G * HD]
            nc.vector.tensor_tensor(out.rearrange("p t (j d) -> p t j d", j=G), o[:, :, :, 0:HD],
                                    rz[:, :, :].unsqueeze(3).to_broadcast([P, HALFQ // P, G, HD]), ALU.mult).then_inc(s["attn"], 1)

        reduce(spread[0])
        for i in range(UNITS * NS):
            reduce(spread[i + 1])
            if i and taken_from(i - 1) is not None:
                normalize(taken_from(i - 1))
        normalize(2 * UNITS - 1)


LEVELS = T.bit_length() - 1
GROUP = 4


def project_out(nc, ctx, dram, keep):
    def sb(name, shape, dt=F32):
        return ctx.enter_context(nc.sbuf_tensor(name, shape, dt))

    w_o = sb("c_w_o", [P, D])
    attnT = sb("c_attnT", [P, 2, GROUP * P])
    a_pow = sb("c_a_pow", [P, 2, P])
    ps_t = ctx.enter_context(nc.psum_tensor("c_ps_t", [P, 2, GROUP * P], F32))
    ps_y = ctx.enter_context(nc.psum_tensor("c_ps_y", [P, 2, GROUP * P], F32))
    ps_a = ctx.enter_context(nc.psum_tensor("c_ps_a", [P, 512], F32))
    s = semaphores(nc, ctx, "out", "w_o turned copied projected added squared power")
    groups = TILES // GROUP
    block = ctx.enter_context(nc.Block())

    @block.sync
    def _(sp):
        sp.dma_start(w_o[:, :], dram["w_o"]).then_inc(s["w_o"], 16)

    @block.tensor
    def _(pe):
        def square(level):
            pe.wait_ge(s["power"], level)
            natural = a_pow[:, level % 2, :]
            nc.tensor.matmul(ps_a[:, 0:P], natural, keep.a_powT[:, level - 1, :], start=True, stop=True)
            nc.tensor.matmul(ps_a[:, P:2 * P], keep.a_powT[:, level - 1, :], natural, start=True, stop=True).then_inc(s["squared"], 1)

        pe.wait_ge(s["w_o"], 16)
        level = 1
        for g in range(groups + 1):
            if g < groups:
                if g >= 2:
                    pe.wait_ge(s["copied"], g - 1)
                for t in range(GROUP):
                    mm = nc.tensor.transpose(ps_t[:, g % 2, t * P:(t + 1) * P], keep.attn[:, g * GROUP + t, :], keep.ident[:, :])
                mm.then_inc(s["turned"], 1)
            if g:
                pe.wait_ge(s["copied"], g)
                if g >= 3:
                    pe.wait_ge(s["added"], g - 2)
                for t in range(GROUP):
                    mm = nc.tensor.matmul(ps_y[:, (g - 1) % 2, t * P:(t + 1) * P],
                                          attnT[:, (g - 1) % 2, t * P:(t + 1) * P], w_o[:, :], start=True, stop=True)
                mm.then_inc(s["projected"], 1)
            square(level)
            level += 1
        while level < LEVELS:
            square(level)
            level += 1

    @block.scalar
    def _(act):
        for g in range(groups):
            act.wait_ge(s["turned"], g + 1)
            if g >= 2:
                act.wait_ge(s["projected"], g - 1)
            nc.scalar.copy(attnT[:, g % 2, :], ps_t[:, g % 2, :]).then_inc(s["copied"], 1)

    @block.vector
    def _(dve):
        nc.vector.tensor_copy(a_pow[:, 1, :], keep.a_nat[:, :])
        nc.vector.tensor_copy(keep.a_powT[:, 0, :], keep.a_T[:, :]).then_inc(s["power"], 1)
        level = 1

        def take_power(level):
            dve.wait_ge(s["squared"], level)
            nc.vector.tensor_copy(keep.a_powT[:, level, :], ps_a[:, 0:P])
            nc.vector.tensor_copy(a_pow[:, (level + 1) % 2, :], ps_a[:, P:2 * P]).then_inc(s["power"], 1)

        for g in range(groups + 1):
            if g:
                dve.wait_ge(s["projected"], g)
                xs = keep.x[:, (g - 1) * GROUP:g * GROUP, :]
                nc.vector.tensor_tensor(xs, ps_y[:, (g - 1) % 2, :].rearrange("p (t d) -> p t d", t=GROUP), xs,
                                        ALU.add).then_inc(s["added"], 1)
            take_power(level)
            level += 1
        while level < LEVELS:
            take_power(level)
            level += 1


class Norm:

    def __init__(self, nc, ctx, keep, tag, out, outT):
        def sb(name, shape, dt=F32):
            return ctx.enter_context(nc.sbuf_tensor(tag + name, shape, dt))
        self.nc, self.keep, self.out, self.outT = nc, keep, out, outT
        self.stats, self.mv = sb("stats", [P, TILES, 6]), sb("mv", [P, TILES, 2])
        self.std, self.rstd = sb("std", [P, TILES]), sb("rstd", [P, TILES])
        self.s = semaphores(nc, ctx, tag + "norm", "mv std rstd xn turned xnT")

    def vector_stats(self, dve, link, b):
        for t in range(b * NT, (b + 1) * NT):
            last = dve.bn_stats(self.stats[:, t, :], self.keep.x[:, t, :])
        link(last)
        for t in range(b * NT, (b + 1) * NT):
            last = dve.bn_aggr(self.mv[:, t, :], self.stats[:, t, :])
        last.then_inc(self.s["mv"], 1)

    def scalar_std(self, act, b):
        at = slice(b * NT, (b + 1) * NT)
        act.wait_ge(self.s["mv"], b + 1)
        act.activation(self.std[:, at], self.mv[:, at, 1], ACT.Sqrt, bias=self.keep.eps[:, 0:1]).then_inc(self.s["std"], 1)

    def vector_scale(self, dve, link, b):
        dve.wait_ge(self.s["std"], b + 1)
        link(dve.reciprocal(self.rstd[:, b * NT:(b + 1) * NT], self.std[:, b * NT:(b + 1) * NT]))
        for t in range(b * NT, (b + 1) * NT):
            last = dve.tensor_scalar(self.out[:, t, 0:D], self.keep.x[:, t, :], self.mv[:, t, 0:1],
                                     self.rstd[:, t:t + 1], ALU.subtract, ALU.mult)
        last.then_inc(self.s["xn"], 1)

    def tensor_turn(self, pe, bank, b):
        pe.wait_ge(self.s["xn"], b + 1)
        if b >= 2:
            pe.wait_ge(self.s["xnT"], b - 1)
        for t in range(NT):
            mm = pe.transpose(bank[:, t * P:(t + 1) * P], self.out[:, b * NT + t, 0:D], self.keep.ident[:, :])
        mm.then_inc(self.s["turned"], 1)

    def scalar_copy(self, act, bank, b):
        act.wait_ge(self.s["turned"], b + 1)
        act.copy(self.outT[:, b * T:(b + 1) * T], bank[:, :]).then_inc(self.s["xnT"], 1)


def route(nc, ctx, dram, keep, tag):
    def sb(name, shape, dt=F32):
        return ctx.enter_context(nc.sbuf_tensor(tag + name, shape, dt))

    logits = sb("logits", [P, TILES, E])
    scores = sb("scores", [P, TILES, E])
    top = sb("top", [P, TILES])
    total = sb("total", [P, TILES])
    best = sb("best", [P, TILES, 8])
    where = sb("where", [P, TILES, 8], U32)
    where_f = sb("where_f", [P, TOPK, TILES])
    chosen = sb("chosen", [P, TOPK, TILES, E])
    either = sb("either", [P, TILES, E])
    tile_sum = sb("tile_sum", [P, TILES, E])
    run = [sb(f"run{i}", [P, TILES, E]) for i in range(2)]
    place = sb("place", [P, TILES, E])
    slot_f = sb("slot_f", [P, TOPK, TILES])
    whole = sb("whole", [P, E])
    whole_i = sb("whole_i", [P, E], I32)
    end = [sb(f"end{i}", [P, E]) for i in range(2)]
    passed = sb("passed", [P, SLOT_TILES, E])
    expert_f = sb("expert_f", [P, SLOT_TILES])
    ps_t = ctx.enter_context(nc.psum_tensor(tag + "ps_t", [P, 2, T], F32))
    ps_g = ctx.enter_context(nc.psum_tensor(tag + "ps_g", [P, TILES, E], F32))
    ps_c = ctx.enter_context(nc.psum_tensor(tag + "ps_c", [P, TILES, E], F32))
    ps_n = ctx.enter_context(nc.psum_tensor(tag + "ps_n", [P, TILES, E], F32))
    norm = Norm(nc, ctx, keep, tag, keep.rows[:, 0], keep.xnT)
    s = semaphores(nc, ctx, tag + "route", "gate less exp either counts chain")
    block = ctx.enter_context(nc.Block())

    @block.tensor
    def _(pe):
        for b in range(B):
            norm.tensor_turn(nc.tensor, ps_t[:, b % 2, :], b)
        pe.wait_ge(norm.s["xnT"], B)
        for t in range(TILES):
            mm = nc.tensor.matmul(ps_g[:, t, :], keep.xnT[:, t * P:(t + 1) * P], keep.gate_w[:, :], start=True, stop=True)
        mm.then_inc(s["gate"], 1)
        pe.wait_ge(s["either"], 1)
        flat = either[:, :, :].rearrange("p t e -> p (t e)")
        nc.tensor.matmul(ps_c[:, :, :].rearrange("p t e -> p (t e)"), keep.before[:, :], flat, start=True, stop=True)
        nc.tensor.matmul(ps_n[:, :, :].rearrange("p t e -> p (t e)"), keep.ones[:, :], flat, start=True, stop=True).then_inc(s["counts"], 1)

    @block.scalar
    def _(act):
        for b in range(B):
            norm.scalar_std(nc.scalar, b)
        for b in range(B):
            norm.scalar_copy(nc.scalar, ps_t[:, b % 2, :], b)
            at = slice(b * NT, (b + 1) * NT)
            nc.scalar.copy(keep.rows[:, 1, at, 0:D], keep.rows[:, 0, at, 0:D])
        act.wait_ge(s["less"], 1)
        nc.scalar.activation(scores[:, :, :], logits[:, :, :], ACT.Exp).then_inc(s["exp"], 1)

    @block.vector
    def _(dve):
        link = chained(dve, s["chain"])
        v = nc.vector
        for b in range(B):
            norm.vector_stats(v, link, b)
            if b:
                norm.vector_scale(v, link, b - 1)
        norm.vector_scale(v, link, B - 1)
        for k in range(TOPK):
            v.tensor_copy(keep.rows[:, k, :, D].bitcast(I32), keep.token_id[:, k, :].bitcast(I32))
        dve.wait_ge(s["gate"], 1)
        link(v.tensor_tensor(logits[:, :, :], ps_g[:, :, :], keep.gate_b[:, :].unsqueeze(1).to_broadcast([P, TILES, E]), ALU.add))
        link(v.tensor_reduce(top[:, :], logits[:, :, :], AX_X, ALU.max))
        v.tensor_tensor(logits[:, :, :], logits[:, :, :], top[:, :].unsqueeze(2).to_broadcast([P, TILES, E]),
                        ALU.subtract).then_inc(s["less"], 1)
        dve.wait_ge(s["exp"], 1)
        link(v.tensor_reduce(total[:, :], scores[:, :, :], AX_X, ALU.add))
        link(v.reciprocal(total[:, :], total[:, :]))
        link(v.tensor_tensor(scores[:, :, :], scores[:, :, :], total[:, :].unsqueeze(2).to_broadcast([P, TILES, E]), ALU.mult))
        for t in range(TILES):
            last = v.max(best[:, t, :], scores[:, t, :])
        link(last)
        for t in range(TILES):
            last = v.max_index(where[:, t, :], best[:, t, :], scores[:, t, :])
        link(last)
        for k in range(TOPK):
            v.tensor_copy(keep.weight[:, k, :], best[:, :, k])
            last = v.tensor_copy(where_f[:, k, :], where[:, :, k])
        link(last)
        numbers = keep.expert_no[:, :].unsqueeze(1).to_broadcast([P, TILES, E])
        for k in range(TOPK):
            last = v.tensor_tensor(chosen[:, k], where_f[:, k, :].unsqueeze(2).to_broadcast([P, TILES, E]), numbers, ALU.is_equal)
        link(last)
        v.tensor_tensor(either[:, :, :], chosen[:, 0], chosen[:, 1], ALU.add).then_inc(s["either"], 1)
        dve.wait_ge(s["counts"], 1)
        link(v.tensor_copy(tile_sum[:, :, :], ps_n[:, :, :]))
        src, step, i = tile_sum, 1, 0
        while step < TILES:
            v.tensor_copy(run[i][:, 0:step, :], src[:, 0:step, :])
            link(v.tensor_tensor(run[i][:, step:, :], src[:, step:, :], src[:, 0:TILES - step, :], ALU.add))
            src, step, i = run[i], 2 * step, 1 - i
        incl = src
        link(v.tensor_scalar(whole[:, :], incl[:, TILES - 1, :], float(P - 1), None, ALU.add))
        link(v.tensor_copy(whole_i[:, :], whole[:, :]))
        link(v.tensor_scalar(whole_i[:, :], whole_i[:, :], P.bit_length() - 1, None, ALU.arith_shift_right))
        link(v.tensor_copy(whole[:, :], whole_i[:, :]))
        src2, step, j = whole, 1, 0
        while step < E:
            v.tensor_copy(end[j][:, 0:step], src2[:, 0:step])
            link(v.tensor_tensor(end[j][:, step:], src2[:, step:], src2[:, 0:E - step], ALU.add))
            src2, step, j = end[j], 2 * step, 1 - j
        ends = src2
        v.tensor_tensor(passed[:, :, :], keep.tile_no[:, :].unsqueeze(2).to_broadcast([P, SLOT_TILES, E]),
                        ends[:, :].unsqueeze(1).to_broadcast([P, SLOT_TILES, E]), ALU.is_ge)
        link(v.tensor_tensor(whole[:, :], ends[:, :], whole[:, :], ALU.subtract))
        link(v.tensor_scalar(whole[:, :], whole[:, :], float(P), None, ALU.mult))
        link(v.tensor_reduce(expert_f[:, :], passed[:, :, :], AX_X, ALU.add))
        link(v.tensor_scalar(expert_f[:, :], expert_f[:, :], float(E - 1), None, ALU.min))
        v.tensor_copy(keep.expert[:, :], expert_f[:, :])
        link(v.tensor_tensor(place[:, :, :], incl[:, :, :], tile_sum[:, :, :], ALU.subtract))
        link(v.tensor_tensor(place[:, :, :], ps_c[:, :, :], place[:, :, :], ALU.add))
        link(v.tensor_tensor(place[:, :, :], place[:, :, :], whole[:, :].unsqueeze(1).to_broadcast([P, TILES, E]), ALU.add))
        for k in range(TOPK):
            last = v.tensor_tensor(chosen[:, k], chosen[:, k], place[:, :, :], ALU.mult)
        link(last)
        for k in range(TOPK):
            last = v.tensor_reduce(slot_f[:, k, :], chosen[:, k], AX_X, ALU.add)
        link(last)
        link(v.tensor_copy(keep.slot[:, :, :], slot_f[:, :, :]))


XS_RING = 8
Y_RING = 4


def experts(nc, ctx, dram, keep, tag, slots_dram, parted_dram, out):
    def sb(name, shape, dt=F32):
        return ctx.enter_context(nc.sbuf_tensor(tag + name, shape, dt))

    sil = sb("sil", [P, 2, 3, HALFQ])
    up = sb("up", [P, 2, 3, HALFQ])
    xs = sb("xs", [P, XS_RING, ROW])
    xsT = sb("xsT", [P, 2, P])
    hg = sb("hg", [P, 2, 2 * F])
    act_h = sb("act_h", [P, 2, F])
    a = sb("a", [P, 2, 2 * P])
    aT = sb("aT", [P, 2, 2 * P])
    y = sb("y", [P, Y_RING, D])
    back = sb("back", [P, 2, NT, TOPK * D])
    ps = ctx.enter_context(nc.psum_tensor(tag + "ps", [P, 8, 512], F32))
    s = semaphores(nc, ctx, tag + "expert", "scattered hidden sil up out added chain xs0 xs1 xs2 xs3 xs4 xs5 xs6 xs7 xT_ps xT h hg act_h a a_ready aT_ps aT "
             "y_ps y sent0 sent1 sent2 sent3 back0 back1 combined")
    xs_in = [s["xs0"], s["xs1"], s["xs2"], s["xs3"], s["xs4"], s["xs5"], s["xs6"], s["xs7"]]
    sent = [s["sent0"], s["sent1"], s["sent2"], s["sent3"]]
    back_in = [s["back0"], s["back1"]]
    CH = [min(P, SF - c * P) for c in range(3)]
    QUADS = B * T // HALFQ
    N = SLOT_TILES
    block = ctx.enter_context(nc.Block())

    def ps_shared(q, c, which):
        return ps[:, 2 * ((3 * q + c) % 3) + which, :]

    @block.sync
    def _(sp):
        def store(b):
            if out is not None:
                sp.dma_start(out[b].rearrange("(t p) d -> p t d", p=P), keep.x[:, b * NT:(b + 1) * NT, :]).then_inc(keep.stored, 16)

        sp.wait_ge(s["scattered"], 16 * TOPK * TILES)
        for i in range(N):
            r = i % XS_RING
            if i >= XS_RING:
                j = i - XS_RING
                sp.wait_ge(sent[j % Y_RING], 16 * (j // Y_RING + 1))
            sp.dma_start(xs[:, r, :], slots_dram[i * P:(i + 1) * P, :]).then_inc(xs_in[r], 16)
        for j in range(Y_RING):
            sp.wait_ge(sent[j], 16 * (N // Y_RING))
        for b in range(B):
            if b >= 2:
                sp.wait_ge(s["combined"], b - 1)
                store(b - 2)
            src = parted_dram[b * T * TOPK:(b + 1) * T * TOPK, :].rearrange("(t p k) d -> p t (k d)", p=P, k=TOPK)
            sp.dma_start(back[:, b % 2, :, :], src).then_inc(back_in[b % 2], 16)
        for b in (B - 2, B - 1):
            sp.wait_ge(s["combined"], b + 1)
            store(b)
        if out is not None:
            sp.wait_ge(keep.stored, 16 * B)

    @block.gpsimd
    def _(pool):
        for t in range(TILES):
            for k in range(TOPK):
                nc.gpsimd.indirect_dma_start(out=slots_dram, out_offset=bass.IndirectOffsetOnAxis(ap=keep.slot[:, k, t:t + 1], axis=0),
                                             in_=keep.rows[:, k, t, :], in_offset=None).then_inc(s["scattered"], 16)
        for i in range(N):
            pool.wait_ge(s["y"], i + 1)
            where = xs[:, i % XS_RING, D:D + 1].bitcast(I32)
            nc.gpsimd.indirect_dma_start(out=parted_dram, out_offset=bass.IndirectOffsetOnAxis(ap=where, axis=0),
                                         in_=y[:, i % Y_RING, :], in_offset=None).then_inc(sent[i % Y_RING], 16)

    @block.tensor
    def _(pe):
        def shared_up(q):
            for c in range(3):
                n = 3 * q + c
                if n >= 3:
                    pe.wait_ge(s["up"], n - 2)
                for which, w in enumerate((keep.sw1, keep.sw3)):
                    mm = nc.tensor.matmul(ps[0:CH[c], 2 * (n % 3) + which, :], w[:, c * P:c * P + CH[c]],
                                          keep.xnT[:, q * HALFQ:(q + 1) * HALFQ], start=True, stop=True)
                mm.then_inc(s["hidden"], 1)

        def shared_down(q):
            pe.wait_ge(s["up"], 3 * q + 3)
            if q >= 2:
                pe.wait_ge(s["added"], q - 1)
            for t in range(HALFQ // P):
                for c in range(3):
                    rows = CH[c] + (c == 2)
                    mm = nc.tensor.matmul(ps[:, 6 + q % 2, t * P:(t + 1) * P], up[0:rows, q % 2, c, t * P:(t + 1) * P],
                                          keep.sw2[0:rows, c, :], start=(c == 0), stop=(c == 2))
            mm.then_inc(s["out"], 1)

        for q in range(QUADS):
            shared_up(q)
            if q:
                shared_down(q - 1)
        shared_down(QUADS - 1)
        pe.wait_ge(s["added"], QUADS)

        which = {0: nc.tensor.value_load(keep.expert[0:1, 0:1], min_val=0, max_val=E - 1)}
        for i in range(N + 4):
            if i < N:
                pe.wait_ge(xs_in[i % XS_RING], 16 * (i // XS_RING + 1))
                if i >= 2:
                    pe.wait_ge(s["xT"], i - 1)
                nc.tensor.transpose(ps[:, i % 2, 0:P], xs[:, i % XS_RING, 0:D], keep.ident[:, :]).then_inc(s["xT_ps"], 1)
            if 1 <= i <= N:
                j = i - 1
                e = which[j]
                pe.wait_ge(s["xT"], j + 1)
                if j >= 2:
                    pe.wait_ge(s["hg"], j - 1)
                w = keep.w13[:, :, :, :].rearrange("p e i f -> p (e i f)")[:, bass.ds(e * (2 * F), 2 * F)]
                nc.tensor.matmul(ps[:, 2 + j % 2, 0:2 * F], xsT[:, j % 2, :], w, start=True, stop=True).then_inc(s["h"], 1)
                if j + 1 < N:
                    which[j + 1] = nc.tensor.value_load(keep.expert[0:1, j + 1:j + 2], min_val=0, max_val=E - 1)
            if 3 <= i < N + 3:
                j = i - 3
                pe.wait_ge(s["a"], j + 1)
                if j >= 2:
                    pe.wait_ge(s["aT"], j - 1)
                for c in range(2):
                    mm = nc.tensor.transpose(ps[:, 4 + j % 2, c * P:(c + 1) * P], a[:, j % 2, c * P:(c + 1) * P], keep.ident[:, :])
                mm.then_inc(s["aT_ps"], 1)
            if 4 <= i:
                j = i - 4
                e = which.pop(j)
                pe.wait_ge(s["aT"], j + 1)
                if j >= 2:
                    pe.wait_ge(s["y"], j - 1)
                for c in range(2):
                    w = keep.w2[:, :, :, :].rearrange("p e c d -> p (e c d)")[:, bass.ds(e * (2 * D) + c * D, D)]
                    mm = nc.tensor.matmul(ps[:, 6 + j % 2, 0:D], aT[:, j % 2, c * P:(c + 1) * P], w, start=(c == 0), stop=(c == 1))
                mm.then_inc(s["y_ps"], 1)

    @block.scalar
    def _(act):
        for q in range(QUADS):
            for c in range(3):
                n = 3 * q + c
                act.wait_ge(s["hidden"], n + 1)
                if q >= 2:
                    act.wait_ge(s["up"], n - 5)
                nc.scalar.activation(sil[0:CH[c], q % 2, c, :], ps[0:CH[c], 2 * (n % 3), :], ACT.Silu,
                                     bias=keep.sbias[0:CH[c], 0, c:c + 1]).then_inc(s["sil"], 1)
        for i in range(N + 3):
            if i < N:
                act.wait_ge(s["xT_ps"], i + 1)
                if i >= 2:
                    act.wait_ge(s["h"], i - 1)
                nc.scalar.copy(xsT[:, i % 2, :], ps[:, i % 2, 0:P]).then_inc(s["xT"], 1)
            if 1 <= i <= N:
                j = i - 1
                act.wait_ge(s["hg"], j + 1)
                if j >= 2:
                    act.wait_ge(s["a"], j - 1)
                nc.scalar.activation(act_h[:, j % 2, :], hg[:, j % 2, 0:F], ACT.Silu).then_inc(s["act_h"], 1)
            if 3 <= i:
                j = i - 3
                act.wait_ge(s["aT_ps"], j + 1)
                if j >= 2:
                    act.wait_ge(s["y_ps"], j - 1)
                nc.scalar.copy(aT[:, j % 2, :], ps[:, 4 + j % 2, 0:2 * P]).then_inc(s["aT"], 1)

    @block.vector
    def _(dve):
        v = nc.vector
        link = chained(dve, s["chain"])
        for h in range(2):
            v.memset(up[SF - 2 * P:SF - 2 * P + 1, h, 2, :], 1.0)
        v.memset(a[:, :, F + 1:2 * P], 0.0)
        v.memset(a[:, :, F:F + 1], 1.0)

        def shared_add(q):
            dve.wait_ge(s["out"], q + 1)
            xq = keep.x[:, q * GROUP:(q + 1) * GROUP, :]
            v.tensor_tensor(xq, ps[:, 6 + q % 2, :].rearrange("p (t d) -> p t d", t=GROUP), xq, ALU.add).then_inc(s["added"], 1)

        for q in range(QUADS):
            for c in range(3):
                n = 3 * q + c
                dve.wait_ge(s["sil"], n + 1)
                if q >= 2 and c == 0:
                    dve.wait_ge(s["out"], q - 1)
                v.scalar_tensor_tensor(out=up[0:CH[c], q % 2, c, :], in0=ps[0:CH[c], 2 * (n % 3) + 1, :],
                                       scalar=keep.sbias[0:CH[c], 1, c:c + 1], in1=sil[0:CH[c], q % 2, c, :],
                                       op0=ALU.add, op1=ALU.mult).then_inc(s["up"], 1)
            if q:
                shared_add(q - 1)
        shared_add(QUADS - 1)
        e = v.value_load(keep.expert[0:1, 0:1], min_val=0, max_val=E - 1)
        for i in range(N + 3):
            if i < N:
                dve.wait_ge(s["h"], i + 1)
                if i >= 2:
                    dve.wait_ge(s["a"], i - 1)
                bias = keep.b13[:, :, :, :].rearrange("p e i f -> p (e i f)")[:, bass.ds(e * (2 * F), 2 * F)]
                v.tensor_tensor(hg[:, i % 2, :], ps[:, 2 + i % 2, 0:2 * F], bias, ALU.add).then_inc(s["hg"], 1)
                if i + 1 < N:
                    e = v.value_load(keep.expert[0:1, i + 1:i + 2], min_val=0, max_val=E - 1)
            if 1 <= i <= N:
                j = i - 1
                dve.wait_ge(s["act_h"], j + 1)
                if j >= 2:
                    dve.wait_ge(s["aT_ps"], j - 1)
                v.tensor_tensor(a[:, j % 2, 0:F], act_h[:, j % 2, :], hg[:, j % 2, F:2 * F], ALU.mult).then_inc(s["a"], 1)
            if 3 <= i:
                j = i - 3
                dve.wait_ge(s["y_ps"], j + 1)
                if j >= Y_RING:
                    dve.wait_ge(sent[j % Y_RING], 16 * (j // Y_RING))
                v.tensor_copy(y[:, j % Y_RING, :], ps[:, 6 + j % 2, 0:D]).then_inc(s["y"], 1)
        for b in range(B):
            dve.wait_ge(back_in[b % 2], 16 * (b // 2 + 1))
            for k in range(TOPK):
                for t in range(NT):
                    g = b * NT + t
                    last = v.scalar_tensor_tensor(out=keep.x[:, g, :], in0=back[:, b % 2, t, k * D:(k + 1) * D],
                                                  scalar=keep.weight[:, k, g:g + 1], in1=keep.x[:, g, :],
                                                  op0=ALU.mult, op1=ALU.add)
                if k == 0:
                    link(last)
            last.then_inc(s["combined"], 1)


def feed_forward(nc, ctx, dram, keep, tag, slots_dram, parted_dram, out=None):
    def sb(name, shape, dt=F32):
        return ctx.enter_context(nc.sbuf_tensor(tag + name, shape, dt))

    keep.rows = sb("rows", [P, TOPK, TILES, ROW])
    keep.xnT = sb("xnT", [P, B * T])
    keep.weight = sb("weight", [P, TOPK, TILES])
    keep.slot = sb("slot", [P, TOPK, TILES], I32)
    keep.expert = sb("expert", [P, SLOT_TILES], I32)
    with ExitStack() as c:
        route(nc, c, dram, keep, tag + "r_")
    with ExitStack() as c:
        experts(nc, c, dram, keep, tag + "e_", slots_dram, parted_dram, out)


def state_space(nc, ctx, dram, keep):
    def sb(name, shape, dt=F32):
        return ctx.enter_context(nc.sbuf_tensor(name, shape, dt))

    xn = sb("s_xn", [P, TILES, D])
    xnT = sb("s_xnT", [P, B * T])
    hs = sb("s_hs", [P, B, T])
    ps_t = ctx.enter_context(nc.psum_tensor("s_ps_t", [P, 2, T], F32))
    ps = ctx.enter_context(nc.psum_tensor("s_ps", [P, 4, 512], F32))
    norm = Norm(nc, ctx, keep, "s_", xn, xnT)
    s = semaphores(nc, ctx, "scan", "chain driven taken moved merged projected added")
    block = ctx.enter_context(nc.Block())

    def moves():
        out = []
        for up in (True, False):
            for level in (range(LEVELS) if up else reversed(range(LEVELS - 1))):
                c = 2 << level
                m = T // c
                cols = m if up else m - 1
                per = min(B, 512 // (m if m <= 512 else 512))
                tree = hs[:, :, :].rearrange("p b (m c) -> p b m c", c=c)
                for b in range(0, B, per):
                    if up:
                        src, dst = tree[:, b:b + per, :, c // 2 - 1], tree[:, b:b + per, :, c - 1]
                    else:
                        src, dst = tree[:, b:b + per, 0:cols, c - 1], tree[:, b:b + per, 1:m, c // 2 - 1]
                    out.append((level, b, per, cols, src, dst))
        return out

    plan = moves()
    needs, last_of = [], [0] * B
    for n, (_, b, per, *_) in enumerate(plan):
        needs.append(max(last_of[b:b + per]))
        for i in range(b, b + per):
            last_of[i] = n + 1

    def result(n):
        _, _, per, cols, _, _ = plan[n]
        return ps[:, n % 4, 0:per * cols].rearrange("p (b m) -> p b m", b=per)

    @block.tensor
    def _(pe):
        for b in range(B):
            norm.tensor_turn(nc.tensor, ps_t[:, b % 2, :], b)
        for n in range(B * T // 512):
            if n % 2 == 0:
                pe.wait_ge(norm.s["xnT"], n // 2 + 1)
            if n >= 4:
                pe.wait_ge(s["taken"], n - 3)
            nc.tensor.matmul(ps[:, n % 4, :], keep.b_T[:, :], xnT[:, n * 512:(n + 1) * 512], start=True, stop=True).then_inc(s["driven"], 1)
        pe.wait_ge(s["taken"], B * T // 512)
        for n, (level, b, per, cols, src, _) in enumerate(plan):
            need = max(needs[n], n - 3)
            if need > 0:
                pe.wait_ge(s["merged"], need)
            nc.tensor.matmul(result(n), keep.a_powT[:, level, :], src, start=True, stop=True).then_inc(s["moved"], 1)
        pe.wait_ge(s["merged"], len(plan))
        flat = hs[:, :, :].rearrange("p b t -> p (b t)")
        for g in range(TILES // GROUP):
            if g >= 4:
                pe.wait_ge(s["added"], g - 3)
            for t in range(GROUP):
                at = (g * GROUP + t) * P
                mm = nc.tensor.matmul(ps[:, g % 4, t * P:(t + 1) * P], flat[:, at:at + P], keep.c_T[:, :], start=True, stop=True)
            mm.then_inc(s["projected"], 1)

    @block.scalar
    def _(act):
        for b in range(B):
            norm.scalar_std(nc.scalar, b)
        for b in range(B):
            norm.scalar_copy(nc.scalar, ps_t[:, b % 2, :], b)
        flat = hs[:, :, :].rearrange("p b t -> p (b t)")
        for n in range(B * T // 512):
            act.wait_ge(s["driven"], n + 1)
            nc.scalar.copy(flat[:, n * 512:(n + 1) * 512], ps[:, n % 4, :]).then_inc(s["taken"], 1)

    @block.vector
    def _(dve):
        link = chained(dve, s["chain"])
        v = nc.vector
        for b in range(B):
            norm.vector_stats(v, link, b)
            if b:
                norm.vector_scale(v, link, b - 1)
        norm.vector_scale(v, link, B - 1)
        dve.wait_ge(s["taken"], B * T // 512)
        for n, (*_, dst) in enumerate(plan):
            dve.wait_ge(s["moved"], n + 1)
            if needs[n] > 0:
                dve.wait_ge(s["merged"], needs[n])
            v.tensor_tensor(dst, result(n), dst, ALU.add).then_inc(s["merged"], 1)
        for g in range(TILES // GROUP):
            dve.wait_ge(s["projected"], g + 1)
            xs = keep.x[:, g * GROUP:(g + 1) * GROUP, :]
            v.tensor_tensor(xs, ps[:, g % 4, :].rearrange("p (t d) -> p t d", t=GROUP), xs, ALU.add).then_inc(s["added"], 1)


def hybrid_kernel(nc, inp, out):
    dram = inp
    keep = Keep()
    with ExitStack() as ctx:
        def sb(name, shape, dt=F32):
            return ctx.enter_context(nc.sbuf_tensor(name, shape, dt))
        keep.x = sb("x", [P, TILES, D])
        keep.ident = sb("ident", [P, P])
        keep.ones = sb("ones", [P, P])
        keep.eps = sb("eps", [P, 1])
        keep.a_nat, keep.a_T = sb("a_nat", [P, P]), sb("a_T", [P, P])
        keep.b_T, keep.c_T = sb("b_T", [P, P]), sb("c_T", [P, P])
        keep.a_powT = sb("a_powT", [P, LEVELS, P])
        place_weights(nc, ctx, keep)
        slots = [nc.dram_tensor(f"slots{i}", [SLOTS, ROW], F32).ap() for i in range(2)]
        parted = [nc.dram_tensor(f"parted{i}", [B * T * TOPK + SLOTS, D], F32).ap() for i in range(2)]
        keep.stored = ctx.enter_context(nc.semaphore("stored"))
        keep.q_parts = nc.dram_tensor("q_parts", [PARTS, P, B * T], BF16).ap()
        keep.k_parts = nc.dram_tensor("k_parts", [PARTS, P, B * T], BF16).ap()
        with ExitStack() as attn_ctx:
            keep.v = attn_ctx.enter_context(nc.sbuf_tensor("v", [P, TILES, H, HD + 1], F32))
            with ExitStack() as c:
                load_and_project(nc, c, dram, keep)
            keep.attn = attn_ctx.enter_context(nc.sbuf_tensor("attn", [P, TILES, D], F32))
            with ExitStack() as c:
                attention(nc, c, dram, keep, slots)
            with ExitStack() as c:
                project_out(nc, c, dram, keep)
        with ExitStack() as c:
            feed_forward(nc, c, dram, keep, "f1", slots[0], parted[0])
        with ExitStack() as c:
            state_space(nc, c, dram, keep)
        with ExitStack() as c:
            feed_forward(nc, c, dram, keep, "f2", slots[1], parted[1], out)


NAMES = {
    "x": "L0_attn_a_x", "w_q": "L0_attn_a_W_q", "w_dkv": "L0_attn_a_W_dkv", "w_uk": "L0_attn_a_W_uk",
    "w_uv": "L0_attn_a_W_uv", "w_o": "L0_attn_a_W_o", "ln_gamma": "L0_attn_a_ln_gamma", "ln_beta": "L0_attn_a_ln_beta",
    "w_a": "L0_attn_b_W_A", "w_b": "L0_attn_b_W_B", "w_c": "L0_attn_b_W_C",
    "gate_w": "L0_ffn_gate_w", "gate_b": "L0_ffn_gate_b", "w1": "L0_ffn_w1", "b1": "L0_ffn_b1", "w3": "L0_ffn_w3",
    "b3": "L0_ffn_b3", "w2": "L0_ffn_w2", "b2": "L0_ffn_b2", "sw1": "L0_ffn_sw1", "sb1": "L0_ffn_sb1",
    "sw3": "L0_ffn_sw3", "sb3": "L0_ffn_sb3", "sw2": "L0_ffn_sw2", "sb2": "L0_ffn_sb2",
}


def shape_constants():
    f = np.float32
    inv_freq = (f(1.0) / f(10000.0) ** (np.arange(HALF, dtype=f) / f(HALF))).astype(f)
    angles = (np.arange(T, dtype=f)[:, None] * inv_freq[None, :]).astype(f)
    rows = np.zeros((SLOTS, ROW), f)
    rows[:, D] = (np.arange(SLOTS, dtype=np.int32) + B * T * TOPK).view(f)
    tokens = np.arange(TILES)[None, :] * P + np.arange(P)[:, None]
    token_id = np.ascontiguousarray(np.stack([tokens * TOPK + k for k in range(TOPK)], axis=1).astype(np.int32))
    return {
        "cos": np.ascontiguousarray(np.cos(angles).astype(f).reshape(NT, P, HALF).transpose(1, 0, 2)),
        "sin": np.ascontiguousarray(np.sin(angles).astype(f).reshape(NT, P, HALF).transpose(1, 0, 2)),
        "ident": np.eye(P, dtype=f),
        "before": np.triu(np.ones((P, P), f), 1),
        "expert_no": np.arange(E, dtype=f),
        "tile_no": np.arange(SLOT_TILES, dtype=f),
        "token_id": token_id.view(f),
        "slot_rows": rows,
    }


def kernel(**inputs):
    import concourse.bacc as bacc
    from concourse.bass_utils import run_bass_kernel_spmd

    nc = bacc.Bacc("TRN2", target_bir_lowering=False, num_devices=1)
    arrays, inp = {}, {}
    held = {short: np.ascontiguousarray(inputs[name]) for short, name in NAMES.items()}
    for short, a in {**held, **shape_constants()}.items():
        arrays[f"in_{short}"] = a
        inp[short] = nc.dram_tensor(f"in_{short}", a.shape, mybir.dt.from_np(a.dtype), kind="ExternalInput").ap()
    out = nc.dram_tensor("out", (B, T, D), F32, kind="ExternalOutput").ap()
    hybrid_kernel(nc, inp, out)
    r = run_bass_kernel_spmd(nc, [arrays], core_ids=[0])
    return r.results[0]["out"]
```

```python
from contextlib import ExitStack

import numpy as np
import concourse.bass as bass
from concourse import mybir

F32 = mybir.dt.float32
BF16 = mybir.dt.bfloat16
I32 = mybir.dt.int32
U32 = mybir.dt.uint32
ALU = mybir.AluOpType
ACT = mybir.ActivationFunctionType
AX_X = mybir.AxisListType.X

P = 128
B, T, D = 4, 1024, 128
NT = T // P
TILES = B * NT
H, HD = 16, 8
HALF = HD // 2
LAT = 32
EPS = 1e-5
SCALE = 1.0 / float(np.sqrt(np.float32(HD)))
PARTS = 3
HT = NT // 2
HALVES = 2 * B
Q_TURN, K_TURN = 4, 6
POWER_ITERS = 10
HALF_STEPS = 2 * POWER_ITERS + 1
ROWS3 = 3 * 32

E, TOPK = 16, 2
F = 176
FH = F - P
SF = 2 * F
SLOT_TILES = B * T * TOPK // P + E
REGION = B * T + P
IDLE = E * REGION
SLOTS = IDLE + E * P
ROW = D + 2


def semaphores(nc, ctx, phase, names):
    made = {n: nc.alloc_semaphore(f"{phase}_{n}") for n in names.split()}

    def give_back():
        nc.clear_and_free_semaphores(list(made.values()))
        nc.all_engine_barrier()

    ctx.callback(give_back)
    return made


class Keep:
    pass


def chained(engine, sem):
    done = [0]

    def link(ins):
        done[0] += 1
        ins.then_inc(sem, 1)
        engine.wait_ge(sem, done[0])

    return link


def load_and_project(nc, ctx, dram, keep):
    def sb(name, shape, dt=F32):
        return ctx.enter_context(nc.sbuf_tensor(name, shape, dt))

    x = keep.x
    xn = sb("a_xn", [P, TILES, D])
    xnT = sb("a_xnT", [P, TILES, P])
    stats = sb("a_stats", [P, TILES, 6])
    mv = sb("a_mv", [P, TILES, 2])
    std = sb("a_std", [P, TILES])
    rstd = sb("a_rstd", [P, TILES])
    lstats = sb("a_lstats", [P, TILES, 6])
    lmv = sb("a_lmv", [P, TILES, 2])
    lstd = sb("a_lstd", [P, TILES])
    lrstd = sb("a_lrstd", [P, TILES])
    w_in = sb("a_w_in", [P, D + LAT])
    w_kv = sb("a_w_kv", [P, 2 * D])
    gamma = sb("a_gamma", [P, LAT])
    beta = sb("a_beta", [P, LAT])
    cos = sb("a_cos", [P, NT, HALF])
    sin = sb("a_sin", [P, NT, HALF])
    q = keep.w13[:, :, :, :].rearrange("p e i f -> p (e i f)")[:, 0:TILES * (D + LAT)].rearrange("p (t c) -> p t c", c=D + LAT)
    k = keep.b13[:, :, :, :].rearrange("p e i f -> p (e i f)")[:, 0:TILES * D].rearrange("p (t c) -> p t c", c=D)
    tmp_q = sb("a_tmp_q", [P, 2, HT, H, HALF])
    tmp_k = sb("a_tmp_k", [P, 2, HT, H, HALF])
    nmr = sb("a_nmr", [P, TILES])
    lat = sb("a_lat", [P, TILES, P])
    latn = sb("a_latn", [P, HT, LAT])
    latT = sb("a_latT", [P, 2, HT * P])
    parts = sb("a_parts", [P, 2, 2, PARTS, HT * P], BF16)
    w_ssm = sb("a_w_ssm", [P, 3, P])
    w_ssmT = sb("a_w_ssmT", [P, 3, P])
    uv = sb("a_uv", [P, 3])
    squares = sb("a_squares", [ROWS3, P])
    unit = sb("a_unit", [ROWS3, P])
    u_last = sb("a_u_last", [ROWS3, P])
    sq_sum = sb("a_sq_sum", [ROWS3, 1])
    norm = sb("a_norm", [ROWS3, 1])
    inv = sb("a_inv", [ROWS3, 1])
    pick = sb("a_pick", [ROWS3, 3])
    sigma = sb("a_sigma", [P, 3])
    qr, kr = xn, lat
    rest = xnT
    ps_t = ctx.enter_context(nc.psum_tensor("a_ps_t", [P, 2, HT * P], F32))
    ps_p = ctx.enter_context(nc.psum_tensor("a_ps_p", [P, 2, HT, 256], F32))
    ps_w = ctx.enter_context(nc.psum_tensor("a_ps_w", [P, 512], F32))
    ps_s = ctx.enter_context(nc.psum_tensor("a_ps_s", [P, 512], F32))
    s = semaphores(nc, ctx, "project", "x_in0 x_in1 x_in2 x_in3 ident tables w_in w_kv ssm zeroed eps mv std xn xnT_ps xnT "
             "proj q_sb nmr k_first k_second lmv lstd lat_sb latT_ps latT kv k_sb v_sb qr chain_v chain_p "
             "qT kT q_h k_h q_rest k_rest q_m k_m q_l k_l pw_mv pw_ss pw_std pw_unit pw_turned pw_uv wT_ps wT scaled "
             "sent_q0 sent_q1 sent_k0 sent_k1 stacked")
    x_in = [s["x_in0"], s["x_in1"], s["x_in2"], s["x_in3"]]
    sent = [[s["sent_q0"], s["sent_q1"]], [s["sent_k0"], s["sent_k1"]]]
    block = ctx.enter_context(nc.Block())

    def tiles(h):
        return slice(h * HT, (h + 1) * HT)

    def live(h):
        return 0 <= h < HALVES

    def rope_views(src, dst, h):
        at = slice(h * HT % NT, h * HT % NT + HT)
        i = src[:, tiles(h), 0:D].rearrange("p t (h s d) -> p t h s d", s=2, d=HALF)
        o = dst[:, tiles(h), :].rearrange("p t (s d h) -> p t h s d", s=2, d=HALF)
        c = cos[:, at, :].unsqueeze(2).to_broadcast([P, HT, H, HALF])
        n = sin[:, at, :].unsqueeze(2).to_broadcast([P, HT, H, HALF])
        return i[:, :, :, 0, :], i[:, :, :, 1, :], o[:, :, :, 0, :], o[:, :, :, 1, :], c, n

    def rope(engine, link, src, dst, tmp, h, done):
        x1, x2, o1, o2, c, n = rope_views(src, dst, h)
        engine.tensor_tensor(o1, x1, c, ALU.mult)
        engine.tensor_tensor(tmp[:, 0], x2, n, ALU.mult)
        engine.tensor_tensor(o2, x1, n, ALU.mult)
        link(engine.tensor_tensor(tmp[:, 1], x2, c, ALU.mult))
        engine.tensor_tensor(o1, o1, tmp[:, 0], ALU.subtract)
        engine.tensor_tensor(o2, o2, tmp[:, 1], ALU.add).then_inc(done, 1)
        engine.wait_ge(done, h + 1)

    def rope_first(engine, link, src, dst, tmp, h, done):
        x1, x2, o1, _, c, n = rope_views(src, dst, h)
        engine.tensor_tensor(o1, x1, c, ALU.mult)
        link(engine.tensor_tensor(tmp, x2, n, ALU.mult))
        engine.tensor_tensor(o1, o1, tmp, ALU.subtract).then_inc(done, 1)

    def rope_second(engine, link, src, dst, tmp, h, done):
        x1, x2, _, o2, c, n = rope_views(src, dst, h)
        engine.tensor_tensor(o2, x1, n, ALU.mult)
        link(engine.tensor_tensor(tmp, x2, c, ALU.mult))
        engine.tensor_tensor(o2, o2, tmp, ALU.add).then_inc(done, 1)
        engine.wait_ge(done, h + 1)

    @block.sync
    def _(sp):
        def load_x(b):
            sp.dma_start(x[:, b * NT:(b + 1) * NT, :], dram["x"][b].rearrange("(t p) d -> p t d", p=P)).then_inc(x_in[b], 16)

        load_x(0)
        sp.dma_start(keep.ident[:, :], dram["ident"]).then_inc(s["ident"], 16)
        for i, w in enumerate((dram["w_a"], dram["w_b"], dram["w_c"])):
            sp.dma_start(w_ssm[:, i, :], w).then_inc(s["ssm"], 16)
        sp.dma_start(w_in[:, 0:D], dram["w_q"]).then_inc(s["w_in"], 16)
        sp.dma_start(w_in[:, D:D + LAT], dram["w_dkv"]).then_inc(s["w_in"], 16)
        load_x(1)
        sp.dma_start(cos[:, :, :], dram["cos"]).then_inc(s["tables"], 16)
        sp.dma_start(sin[:, :, :], dram["sin"]).then_inc(s["tables"], 16)
        sp.dma_start(gamma[:, :], dram["ln_gamma"].partition_broadcast(P)).then_inc(s["tables"], 16)
        sp.dma_start(beta[:, :], dram["ln_beta"].partition_broadcast(P)).then_inc(s["tables"], 16)
        sp.dma_start(w_kv[0:LAT, 0:D], dram["w_uk"]).then_inc(s["w_kv"], 16)
        sp.dma_start(w_kv[0:LAT, D:2 * D], dram["w_uv"]).then_inc(s["w_kv"], 16)
        load_x(2)
        load_x(3)
        for h in range(HALVES + K_TURN - Q_TURN):
            for n, (out, ready, j) in enumerate(((keep.q_parts, s["q_l"], h), (keep.k_parts, s["k_l"], h - (K_TURN - Q_TURN)))):
                if live(j):
                    sp.wait_ge(ready, j + 1)
                    at = slice(j * HT * P, (j + 1) * HT * P)
                    sp.dma_start(out[:, :, at].rearrange("i r t -> r i t"), parts[:, n, j % 2, :, :]).then_inc(sent[n][j % 2], 16)
            if h == K_TURN - Q_TURN + 3:
                for done in sent[0] + sent[1]:
                    sp.wait_ge(done, 16)
                load_stacks(sp, keep, 0, s["stacked"])
        sp.wait_ge(s["stacked"], 16 * STACK_DMAS)
        for done in sent[0] + sent[1]:
            sp.wait_ge(done, 16 * HALVES // 2)

    @block.gpsimd
    def _(pool):
        nc.gpsimd.memset(keep.eps[:, :], EPS).then_inc(s["eps"], 1)
        pool.wait_ge(s["eps"], 1)
        for g in range(1, P // LAT):
            nc.gpsimd.memset(w_kv[g * LAT:(g + 1) * LAT, :], 0.0).then_inc(s["zeroed"], 1)
            pool.wait_ge(s["zeroed"], g)
        nc.gpsimd.memset(lat[:, :, :], 0.0).then_inc(s["zeroed"], 1)
        link = chained(pool, s["chain_p"])

        def last_part(n, j, middle, done):
            pool.wait_ge(middle, j + 1)
            r = rest[:, tiles(j), :].rearrange("p t c -> p (t c)")
            nc.gpsimd.tensor_tensor(parts[:, n, j % 2, 2, :], r, parts[:, n, j % 2, 1, :], ALU.subtract).then_inc(done, 1)
            pool.wait_ge(done, j + 1)

        pool.wait_ge(s["tables"], 64)
        for h in range(HALVES + K_TURN - Q_TURN):
            if live(h):
                last_part(0, h, s["q_m"], s["q_l"])
            if live(h):
                pool.wait_ge(s["k_sb"], h + 1)
                rope_second(nc.gpsimd, link, k, kr, tmp_k[:, 1], h, s["k_second"])
            j = h - (K_TURN - Q_TURN)
            if live(j):
                last_part(1, j, s["k_m"], s["k_l"])

    @block.tensor
    def _(pe):
        def vectors(n):
            if n > HALF_STEPS:
                return
            w = w_ssm if n % 2 == 0 else w_ssmT
            pe.wait_ge(s["pw_uv"], n + 1)
            for i in range(3):
                mm = nc.tensor.matmul(ps_w[32 * i:32 * i + 1, 0:P], uv[:, i:i + 1], w[:, i, :], start=True, stop=True)
            mm.then_inc(s["pw_mv"], 1)

        def turn_vectors(n):
            if n > HALF_STEPS:
                return
            pe.wait_ge(s["pw_unit"], n + 1)
            if n < HALF_STEPS:
                nc.tensor.transpose(ps_s[:, 0:ROWS3], unit[:, :], keep.ident[0:ROWS3, 0:ROWS3]).then_inc(s["pw_turned"], 1)
            else:
                nc.tensor.matmul(ps_s[:, 0:3], unit[:, :], pick[:, :], start=True, stop=True).then_inc(s["pw_turned"], 1)

        def turn(src, h, bank, done):
            for t in range(HT):
                mm = nc.tensor.transpose(ps_t[:, bank, t * P:(t + 1) * P], src[:, h * HT + t, :], keep.ident[:, :])
            mm.then_inc(done, 1)

        pe.wait_ge(s["ident"], 16)
        pe.wait_ge(s["ssm"], 48)
        for i in range(3):
            mm = nc.tensor.transpose(ps_s[:, i * P:(i + 1) * P], w_ssm[:, i, :], keep.ident[:, :])
        mm.then_inc(s["wT_ps"], 1)
        for i in range(HALVES + K_TURN):
            vectors(2 * i)
            if live(i - 1):
                j = i - 1
                if j == 0:
                    pe.wait_ge(s["w_in"], 32)
                pe.wait_ge(s["xnT"], j + 1)
                if j:
                    pe.wait_ge(s["q_sb"], j)
                for t in range(HT):
                    mm = nc.tensor.matmul(ps_p[:, 0, t, 0:D + LAT], xnT[:, j * HT + t, :], w_in[:, :], start=True, stop=True)
                mm.then_inc(s["proj"], 1)
            turn_vectors(2 * i)
            if live(i):
                pe.wait_ge(s["xn"], i + 1)
                if i:
                    pe.wait_ge(s["xnT"], i)
                if live(i - Q_TURN - 1):
                    pe.wait_ge(s["q_rest"], i - Q_TURN)
                turn(xn, i, 0, s["xnT_ps"])
            vectors(2 * i + 1)
            if live(i - Q_TURN - 1):
                j = i - Q_TURN - 1
                if j == 0:
                    pe.wait_ge(s["w_kv"], 32)
                    pe.wait_ge(s["zeroed"], P // LAT)
                pe.wait_ge(s["latT"], j + 1)
                if j:
                    pe.wait_ge(s["v_sb"], j)
                for t in range(HT):
                    mm = nc.tensor.matmul(ps_p[:, 1, t, :], latT[:, j % 2, t * P:(t + 1) * P], w_kv[:, :], start=True, stop=True)
                mm.then_inc(s["kv"], 1)
            turn_vectors(2 * i + 1)
            if live(i - Q_TURN):
                j = i - Q_TURN
                pe.wait_ge(s["lat_sb"], j + 1)
                if j:
                    pe.wait_ge(s["latT"], j)
                if live(i - K_TURN - 1):
                    pe.wait_ge(s["k_rest"], i - K_TURN)
                turn(lat, j, 1, s["latT_ps"])
            if live(i - Q_TURN):
                j = i - Q_TURN
                pe.wait_ge(s["qr"], j + 1)
                pe.wait_ge(s["xnT"], min(i + 1, HALVES))
                if j:
                    pe.wait_ge(s["q_rest"], j)
                turn(qr, j, 0, s["qT"])
            if live(i - K_TURN):
                j = i - K_TURN
                pe.wait_ge(s["k_first"], j + 1)
                pe.wait_ge(s["k_second"], j + 1)
                pe.wait_ge(s["latT"], min(i - Q_TURN + 1, HALVES))
                if j:
                    pe.wait_ge(s["k_rest"], j)
                turn(kr, j, 1, s["kT"])

    @block.scalar
    def _(act):
        def length(n):
            if n >= HALF_STEPS:
                return
            act.wait_ge(s["pw_mv"], n + 1)
            nc.scalar.activation(squares[:, :], ps_w[0:ROWS3, 0:P], ACT.Square, accum_out=sq_sum[:, :]).then_inc(s["pw_ss"], 1)
            act.wait_ge(s["pw_ss"], n + 1)
            nc.scalar.activation(norm[:, :], sq_sum[:, :], ACT.Sqrt).then_inc(s["pw_std"], 1)

        def columns(n):
            if n >= HALF_STEPS:
                return
            act.wait_ge(s["pw_turned"], n + 1)
            nc.scalar.copy(uv[:, :], ps_s[:, 0:ROWS3].rearrange("p (i c) -> p i c", c=LAT)[:, :, 0]).then_inc(s["pw_uv"], 1)

        def first_part(n, j, turned, done):
            act.wait_ge(turned, j + 1)
            if j >= 2:
                act.wait_ge(sent[n][j % 2], 16 * (j // 2))
            nc.scalar.copy(parts[:, n, j % 2, 0, :], ps_t[:, n, :]).then_inc(done, 1)

        def middle_part(n, j, ready, done):
            act.wait_ge(ready, j + 1)
            nc.scalar.copy(parts[:, n, j % 2, 1, :], rest[:, tiles(j), :].rearrange("p t c -> p (t c)")).then_inc(done, 1)

        act.wait_ge(s["eps"], 1)

        def deviation(h):
            act.wait_ge(s["mv"], h + 1)
            nc.scalar.activation(std[:, tiles(h)], mv[:, tiles(h), 1], ACT.Sqrt, bias=keep.eps[:, 0:1]).then_inc(s["std"], 1)

        deviation(0)
        act.wait_ge(s["wT_ps"], 1)
        nc.scalar.copy(w_ssmT[:, :, :], ps_s[:, 0:3 * P].rearrange("p (i o) -> p i o", i=3)).then_inc(s["wT"], 1)
        for i in range(HALVES + K_TURN + 1):
            if live(i + 1):
                deviation(i + 1)
            length(2 * i)
            if live(i):
                act.wait_ge(s["nmr"], i + 1)
                for t in range(i * HT, (i + 1) * HT):
                    last = nc.scalar.activation(xn[:, t, :], x[:, t, :], ACT.Identity, bias=nmr[:, t:t + 1], scale=rstd[:, t:t + 1])
                last.then_inc(s["xn"], 1)
            if live(i - 1):
                act.wait_ge(s["proj"], i)
                nc.scalar.copy(q[:, tiles(i - 1), :], ps_p[:, 0, :, 0:D + LAT]).then_inc(s["q_sb"], 1)
            columns(2 * i)
            if live(i):
                act.wait_ge(s["xnT_ps"], i + 1)
                nc.scalar.copy(xnT[:, tiles(i), :], ps_t[:, 0, :].rearrange("p (t c) -> p t c", t=HT)).then_inc(s["xnT"], 1)
            length(2 * i + 1)
            if live(i - 2):
                act.wait_ge(s["lmv"], i - 1)
                nc.scalar.activation(lstd[:, tiles(i - 2)], lmv[:, tiles(i - 2), 1], ACT.Sqrt, bias=keep.eps[:, 0:1]).then_inc(s["lstd"], 1)
            if live(i - Q_TURN - 1):
                middle_part(0, i - Q_TURN - 1, s["q_rest"], s["q_m"])
                j = i - Q_TURN - 1
                act.wait_ge(s["kv"], j + 1)
                nc.scalar.copy(k[:, tiles(j), :], ps_p[:, 1, :, 0:D]).then_inc(s["k_sb"], 1)
                nc.scalar.copy(keep.v[:, tiles(j), :, 0:HD], ps_p[:, 1, :, D:2 * D].rearrange("p t (h d) -> p t h d", h=H)).then_inc(s["v_sb"], 1)
            columns(2 * i + 1)
            if live(i - K_TURN - 1):
                middle_part(1, i - K_TURN - 1, s["k_rest"], s["k_m"])
            if live(i - Q_TURN):
                j = i - Q_TURN
                act.wait_ge(s["latT_ps"], j + 1)
                if j >= 2:
                    act.wait_ge(s["kv"], j - 1)
                nc.scalar.copy(latT[:, j % 2, :], ps_t[:, 1, :]).then_inc(s["latT"], 1)
                first_part(0, j, s["qT"], s["q_h"])
            if live(i - K_TURN):
                act.wait_ge(s["q_l"], i - K_TURN + 1)
                first_part(1, i - K_TURN, s["kT"], s["k_h"])

    @block.vector
    def _(dve):
        link = chained(dve, s["chain_v"])
        v = nc.vector

        def statistics(h):
            dve.wait_ge(x_in[h * HT // NT], 16)
            for t in range(h * HT, (h + 1) * HT):
                last = v.bn_stats(stats[:, t, :], x[:, t, :])
            link(last)
            for t in range(h * HT, (h + 1) * HT):
                last = v.bn_aggr(mv[:, t, :], stats[:, t, :])
            last.then_inc(s["mv"], 1)

        def units(n):
            if n > HALF_STEPS:
                return
            if n < HALF_STEPS:
                dve.wait_ge(s["pw_std"], n + 1)
                link(v.tensor_scalar(inv[:, :], norm[:, :], 1e-12, None, ALU.add))
                link(v.reciprocal(inv[:, :], inv[:, :]))
                if n == HALF_STEPS - 2:
                    v.tensor_scalar(u_last[:, :], ps_w[0:ROWS3, 0:P], inv[:, 0:1], None, ALU.mult)
                v.tensor_scalar(unit[:, :], ps_w[0:ROWS3, 0:P], inv[:, 0:1], None, ALU.mult).then_inc(s["pw_unit"], 1)
                return
            dve.wait_ge(s["pw_mv"], n + 1)
            link(v.tensor_copy(unit[:, :], ps_w[0:ROWS3, 0:P]))
            link(v.tensor_tensor_reduce(squares[:, :], unit[:, :], u_last[:, :], 1.0, 0.0, ALU.mult, ALU.add, sq_sum[:, :]))
            link(v.tensor_scalar(unit[:, :], keep.ones[0:ROWS3, :], sq_sum[:, 0:1], None, ALU.mult))
            v.tensor_copy(pick[:, :], keep.ident[0:ROWS3, 0:ROWS3].rearrange("p (i c) -> p i c", c=LAT)[:, :, 0]).then_inc(s["pw_unit"], 1)
            dve.wait_ge(s["pw_turned"], n + 1)
            link(v.tensor_copy(sigma[:, :], ps_s[:, 0:3]))
            link(v.reciprocal(sigma[:, :], sigma[:, :]))
            v.tensor_scalar(keep.a_nat[:, :], w_ssm[:, 0, :], sigma[:, 0:1], None, ALU.mult)
            v.tensor_scalar(keep.a_T[:, :], w_ssmT[:, 0, :], sigma[:, 0:1], None, ALU.mult)
            v.tensor_scalar(keep.b_T[:, :], w_ssmT[:, 1, :], sigma[:, 1:2], None, ALU.mult)
            v.tensor_scalar(keep.c_T[:, :], w_ssmT[:, 2, :], sigma[:, 2:3], None, ALU.mult).then_inc(s["scaled"], 1)

        def take_rest(n, j, first, done):
            dve.wait_ge(first, j + 1)
            r = rest[:, tiles(j), :].rearrange("p t c -> p (t c)")
            v.tensor_tensor(r, ps_t[:, n, :], parts[:, n, j % 2, 0, :], ALU.subtract).then_inc(done, 1)

        v.memset(keep.ones[:, :], 1.0)
        v.memset(keep.v[:, :, :, HD:HD + 1], 1.0)
        v.memset(uv[:, :], float(1.0 / np.sqrt(np.float32(P))))
        link(v.memset(ps_w[:, 0:P], 0.0))
        statistics(0)
        dve.wait_ge(s["wT"], 1)
        v.memset(squares[:, :], 0.0).then_inc(s["pw_uv"], 1)
        for i in range(HALVES + K_TURN + 1):
            if live(i + 1):
                statistics(i + 1)
            if live(i):
                dve.wait_ge(s["std"], i + 1)
                link(v.reciprocal(rstd[:, tiles(i)], std[:, tiles(i)]))
                v.scalar_tensor_tensor(out=nmr[:, tiles(i)], in0=mv[:, tiles(i), 0], scalar=-1.0, in1=rstd[:, tiles(i)],
                                       op0=ALU.mult, op1=ALU.mult).then_inc(s["nmr"], 1)
            units(2 * i)
            if live(i - Q_TURN - 1):
                take_rest(0, i - Q_TURN - 1, s["q_h"], s["q_rest"])
            if live(i - K_TURN - 1):
                take_rest(1, i - K_TURN - 1, s["k_h"], s["k_rest"])
            if live(i - K_TURN):
                dve.wait_ge(s["k_sb"], i - K_TURN + 1)
                rope_first(v, link, k, kr, tmp_k[:, 0], i - K_TURN, s["k_first"])
            if live(i - 2):
                j = i - 2
                dve.wait_ge(s["q_sb"], j + 1)
                for t in range(j * HT, (j + 1) * HT):
                    last = v.bn_stats(lstats[:, t, :], q[:, t, D:D + LAT])
                link(last)
                for t in range(j * HT, (j + 1) * HT):
                    last = v.bn_aggr(lmv[:, t, :], lstats[:, t, :])
                last.then_inc(s["lmv"], 1)
            if live(i - 3):
                j = i - 3
                if j == 0:
                    dve.wait_ge(s["tables"], 64)
                    dve.wait_ge(s["zeroed"], P // LAT)
                dve.wait_ge(s["lstd"], j + 1)
                link(v.reciprocal(lrstd[:, tiles(j)], lstd[:, tiles(j)]))
                wide = [P, HT, LAT]
                for t in range(HT):
                    g = j * HT + t
                    last = v.tensor_scalar(latn[:, t, :], q[:, g, D:D + LAT], lmv[:, g, 0:1], lrstd[:, g:g + 1], ALU.subtract, ALU.mult)
                link(last)
                link(v.tensor_tensor(latn[:, :, :], latn[:, :, :], gamma[:, :].unsqueeze(1).to_broadcast(wide), ALU.mult))
                v.tensor_tensor(lat[:, tiles(j), 0:LAT], latn[:, :, :], beta[:, :].unsqueeze(1).to_broadcast(wide),
                                ALU.add).then_inc(s["lat_sb"], 1)
            units(2 * i + 1)
            if live(i - 3):
                rope(v, link, q, qr, tmp_q, i - 3, s["qr"])
        dve.wait_ge(s["scaled"], 1)


def place_weights(nc, ctx, keep):
    def sb(name, shape, dt=F32):
        return ctx.enter_context(nc.sbuf_tensor(name, shape, dt))

    keep.w13 = sb("w13", [P, E, 2, F])
    keep.b13 = sb("b13", [P, E, 2, F])
    keep.w2 = sb("w2", [P, E, 2, D])
    keep.sw1, keep.sw3 = sb("sw1", [P, SF]), sb("sw3", [P, SF])
    keep.sbias = sb("sbias", [P, 2, 3])
    keep.sw2 = sb("sw2", [P, 3, D])
    keep.gate_w = sb("gate_w", [P, E])
    keep.gate_b = sb("gate_b", [P, E])
    keep.before = sb("before", [P, P])
    keep.expert_no = sb("expert_no", [P, E])
    keep.tile_no = sb("tile_no", [P, SLOT_TILES])
    keep.token_id = sb("token_id", [P, TOPK, TILES])
    keep.region = sb("region", [P, E])


def background_loads(dram, keep, slots):
    rows = [(c, min(P, SF - c * P)) for c in range(3)]
    half = E // 2
    out = [(keep.gate_w[:, :], dram["gate_w"]),
           (keep.gate_b[:, :], dram["gate_b"].partition_broadcast(P)),
           (keep.before[:, :], dram["before"]),
           (keep.expert_no[:, :], dram["expert_no"].partition_broadcast(P)),
           (keep.tile_no[:, :], dram["tile_no"].partition_broadcast(P)),
           (keep.token_id[:, :, :], dram["token_id"]),
           (keep.region[:, :], dram["region"].partition_broadcast(P)),
           (keep.sw1[:, :], dram["sw1"]),
           (keep.sw3[:, :], dram["sw3"])]
    out += [(keep.sbias[0:n, i, c:c + 1], v[c * P:c * P + n].unsqueeze(1))
            for i, v in enumerate((dram["sb1"], dram["sb3"])) for c, n in rows]
    out += [(keep.sw2[0:n, c, :], dram["sw2"][c * P:c * P + n, :]) for c, n in rows]
    out += [(keep.sw2[SF - 2 * P:SF - 2 * P + 1, 2, :], dram["sb2"].unsqueeze(0))]
    for e in (slice(0, half), slice(half, E)):
        out += [(keep.w13[:, e, 0, :], dram["w1"][e].rearrange("e d f -> d e f")),
                (keep.w13[:, e, 1, :], dram["w3"][e].rearrange("e d f -> d e f")),
                (keep.b13[:, e, 0, :], dram["b1"][e].partition_broadcast(P)),
                (keep.b13[:, e, 1, :], dram["b3"][e].partition_broadcast(P)),
                (keep.w2[:, e, 0, :], dram["w2"][e, 0:P, :].rearrange("e f d -> f e d")),
                (keep.w2[0:FH, e, 1, :], dram["w2"][e, P:F, :].rearrange("e f d -> f e d")),
                (keep.w2[FH:FH + 1, e, 1, :], dram["b2"][e].unsqueeze(0))]
    out += [(slots[IDLE:SLOTS].rearrange("(a b) c -> a (b c)", a=P), dram["slot_rows"][E * P:].rearrange("(a b) c -> a (b c)", a=P))]
    return out


G = 4
UNITS = B * H // G
RING = 3
PAIRS = PARTS * PARTS
KROWS = PAIRS * HD
SROWS = KROWS + PARTS
HALFQ = 512
LEAD = 1.33
ROWS_LATER = 5
OUTPUT = -1
SPARE = 3
LAG = 2


STACK_DMAS = PARTS + PAIRS


def load_stacks(engine, keep, u, done):
    b, g, r = u // G, u % G, u % RING
    q_src, k_src = (x.rearrange("i (d h) t -> (i d) h t", h=H)[:, g * G:(g + 1) * G, b * T:(b + 1) * T]
                    for x in (keep.q_parts, keep.k_parts))
    for i in range(PARTS):
        at = i * PARTS * HD
        engine.dma_start(keep.k_stack[r][at:at + PARTS * HD, :, :], k_src).then_inc(done, 16)
        for j in range(PARTS):
            engine.dma_start(keep.q_stack[r][at + j * HD:at + (j + 1) * HD, :, :], q_src[i * HD:(i + 1) * HD]).then_inc(done, 16)


def unit_steps():
    return [(hf, kb, max(kb * P, hf * HALFQ), (hf + 1) * HALFQ - max(kb * P, hf * HALFQ))
            for hf in range(T // HALFQ) for kb in range((hf + 1) * HALFQ // P)]


def max_tasks():
    return [(j, qt, c, min(HALFQ, (qt + 1) * P - c)) for j in range(G) for qt in range(NT)
            for c in range(0, (qt + 1) * P, HALFQ)]


def maxima_stream():
    tasks = len(max_tasks())
    out = []
    for u in range(UNITS):
        for n in range(tasks):
            out.append((u, n))
            if u and n == ROWS_LATER:
                out.append((u - 1, None))
    return out + [(UNITS - 1, None)]


def taken_from(i):
    steps = len(unit_steps())
    u, k = divmod(i, steps)
    if k == half_ends()[0] + LAG and u < UNITS:
        return 2 * u
    if k == LAG - 1 and u:
        return 2 * u - 1
    return None


def half_ends():
    steps = len(unit_steps())
    return [steps // 3 - 1, steps - 1]


def spread_stream():
    stream, steps = maxima_stream(), unit_steps()
    width, per_unit = sum(w for *_, w in steps), len(stream) / UNITS
    turns, spread, at = [], [], 0
    for i in range(-1, UNITS * len(steps)):
        u, k = divmod(i + 1, len(steps))
        goal = min(len(stream), int(per_unit * (LEAD + u + sum(w for *_, w in steps[:k]) / width)))
        n = goal - at
        places = []
        for place in range(4 if i >= 0 else 1):
            first = len(turns)
            cut = (at + place * n // 4, at + (place + 1) * n // 4) if i >= 0 else (at, goal)
            if place == 3 and i > 0 and taken_from(i - 1) is not None:
                turns.append((OUTPUT, taken_from(i - 1)))
            turns += stream[cut[0]:cut[1]]
            places.append(range(first, len(turns)))
        spread.append(places)
        at = goal
    turns.append((OUTPUT, 2 * UNITS - 1))
    return turns, spread


def attention(nc, ctx, dram, keep, slots):
    def sb(name, shape, dt=F32):
        return ctx.enter_context(nc.sbuf_tensor(name, shape, dt))

    for r in range(1, RING):
        keep.q_stack.append(sb(f"b_q_stack{r}", [SROWS, G, T], BF16))
        keep.k_stack.append(sb(f"b_k_stack{r}", [SROWS, G, T], BF16))
    q_stack, k_stack = keep.q_stack, keep.k_stack
    ones_row = sb("b_ones_row", [PARTS, T], BF16)
    ident_b = sb("b_ident_b", [P, P], BF16)
    maskneg = sb("b_maskneg", [P, P], BF16)
    probs = sb("b_probs", [P, 3, G, HALFQ])
    mx = sb("b_mx", [P, 2, 2, G * NT])
    top = sb("b_top", [P, 2, G * NT])
    max_parts = sb("b_max_parts", [P, PARTS, G * NT], BF16)
    max_rows = sb("b_max_rows", [PARTS * G * NT, P], BF16)
    o_sb = sb("b_o_sb", [P, 2, HALFQ])
    rz = sb("b_rz", [P, HALFQ // P, G])
    ps_sm = ctx.enter_context(nc.psum_tensor("b_ps_sm", [P, 4 + SPARE, HALFQ], F32))
    ps_s = ps_sm[:, 0:4, :].rearrange("p (a b) q -> p a b q", a=2)
    ps_o = ctx.enter_context(nc.psum_tensor("b_ps_o", [P, HALFQ], F32))
    s = semaphores(nc, ctx, "attend", "ones masks ones0 ones1 ones2 stack0 stack1 stack2 max_in0 max_in1 max_in2 ps_zero scores exp mask pv "
             "cand reduced mx_chain top max_ready w2_zero loaded o_sb chain_v")
    stacked = [s["stack0"], s["stack1"], s["stack2"]]
    ones_in = [s["ones0"], s["ones1"], s["ones2"]]
    max_in = [s["max_in0"], s["max_in1"], s["max_in2"]]
    steps, tasks = unit_steps(), max_tasks()
    stream, spread = spread_stream()
    NS = len(steps)
    NTASK = len(tasks)
    diag = [kb * P >= hf * HALFQ for hf, kb, _, _ in steps]
    loads = background_loads(dram, keep, slots)
    half_end = half_ends()
    turn_of_rows = {u: at for at, (u, n) in enumerate(stream) if n is None}
    turn_of_output = {n: at for at, (u, n) in enumerate(stream) if u == OUTPUT}
    block = ctx.enter_context(nc.Block())

    before_steps = len(spread[0][0])

    bank_of, bank_before, last_user = [], [], {}
    for at in range(len(stream)):
        bank = at % (4 + SPARE) if at < before_steps else 4 + at % SPARE
        bank_of.append(bank)
        bank_before.append(last_user.get(bank))
        last_user[bank] = at

    def masks_until(i):
        return i // NS * sum(diag) + sum(diag[:i % NS + 1])

    @block.sync
    def _(sp):
        sp.wait_ge(s["ones"], 1)
        for r in range(RING):
            for h in range(G):
                sp.dma_start(k_stack[r][KROWS:SROWS, h, :], ones_row[:, :]).then_inc(ones_in[r], 16)

        def stacks(u):
            if u >= RING:
                sp.wait_ge(s["scores"], 2 * NS * (u - RING + 1))
            load_stacks(sp, keep, u, stacked[u % RING])

        def maxima(u):
            sp.wait_ge(s["reduced"], turn_of_rows[u] + 1)
            for i in range(PARTS):
                n = G * NT
                sp.dma_start(q_stack[u % RING][KROWS + i:KROWS + i + 1, :, :].rearrange("r h (t c) -> r (h t) c", c=P),
                             max_rows[i * n:(i + 1) * n, :]).then_inc(max_in[u % RING], 16)

        for u in range(UNITS):
            if u + 1 < UNITS:
                stacks(u + 1)
            maxima(u)
            for to, src in loads[u::UNITS]:
                if u == 0:
                    sp.wait_ge(s["w2_zero"], 1)
                sp.dma_start(to, src).then_inc(s["loaded"], 16)
        sp.wait_ge(s["loaded"], 16 * len(loads))

    @block.gpsimd
    def _(pool):
        nc.gpsimd.memset(keep.w2[:, :, 1, :], 0.0).then_inc(s["w2_zero"], 1)
        pool.wait_ge(s["w2_zero"], 1)
        nc.gpsimd.memset(maskneg[:, :], 0.0).then_inc(s["mx_chain"], 1)
        pool.wait_ge(s["mx_chain"], 1)
        nc.gpsimd.affine_select(out=maskneg[:, :], in_=maskneg[:, :], compare_op=ALU.is_ge, fill=-1e30, base=0,
                                pattern=[[-1, P]], channel_multiplier=1).then_inc(s["masks"], 1)

        def split_maxima(u):
            pool.wait_ge(s["top"], u + 1)
            if u:
                pool.wait_ge(s["reduced"], turn_of_rows[u - 1] + 1)
            steps_before = 1 + 2 * (PARTS - 1) * u
            left = top[:, u % 2, :]
            for part in range(PARTS - 1):
                nc.gpsimd.tensor_copy(max_parts[:, part, :], left).then_inc(s["mx_chain"], 1)
                pool.wait_ge(s["mx_chain"], steps_before + 2 * part + 1)
                nc.gpsimd.tensor_tensor(left, left, max_parts[:, part, :], ALU.subtract).then_inc(s["mx_chain"], 1)
                pool.wait_ge(s["mx_chain"], steps_before + 2 * part + 2)
            nc.gpsimd.tensor_copy(max_parts[:, PARTS - 1, :], left).then_inc(s["max_ready"], 1)
            pool.wait_ge(s["max_ready"], u + 1)

        for i in range(-1, UNITS * NS):
            for at in (at for place in spread[i + 1] for at in place):
                if stream[at][0] != OUTPUT and stream[at][1] == NTASK - 1:
                    split_maxima(stream[at][0])
            if i < 0 or not diag[i % NS]:
                continue
            pool.wait_ge(s["exp"], 2 * i + 2)
            blk = probs[:, i % 3, :, 0:P]
            nc.gpsimd.affine_select(out=blk, in_=blk, compare_op=ALU.is_ge, fill=0.0, base=0,
                                    pattern=[[0, G], [1, P]], channel_multiplier=-1).then_inc(s["mask"], 1)

    @block.scalar
    def _(act):
        def take_outputs(n):
            act.wait_ge(s["pv"], n // 2 * NS + half_end[n % 2] + 1)
            if n >= 2:
                act.wait_ge(s["cand"], turn_of_output[n - 2] + 1)
            nc.scalar.copy(o_sb[:, n % 2, :], ps_o[:, :]).then_inc(s["o_sb"], 1)

        for i in range(UNITS * NS):
            u, k = divmod(i, NS)
            w = steps[k][3]
            if i >= 3:
                act.wait_ge(s["pv"], i - 2)
            for hp in range(2):
                act.wait_ge(s["scores"], 2 * i + hp + 1)
                nc.scalar.activation(probs[:, i % 3, 2 * hp:2 * hp + 2, 0:w], ps_s[:, hp, :, 0:w], ACT.Exp,
                                     scale=SCALE).then_inc(s["exp"], 1)
            if taken_from(i) is not None:
                take_outputs(taken_from(i))
        take_outputs(2 * UNITS - 1)

    @block.tensor
    def _(pe):
        def maximum_scores(turns):
            for at in turns:
                u, n = stream[at]
                r = u % RING
                bank = bank_of[at]
                if bank_before[at] is not None:
                    pe.wait_ge(s["reduced"], bank_before[at] + 1)
                if u == OUTPUT:
                    pe.wait_ge(s["o_sb"], n + 1)
                    for t in range(HALFQ // P):
                        mm = nc.tensor.transpose(ps_sm[:, bank, t * P:(t + 1) * P], o_sb[:, n % 2, t * P:(t + 1) * P], keep.ident[:, :])
                    mm.then_inc(s["cand"], 1)
                    continue
                if n is None:
                    pe.wait_ge(s["max_ready"], u + 1)
                    nc.tensor.transpose(ps_sm[0:PARTS * G * NT, bank_of[at], 0:P // 2].bitcast(BF16),
                                        max_parts[:, :, :].rearrange("p i n -> p (i n)"), ident_b[:, :]).then_inc(s["cand"], 1)
                    continue
                if n == 0 and u:
                    loads_here = (u + RING - 1) // RING if r == 0 else u // RING + 1
                    pe.wait_ge(stacked[r], 16 * STACK_DMAS * loads_here)
                j, qt, c, keys = tasks[n]
                out = ps_sm[:, bank, 0:keys]
                on_diagonal = c + keys == (qt + 1) * P
                mm = nc.tensor.matmul(out, q_stack[r][0:KROWS, j, qt * P:(qt + 1) * P],
                                      k_stack[r][0:KROWS, j, c:c + keys], start=True, stop=not on_diagonal,
                                      skip_group_check=True)
                if on_diagonal:
                    mm = nc.tensor.matmul(out[:, keys - P:keys], ident_b[:, :], maskneg[:, :], start=False, stop=True,
                                          skip_group_check=True)
                mm.then_inc(s["cand"], 1)

        def weighted_values(i):
            u, k = divmod(i, NS)
            hf, kb, lo, w = steps[k]
            b, g = u // G, u % G
            pe.wait_ge(s["exp"], 2 * i + 2)
            if diag[k]:
                pe.wait_ge(s["mask"], masks_until(i))
            if kb == 0:
                pe.wait_ge(s["ps_zero"], 1)
                if 2 * u + hf:
                    pe.wait_ge(s["o_sb"], 2 * u + hf)
            for j in range(G):
                mm = nc.tensor.matmul(ps_o[32 * j:32 * j + HD + 1, lo - hf * HALFQ:HALFQ],
                                      keep.v[:, b * NT + kb, g * G + j, :], probs[:, i % 3, j, 0:w],
                                      start=(kb == 0), stop=(k in half_end), skip_group_check=True)
            mm.then_inc(s["pv"], 1)

        pe.wait_ge(s["masks"], 2)
        maximum_scores(spread[0][0])
        pe.wait_ge(s["reduced"], before_steps)
        for i in range(UNITS * NS):
            u, k = divmod(i, NS)
            hf, kb, lo, w = steps[k]
            r = u % RING
            if k == 0:
                if u < RING:
                    pe.wait_ge(ones_in[r], 16 * G)
                pe.wait_ge(max_in[r], 16 * PARTS * (u // RING + 1))
            cut = spread[i + 1]
            for hp in range(2):
                if i:
                    pe.wait_ge(s["exp"], 2 * i + hp - 1)
                for jj in range(2):
                    j = 2 * hp + jj
                    mm = nc.tensor.matmul(ps_s[:, hp, jj, 0:w], k_stack[r][0:SROWS, j, kb * P:(kb + 1) * P],
                                          q_stack[r][0:SROWS, j, lo:lo + w], start=True, stop=True)
                mm.then_inc(s["scores"], 1)
                maximum_scores(cut[hp])
            if i >= LAG:
                weighted_values(i - LAG)
            maximum_scores(cut[2])
            maximum_scores(cut[3])
        for i in range(UNITS * NS - LAG, UNITS * NS):
            weighted_values(i)
        maximum_scores([len(stream) - 1])

    @block.vector
    def _(dve):
        link = chained(dve, s["chain_v"])
        nc.vector.memset(ones_row[:, :], -1.0).then_inc(s["ones"], 1)
        nc.vector.memset(mx[:, :, :, :], -1e30)
        nc.vector.memset(ps_o[:, :], 0.0).then_inc(s["ps_zero"], 1)
        nc.vector.tensor_copy(ident_b[:, :], keep.ident[:, :]).then_inc(s["masks"], 1)

        def normalize(n, at):
            u, hf = divmod(n, 2)
            b, g = divmod(u, G)
            if n:
                dve.wait_ge(s["reduced"], turn_of_output[n - 1] + 1)
            o = ps_sm[:, bank_of[at], :].rearrange("p (t j c) -> p t j c", t=HALFQ // P, j=G)
            link(nc.vector.reciprocal(rz[:, :, :], o[:, :, :, HD]))
            first = b * NT + hf * HALFQ // P
            out = keep.attn[:, first:first + HALFQ // P, g * G * HD:(g + 1) * G * HD]
            nc.vector.tensor_tensor(out.rearrange("p t (j d) -> p t j d", j=G), o[:, :, :, 0:HD],
                                    rz[:, :, :].unsqueeze(3).to_broadcast([P, HALFQ // P, G, HD]), ALU.mult).then_inc(s["reduced"], 1)

        def reduce(turns):
            for at in turns:
                u, n = stream[at]
                dve.wait_ge(s["cand"], at + 1)
                if u == OUTPUT:
                    normalize(n, at)
                    continue
                if n is None:
                    if u:
                        before = u - 1
                        dve.wait_ge(max_in[before % RING], 16 * PARTS * (before // RING + 1))
                    nc.vector.tensor_copy(max_rows[:, :], ps_sm[0:PARTS * G * NT, bank_of[at], 0:P // 2].bitcast(BF16)).then_inc(s["reduced"], 1)
                    continue
                j, qt, c, keys = tasks[n]
                nc.vector.tensor_reduce(mx[:, u % 2, c // HALFQ, j * NT + qt:j * NT + qt + 1], ps_sm[:, bank_of[at], 0:keys],
                                        AX_X, ALU.max).then_inc(s["reduced"], 1)
                if n == NTASK - 1:
                    dve.wait_ge(s["reduced"], at + 1)
                    if u >= 2:
                        dve.wait_ge(s["max_ready"], u - 1)
                    nc.vector.tensor_tensor(top[:, u % 2, :], mx[:, u % 2, 0, :], mx[:, u % 2, 1, :], ALU.max).then_inc(s["top"], 1)

        reduce(spread[0][0])
        for i in range(UNITS * NS):
            for place in spread[i + 1]:
                reduce(place)
        reduce([len(stream) - 1])


LEVELS = T.bit_length() - 1
GROUP = 4


class Stats:

    def __init__(self, nc, ctx, keep, tag):
        self.keep = keep
        self.s = semaphores(nc, ctx, tag + "stats", "bn mv std rstd")

    def vector_mean(self, dve, b):
        for t in range(b * NT, (b + 1) * NT):
            last = dve.bn_stats(self.keep.stats[:, t, :], self.keep.x[:, t, :])
        last.then_inc(self.s["bn"], 1)
        dve.wait_ge(self.s["bn"], b + 1)
        for t in range(b * NT, (b + 1) * NT):
            last = dve.bn_aggr(self.keep.mv[:, t, :], self.keep.stats[:, t, :])
        last.then_inc(self.s["mv"], 1)

    def scalar_std(self, act, b):
        at = slice(b * NT, (b + 1) * NT)
        act.wait_ge(self.s["mv"], b + 1)
        act.activation(self.keep.std[:, at], self.keep.mv[:, at, 1], ACT.Sqrt, bias=self.keep.eps[:, 0:1]).then_inc(self.s["std"], 1)

    def vector_rstd(self, dve, b):
        dve.wait_ge(self.s["std"], b + 1)
        at = slice(b * NT, (b + 1) * NT)
        dve.reciprocal(self.keep.rstd[:, at], self.keep.std[:, at]).then_inc(self.s["rstd"], 1)
        dve.wait_ge(self.s["rstd"], b + 1)
        dve.scalar_tensor_tensor(out=self.keep.shift[:, at], in0=self.keep.mv[:, at, 0], scalar=-1.0, in1=self.keep.rstd[:, at],
                                 op0=ALU.mult, op1=ALU.mult)


def project_out(nc, ctx, dram, keep):
    def sb(name, shape, dt=F32):
        return ctx.enter_context(nc.sbuf_tensor(name, shape, dt))

    w_o = sb("c_w_o", [P, D])
    attnT = sb("c_attnT", [P, 2, GROUP * P])
    a_pow = sb("c_a_pow", [P, 2, P])
    ps_t = ctx.enter_context(nc.psum_tensor("c_ps_t", [P, 2, GROUP * P], F32))
    ps_y = ctx.enter_context(nc.psum_tensor("c_ps_y", [P, 2, GROUP * P], F32))
    ps_a = ctx.enter_context(nc.psum_tensor("c_ps_a", [P, 512], F32))
    s = semaphores(nc, ctx, "out", "w_o turned copied projected added squared power")
    groups = TILES // GROUP
    stats = Stats(nc, ctx, keep, "c_")
    block = ctx.enter_context(nc.Block())

    @block.sync
    def _(sp):
        sp.dma_start(w_o[:, :], dram["w_o"]).then_inc(s["w_o"], 16)

    @block.tensor
    def _(pe):
        def square(level):
            pe.wait_ge(s["power"], level)
            natural = a_pow[:, level % 2, :]
            nc.tensor.matmul(ps_a[:, 0:P], natural, keep.a_powT[:, level - 1, :], start=True, stop=True)
            nc.tensor.matmul(ps_a[:, P:2 * P], keep.a_powT[:, level - 1, :], natural, start=True, stop=True).then_inc(s["squared"], 1)

        pe.wait_ge(s["w_o"], 16)
        level = 1
        for g in range(groups + 1):
            if g < groups:
                if g >= 2:
                    pe.wait_ge(s["copied"], g - 1)
                for t in range(GROUP):
                    mm = nc.tensor.transpose(ps_t[:, g % 2, t * P:(t + 1) * P], keep.attn[:, g * GROUP + t, :], keep.ident[:, :])
                mm.then_inc(s["turned"], 1)
            if g:
                pe.wait_ge(s["copied"], g)
                if g >= 3:
                    pe.wait_ge(s["added"], g - 2)
                for t in range(GROUP):
                    mm = nc.tensor.matmul(ps_y[:, (g - 1) % 2, t * P:(t + 1) * P],
                                          attnT[:, (g - 1) % 2, t * P:(t + 1) * P], w_o[:, :], start=True, stop=True)
                mm.then_inc(s["projected"], 1)
            square(level)
            level += 1
        while level < LEVELS:
            square(level)
            level += 1

    @block.scalar
    def _(act):
        for g in range(groups):
            act.wait_ge(s["turned"], g + 1)
            if g >= 2:
                act.wait_ge(s["projected"], g - 1)
            nc.scalar.copy(attnT[:, g % 2, :], ps_t[:, g % 2, :]).then_inc(s["copied"], 1)
        for b in range(B):
            stats.scalar_std(nc.scalar, b)

    @block.vector
    def _(dve):
        nc.vector.tensor_copy(a_pow[:, 1, :], keep.a_nat[:, :])
        nc.vector.tensor_copy(keep.a_powT[:, 0, :], keep.a_T[:, :]).then_inc(s["power"], 1)
        level = 1

        def take_power(level):
            dve.wait_ge(s["squared"], level)
            nc.vector.tensor_copy(keep.a_powT[:, level, :], ps_a[:, 0:P])
            nc.vector.tensor_copy(a_pow[:, (level + 1) % 2, :], ps_a[:, P:2 * P]).then_inc(s["power"], 1)

        for g in range(groups + 1):
            if g:
                dve.wait_ge(s["projected"], g)
                xs = keep.x[:, (g - 1) * GROUP:g * GROUP, :]
                last = nc.vector.tensor_tensor(xs, ps_y[:, (g - 1) % 2, :].rearrange("p (t d) -> p t d", t=GROUP), xs, ALU.add)
                last.then_inc(s["added"], 1)
            take_power(level)
            level += 1
            if g and g % 2 == 0:
                dve.wait_ge(s["added"], g)
                stats.vector_mean(nc.vector, g // 2 - 1)
        while level < LEVELS:
            take_power(level)
            level += 1
        for b in range(B):
            stats.vector_rstd(nc.vector, b)


class Norm:

    def __init__(self, nc, ctx, keep, tag, out, outT, by_vector):
        self.nc, self.keep, self.out, self.outT, self.by_vector = nc, keep, out, outT, by_vector
        self.s = semaphores(nc, ctx, tag + "norm", "xn_v xn_s turned xnT")

    def vector_scale(self, dve, b):
        for t in range(b * NT, b * NT + self.by_vector[b]):
            dve.tensor_scalar(self.out[:, t, 0:D], self.keep.x[:, t, :], self.keep.mv[:, t, 0:1],
                              self.keep.rstd[:, t:t + 1], ALU.subtract, ALU.mult).then_inc(self.s["xn_v"], 1)

    def scalar_scale(self, act, b):
        for t in range(b * NT + self.by_vector[b], (b + 1) * NT):
            act.activation(self.out[:, t, 0:D], self.keep.x[:, t, :], ACT.Identity, bias=self.keep.shift[:, t:t + 1],
                           scale=self.keep.rstd[:, t:t + 1]).then_inc(self.s["xn_s"], 1)

    def wait_xn(self, engine, b):
        of_vector = sum(self.by_vector[:b + 1])
        if of_vector:
            engine.wait_ge(self.s["xn_v"], of_vector)
        engine.wait_ge(self.s["xn_s"], (b + 1) * NT - of_vector)

    def tensor_turn(self, pe, bank, b):
        self.wait_xn(pe, b)
        if b >= 2:
            pe.wait_ge(self.s["xnT"], b - 1)
        for t in range(NT):
            mm = pe.transpose(bank[:, t * P:(t + 1) * P], self.out[:, b * NT + t, 0:D], self.keep.ident[:, :])
        mm.then_inc(self.s["turned"], 1)

    def scalar_copy(self, act, bank, b):
        act.wait_ge(self.s["turned"], b + 1)
        act.copy(self.outT[:, b * T:(b + 1) * T], bank[:, :]).then_inc(self.s["xnT"], 1)


PACE = 5


def route_and_share(nc, ctx, dram, keep, tag, slots_dram):
    def sb(name, shape, dt=F32):
        return ctx.enter_context(nc.sbuf_tensor(tag + name, shape, dt))

    QUADS = B * T // HALFQ
    CH = [min(P, SF - c * P) for c in range(3)]
    logits = sb("logits", [P, NT, E])
    scores = sb("scores", [P, NT, E])
    top = sb("top", [P, NT])
    total = sb("total", [P, NT])
    best = sb("best", [P, NT, 8])
    where = sb("where", [P, NT, 8], U32)
    where_f = sb("where_f", [P, TOPK, NT])
    chosen = sb("chosen", [P, TOPK, NT, E])
    either = sb("either", [P, NT, E])
    tile_sum = sb("tile_sum", [P, NT, E])
    run = [sb(f"run{i}", [P, NT, E]) for i in range(2)]
    place = sb("place", [P, NT, E])
    slot_f = sb("slot_f", [P, TOPK, NT])
    taken = [sb(f"taken{i}", [P, E]) for i in range(2)]
    taken_i = sb("taken_i", [P, E], I32)
    whole = sb("whole", [P, E])
    whole_i = sb("whole_i", [P, E], I32)
    end = [sb(f"end{i}", [P, E]) for i in range(2)]
    passed = sb("passed", [P, SLOT_TILES, E])
    expert_f = sb("expert_f", [P, SLOT_TILES])
    first_f = sb("first_f", [P, SLOT_TILES])
    sil = sb("sil", [P, 2, 3, HALFQ])
    up = sb("up", [P, 2, 3, HALFQ])
    ps = ctx.enter_context(nc.psum_tensor(tag + "ps", [P, 8, 512], F32))
    ps_gate, ps_before, ps_sum = (ps[:, 7, i * NT * E:(i + 1) * NT * E] for i in range(3))
    norm = Norm(nc, ctx, keep, tag, keep.rows[:, 0], keep.xnT, [HT] + [0] * (B - 1))
    s = semaphores(nc, ctx, tag + "route", "gate less exp either counts counted slots rows ends padded scattered hidden sil up out added chain")
    block = ctx.enter_context(nc.Block())

    def split(x):
        return x.rearrange("p (t e) -> p t e", e=E)

    def pad(engine, of):
        engine.wait_ge(s["ends"], 1)
        for e in of:
            at = engine.value_load(taken_i[0:1, e:e + 1], min_val=e * REGION * ROW, max_val=(e * REGION + B * T) * ROW)
            engine.dma_start(slots_dram.rearrange("n c -> (n c)")[bass.ds(at, P * ROW)],
                             dram["slot_rows"][e * P:(e + 1) * P, :].rearrange("n c -> (n c)")).then_inc(s["padded"], 16)

    @block.sync
    def _(sp):
        pad(sp, [e for e in range(E) if e % 4])
        sp.wait_ge(s["padded"], 16 * E)
        sp.wait_ge(s["scattered"], 16 * TOPK * TILES)

    @block.gpsimd
    def _(pool):
        for b in range(B):
            pool.wait_ge(s["slots"], b + 1)
            pool.wait_ge(s["rows"], b + 1)
            for t in range(b * NT, (b + 1) * NT):
                for k in range(TOPK):
                    nc.gpsimd.indirect_dma_start(out=slots_dram, out_offset=bass.IndirectOffsetOnAxis(ap=keep.slot[:, k, t:t + 1], axis=0),
                                                 in_=keep.rows[:, k, t, :], in_offset=None).then_inc(s["scattered"], 16)

    @block.tensor
    def _(pe):
        def turn(b):
            norm.wait_xn(pe, b)
            for h in (2 * b, 2 * b + 1):
                if h >= 2:
                    pe.wait_ge(norm.s["xnT"], h - 1)
                for t in range(GROUP):
                    mm = nc.tensor.transpose(ps[:, h % 2, t * P:(t + 1) * P], keep.rows[:, 0, h * GROUP + t, 0:D], keep.ident[:, :])
                mm.then_inc(norm.s["turned"], 1)

        def gate(b):
            pe.wait_ge(norm.s["xnT"], 2 * b + 2)
            if b:
                pe.wait_ge(s["counted"], b)
            for t in range(NT):
                at = (b * NT + t) * P
                mm = nc.tensor.matmul(ps_gate[:, t * E:(t + 1) * E], keep.xnT[:, at:at + P], keep.gate_w[:, :], start=True, stop=True)
            mm.then_inc(s["gate"], 1)

        def counts(b):
            pe.wait_ge(s["either"], b + 1)
            flat = either[:, :, :].rearrange("p t e -> p (t e)")
            nc.tensor.matmul(ps_before, keep.before[:, :], flat, start=True, stop=True)
            nc.tensor.matmul(ps_sum, keep.ones[:, :], flat, start=True, stop=True).then_inc(s["counts"], 1)

        def shared_up(n):
            q, c = divmod(n, 3)
            if n >= 2:
                pe.wait_ge(s["up"], n - 1)
            for which, w in enumerate((keep.sw1, keep.sw3)):
                mm = nc.tensor.matmul(ps[0:CH[c], 2 + 2 * (n % 2) + which, :], w[:, c * P:c * P + CH[c]],
                                      keep.xnT[:, q * HALFQ:(q + 1) * HALFQ], start=True, stop=True)
            mm.then_inc(s["hidden"], 1)

        def shared_down(q):
            pe.wait_ge(s["up"], 3 * q + 3)
            if q:
                pe.wait_ge(s["added"], q)
            for t in range(GROUP):
                for c in range(3):
                    rows = CH[c] + (c == 2)
                    mm = nc.tensor.matmul(ps[:, 6, t * P:(t + 1) * P], up[0:rows, q % 2, c, t * P:(t + 1) * P],
                                          keep.sw2[0:rows, c, :], start=(c == 0), stop=(c == 2))
            mm.then_inc(s["out"], 1)

        def chunk(n):
            shared_up(n)
            if n >= 3 and n % 3 == 0:
                shared_down(n // 3 - 1)

        turn(0)
        gate(0)
        for b in range(B):
            n = PACE * b
            chunk(n)
            chunk(n + 1)
            chunk(n + 2)
            counts(b)
            if b + 1 < B:
                turn(b + 1)
            chunk(n + 3)
            if b + 1 < B:
                gate(b + 1)
            chunk(n + 4)
        for n in range(PACE * B, 3 * QUADS):
            chunk(n)
        shared_down(QUADS - 1)

    @block.scalar
    def _(act):
        def take(b):
            for h in (2 * b, 2 * b + 1):
                act.wait_ge(norm.s["turned"], h + 1)
                nc.scalar.copy(keep.xnT[:, h * HALFQ:(h + 1) * HALFQ], ps[:, h % 2, :]).then_inc(norm.s["xnT"], 1)

        def second_rows(b):
            at = slice(b * NT, (b + 1) * NT)
            norm.wait_xn(act, b)
            nc.scalar.copy(keep.rows[:, 1, at, 0:D], keep.rows[:, 0, at, 0:D]).then_inc(s["rows"], 1)

        def silu(n):
            q, c = divmod(n, 3)
            act.wait_ge(s["hidden"], n + 1)
            if q >= 2:
                act.wait_ge(s["up"], n - 5)
            nc.scalar.activation(sil[0:CH[c], q % 2, c, :], ps[0:CH[c], 2 + 2 * (n % 2), :], ACT.Silu,
                                 bias=keep.sbias[0:CH[c], 0, c:c + 1]).then_inc(s["sil"], 1)

        norm.scalar_scale(nc.scalar, 0)
        take(0)
        second_rows(0)
        for b in range(B):
            act.wait_ge(s["less"], b + 1)
            nc.scalar.activation(scores[:, :, :], logits[:, :, :], ACT.Exp).then_inc(s["exp"], 1)
            silu(PACE * b)
            if b + 1 < B:
                norm.scalar_scale(nc.scalar, b + 1)
            silu(PACE * b + 1)
            silu(PACE * b + 2)
            if b + 1 < B:
                take(b + 1)
            silu(PACE * b + 3)
            if b + 1 < B:
                second_rows(b + 1)
            silu(PACE * b + 4)
        pad(act, range(0, E, 4))
        for n in range(PACE * B, 3 * QUADS):
            silu(n)

    @block.vector
    def _(dve):
        link = chained(dve, s["chain"])
        v = nc.vector

        def shared_mid(n):
            q, c = divmod(n, 3)
            dve.wait_ge(s["sil"], n + 1)
            if q >= 2 and c == 0:
                dve.wait_ge(s["out"], q - 1)
            v.scalar_tensor_tensor(out=up[0:CH[c], q % 2, c, :], in0=ps[0:CH[c], 3 + 2 * (n % 2), :],
                                   scalar=keep.sbias[0:CH[c], 1, c:c + 1], in1=sil[0:CH[c], q % 2, c, :],
                                   op0=ALU.add, op1=ALU.mult).then_inc(s["up"], 1)

        def shared_add(q):
            dve.wait_ge(s["out"], q + 1)
            xq = keep.x[:, q * GROUP:(q + 1) * GROUP, :]
            v.tensor_tensor(xq, ps[:, 6, :].rearrange("p (t d) -> p t d", t=GROUP), xq, ALU.add).then_inc(s["added"], 1)

        def chunk(n):
            shared_mid(n)
            if n >= 4 and n % 3 == 1:
                shared_add(n // 3 - 1)

        norm.vector_scale(v, 0)
        for h in range(2):
            v.memset(up[SF - 2 * P:SF - 2 * P + 1, h, 2, :], 1.0)
        v.tensor_copy(keep.rows[:, :, :, D].bitcast(I32), keep.token_id[:, :, :].bitcast(I32))
        v.tensor_copy(taken[0][:, :], keep.region[:, :])
        numbers = keep.expert_no[:, :].unsqueeze(1).unsqueeze(1).to_broadcast([P, TOPK, NT, E])
        for b in range(B):
            at, n = slice(b * NT, (b + 1) * NT), PACE * b
            dve.wait_ge(s["gate"], b + 1)
            link(v.tensor_tensor(logits[:, :, :], split(ps_gate), keep.gate_b[:, :].unsqueeze(1).to_broadcast([P, NT, E]), ALU.add))
            link(v.tensor_reduce(top[:, :], logits[:, :, :], AX_X, ALU.max))
            v.tensor_tensor(logits[:, :, :], logits[:, :, :], top[:, :].unsqueeze(2).to_broadcast([P, NT, E]),
                            ALU.subtract).then_inc(s["less"], 1)
            if b:
                chunk(n - 1)
            dve.wait_ge(s["exp"], b + 1)
            link(v.tensor_reduce(total[:, :], scores[:, :, :], AX_X, ALU.add))
            link(v.reciprocal(total[:, :], total[:, :]))
            link(v.tensor_tensor(scores[:, :, :], scores[:, :, :], total[:, :].unsqueeze(2).to_broadcast([P, NT, E]), ALU.mult))
            for t in range(NT):
                last = v.max(best[:, t, :], scores[:, t, :])
            link(last)
            chunk(n)
            for t in range(NT):
                last = v.max_index(where[:, t, :], best[:, t, :], scores[:, t, :])
            link(last)
            v.tensor_copy(keep.rows[:, :, at, D + 1], best[:, :, 0:TOPK].rearrange("p t k -> p k t"))
            link(v.tensor_copy(where_f[:, :, :], where[:, :, 0:TOPK].rearrange("p t k -> p k t")))
            link(v.tensor_tensor(chosen[:, :, :, :], where_f[:, :, :].unsqueeze(3).to_broadcast([P, TOPK, NT, E]), numbers, ALU.is_equal))
            v.tensor_tensor(either[:, :, :], chosen[:, 0], chosen[:, 1], ALU.add).then_inc(s["either"], 1)
            chunk(n + 1)
            dve.wait_ge(s["counts"], b + 1)
            v.tensor_tensor(place[:, :, :], split(ps_before), taken[b % 2][:, :].unsqueeze(1).to_broadcast([P, NT, E]), ALU.add)
            last = v.tensor_copy(tile_sum[:, :, :], split(ps_sum))
            last.then_inc(s["counted"], 1)
            dve.wait_ge(s["counted"], b + 1)
            src, step, i = tile_sum, 1, 0
            while step < NT:
                v.tensor_copy(run[i][:, 0:step, :], src[:, 0:step, :])
                link(v.tensor_tensor(run[i][:, step:, :], src[:, step:, :], src[:, 0:NT - step, :], ALU.add))
                src, step, i = run[i], 2 * step, 1 - i
            chunk(n + 2)
            v.tensor_tensor(taken[1 - b % 2][:, :], taken[b % 2][:, :], src[:, NT - 1, :], ALU.add)
            link(v.tensor_tensor(place[:, 1:, :], place[:, 1:, :], src[:, 0:NT - 1, :], ALU.add))
            link(v.tensor_tensor(chosen[:, :, :, :], chosen[:, :, :, :], place[:, :, :].unsqueeze(1).to_broadcast([P, TOPK, NT, E]), ALU.mult))
            link(v.tensor_reduce(slot_f[:, :, :], chosen[:, :, :, :], AX_X, ALU.add))
            v.tensor_copy(keep.slot[:, :, at], slot_f[:, :, :]).then_inc(s["slots"], 1)
            if b + 1 == B:
                last_taken = taken[B % 2]
                link(v.tensor_scalar(end[1][:, :], last_taken[:, :], float(ROW), None, ALU.mult))
                v.tensor_copy(taken_i[:, :], end[1][:, :]).then_inc(s["ends"], 1)
            chunk(n + 3)
            if b + 1 == B:
                chunk(n + 4)
                link(v.tensor_tensor(whole[:, :], last_taken[:, :], keep.region[:, :], ALU.subtract))
                link(v.tensor_scalar(whole[:, :], whole[:, :], float(P - 1), None, ALU.add))
                link(v.tensor_copy(whole_i[:, :], whole[:, :]))
                link(v.tensor_scalar(whole_i[:, :], whole_i[:, :], P.bit_length() - 1, None, ALU.arith_shift_right))
                link(v.tensor_copy(whole[:, :], whole_i[:, :]))
                src, step, i = whole, 1, 0
                while step < E:
                    v.tensor_copy(end[i][:, 0:step], src[:, 0:step])
                    link(v.tensor_tensor(end[i][:, step:], src[:, step:], src[:, 0:E - step], ALU.add))
                    src, step, i = end[i], 2 * step, 1 - i
                link(v.tensor_tensor(passed[:, :, :], keep.tile_no[:, :].unsqueeze(2).to_broadcast([P, SLOT_TILES, E]),
                                     src[:, :].unsqueeze(1).to_broadcast([P, SLOT_TILES, E]), ALU.is_ge))
                chunk(PACE * B)
                link(v.tensor_reduce(expert_f[:, :], passed[:, :, :], AX_X, ALU.add))
                chunk(PACE * B + 1)
                link(v.tensor_tensor(passed[:, :, :], passed[:, :, :], whole[:, :].unsqueeze(1).to_broadcast([P, SLOT_TILES, E]), ALU.mult))
                link(v.tensor_reduce(first_f[:, :], passed[:, :, :], AX_X, ALU.add))
                link(v.tensor_tensor(first_f[:, :], keep.tile_no[:, :], first_f[:, :], ALU.subtract))
                link(v.scalar_tensor_tensor(out=first_f[:, :], in0=expert_f[:, :], scalar=float(REGION // P), in1=first_f[:, :],
                                            op0=ALU.mult, op1=ALU.add))
                link(v.tensor_scalar(first_f[:, :], first_f[:, :], float(P), None, ALU.mult))
                link(v.tensor_scalar(expert_f[:, :], expert_f[:, :], float(E - 1), None, ALU.min))
                v.tensor_copy(keep.source[:, :], first_f[:, :])
                v.tensor_copy(keep.expert[:, :], expert_f[:, :])
        for n in range(PACE * B + 2, 3 * QUADS):
            chunk(n)
        shared_add(QUADS - 1)


XS_RING = 12
Y_RING = 4


def experts(nc, ctx, dram, keep, tag, slots_dram, parted_dram, out):
    def sb(name, shape, dt=F32):
        return ctx.enter_context(nc.sbuf_tensor(tag + name, shape, dt))

    xs = sb("xs", [P, XS_RING, ROW])
    xsT = sb("xsT", [P, 3, P])
    hg = sb("hg", [P, 2, 2 * F])
    act_h = sb("act_h", [P, 2, F])
    a = sb("a", [P, 2, 2 * P])
    aT = sb("aT", [P, 2, 2 * P])
    y = sb("y", [P, Y_RING, D])
    back = sb("back", [P, B, NT, TOPK * D])
    ps = ctx.enter_context(nc.psum_tensor(tag + "ps", [P, 8, 512], F32))
    s = semaphores(nc, ctx, tag + "expert", "chain xs0 xs1 xs2 xs3 xs4 xs5 xs6 xs7 xs8 xs9 xs10 xs11 xT_ps xT h hg act_h a aT_ps aT "
             "y_ps y sent0 sent1 sent2 sent3 back0 back1 back2 back3 summed combined")
    xs_in = [s[f"xs{r}"] for r in range(XS_RING)]
    sent = [s["sent0"], s["sent1"], s["sent2"], s["sent3"]]
    back_in = [s[f"back{b}"] for b in range(B)]
    N = SLOT_TILES
    stats = Stats(nc, ctx, keep, tag) if out is None else None
    block = ctx.enter_context(nc.Block())

    @block.sync
    def _(sp):
        def store(b):
            if out is not None:
                sp.dma_start(out[b].rearrange("(t p) d -> p t d", p=P), keep.x[:, b * NT:(b + 1) * NT, :]).then_inc(keep.stored, 16)

        first = sp.value_load(keep.source[0:1, 0:1], min_val=0, max_val=SLOTS - P)
        for i in range(N):
            r = i % XS_RING
            if i >= XS_RING:
                j = i - XS_RING
                sp.wait_ge(sent[j % Y_RING], 16 * (j // Y_RING + 1))
            sp.dma_start(xs[:, r, :], slots_dram[bass.ds(first, P), :]).then_inc(xs_in[r], 16)
            if i + 1 < N:
                first = sp.value_load(keep.source[0:1, i + 1:i + 2], min_val=0, max_val=SLOTS - P)
        for j in range(Y_RING):
            sp.wait_ge(sent[j], 16 * (N // Y_RING))
        for b in range(B):
            src = parted_dram[b * T * TOPK:(b + 1) * T * TOPK, :].rearrange("(t p k) d -> p t (k d)", p=P, k=TOPK)
            sp.dma_start(back[:, b, :, :], src).then_inc(back_in[b], 16)
        for b in range(B):
            sp.wait_ge(s["combined"], b + 1)
            store(b)
        if out is not None:
            sp.wait_ge(keep.stored, 16 * B)

    @block.gpsimd
    def _(pool):
        for i in range(N):
            pool.wait_ge(s["y"], i + 1)
            where = xs[:, i % XS_RING, D:D + 1].bitcast(I32)
            nc.gpsimd.indirect_dma_start(out=parted_dram, out_offset=bass.IndirectOffsetOnAxis(ap=where, axis=0),
                                         in_=y[:, i % Y_RING, :], in_offset=None).then_inc(sent[i % Y_RING], 16)
        for b in range(B):
            pool.wait_ge(back_in[b], 16)
            nc.gpsimd.tensor_tensor(back[:, b, :, 0:D], back[:, b, :, 0:D], back[:, b, :, D:2 * D], ALU.add).then_inc(s["summed"], 1)

    @block.tensor
    def _(pe):
        which = {0: nc.tensor.value_load(keep.expert[0:1, 0:1], min_val=0, max_val=E - 1)}
        for i in range(N + 5):
            if i < N:
                pe.wait_ge(xs_in[i % XS_RING], 16 * (i // XS_RING + 1))
                if i >= 2:
                    pe.wait_ge(s["xT"], i - 1)
                nc.tensor.transpose(ps[:, i % 2, 0:P], xs[:, i % XS_RING, 0:D], keep.ident[:, :]).then_inc(s["xT_ps"], 1)
            if 2 <= i < N + 2:
                j = i - 2
                e = which[j]
                pe.wait_ge(s["xT"], j + 1)
                if j >= 2:
                    pe.wait_ge(s["hg"], j - 1)
                w = keep.w13[:, :, :, :].rearrange("p e i f -> p (e i f)")[:, bass.ds(e * (2 * F), 2 * F)]
                nc.tensor.matmul(ps[:, 2 + j % 2, 0:2 * F], xsT[:, j % 3, :], w, start=True, stop=True).then_inc(s["h"], 1)
                if j + 1 < N:
                    which[j + 1] = nc.tensor.value_load(keep.expert[0:1, j + 1:j + 2], min_val=0, max_val=E - 1)
            if 4 <= i < N + 4:
                j = i - 4
                pe.wait_ge(s["a"], j + 1)
                if j >= 2:
                    pe.wait_ge(s["aT"], j - 1)
                for c in range(2):
                    mm = nc.tensor.transpose(ps[:, 4 + j % 2, c * P:(c + 1) * P], a[:, j % 2, c * P:(c + 1) * P], keep.ident[:, :])
                mm.then_inc(s["aT_ps"], 1)
            if 5 <= i:
                j = i - 5
                e = which.pop(j)
                pe.wait_ge(s["aT"], j + 1)
                if j >= 2:
                    pe.wait_ge(s["y"], j - 1)
                for c in range(2):
                    w = keep.w2[:, :, :, :].rearrange("p e c d -> p (e c d)")[:, bass.ds(e * (2 * D) + c * D, D)]
                    mm = nc.tensor.matmul(ps[:, 6 + j % 2, 0:D], aT[:, j % 2, c * P:(c + 1) * P], w, start=(c == 0), stop=(c == 1))
                mm.then_inc(s["y_ps"], 1)

    @block.scalar
    def _(act):
        for i in range(N + 4):
            if i < N:
                act.wait_ge(s["xT_ps"], i + 1)
                if i >= 3:
                    act.wait_ge(s["h"], i - 2)
                nc.scalar.copy(xsT[:, i % 3, :], ps[:, i % 2, 0:P]).then_inc(s["xT"], 1)
            if 2 <= i < N + 2:
                j = i - 2
                act.wait_ge(s["hg"], j + 1)
                if j >= 2:
                    act.wait_ge(s["a"], j - 1)
                nc.scalar.activation(act_h[:, j % 2, :], hg[:, j % 2, 0:F], ACT.Silu).then_inc(s["act_h"], 1)
            if 4 <= i:
                j = i - 4
                act.wait_ge(s["aT_ps"], j + 1)
                if j >= 2:
                    act.wait_ge(s["y_ps"], j - 1)
                nc.scalar.copy(aT[:, j % 2, :], ps[:, 4 + j % 2, 0:2 * P]).then_inc(s["aT"], 1)
        if out is None:
            for b in range(B):
                stats.scalar_std(nc.scalar, b)

    @block.vector
    def _(dve):
        v = nc.vector
        link = chained(dve, s["chain"])
        v.memset(a[:, :, F + 1:2 * P], 0.0)
        v.memset(a[:, :, F:F + 1], 1.0)

        e = v.value_load(keep.expert[0:1, 0:1], min_val=0, max_val=E - 1)
        for i in range(N + 3):
            if i < N:
                dve.wait_ge(s["h"], i + 1)
                if i >= 2:
                    dve.wait_ge(s["a"], i - 1)
                bias = keep.b13[:, :, :, :].rearrange("p e i f -> p (e i f)")[:, bass.ds(e * (2 * F), 2 * F)]
                v.tensor_tensor(hg[:, i % 2, :], ps[:, 2 + i % 2, 0:2 * F], bias, ALU.add).then_inc(s["hg"], 1)
                if i + 1 < N:
                    e = v.value_load(keep.expert[0:1, i + 1:i + 2], min_val=0, max_val=E - 1)
            if 1 <= i <= N:
                j = i - 1
                dve.wait_ge(s["act_h"], j + 1)
                if j >= 2:
                    dve.wait_ge(s["aT_ps"], j - 1)
                v.tensor_tensor(a[:, j % 2, 0:F], act_h[:, j % 2, :], hg[:, j % 2, F:2 * F], ALU.mult).then_inc(s["a"], 1)
            if 3 <= i:
                j = i - 3
                dve.wait_ge(s["y_ps"], j + 1)
                if j >= Y_RING:
                    dve.wait_ge(sent[j % Y_RING], 16 * (j // Y_RING))
                v.tensor_scalar(y[:, j % Y_RING, :], ps[:, 6 + j % 2, 0:D], xs[:, j % XS_RING, D + 1:D + 2], None,
                                ALU.mult).then_inc(s["y"], 1)
        for b in range(B):
            dve.wait_ge(s["summed"], b + 1)
            xb = keep.x[:, b * NT:(b + 1) * NT, :]
            v.tensor_tensor(xb, back[:, b, :, 0:D], xb, ALU.add).then_inc(s["combined"], 1)
            if out is None:
                dve.wait_ge(s["combined"], b + 1)
                stats.vector_mean(v, b)
                if b:
                    stats.vector_rstd(v, b - 1)
        if out is None:
            stats.vector_rstd(v, B - 1)


def feed_forward(nc, ctx, dram, keep, tag, slots_dram, parted_dram, out=None):
    def sb(name, shape, dt=F32):
        return ctx.enter_context(nc.sbuf_tensor(tag + name, shape, dt))

    keep.rows = sb("rows", [P, TOPK, TILES, ROW])
    keep.xnT = sb("xnT", [P, B * T])
    keep.slot = sb("slot", [P, TOPK, TILES], I32)
    keep.expert = sb("expert", [P, SLOT_TILES], I32)
    keep.source = sb("source", [P, SLOT_TILES], I32)
    with ExitStack() as c:
        route_and_share(nc, c, dram, keep, tag + "r_", slots_dram)
    with ExitStack() as c:
        experts(nc, c, dram, keep, tag + "e_", slots_dram, parted_dram, out)


def state_space(nc, ctx, dram, keep):
    def sb(name, shape, dt=F32):
        return ctx.enter_context(nc.sbuf_tensor(name, shape, dt))

    xn = sb("s_xn", [P, TILES, D])
    xnT = sb("s_xnT", [P, B * T])
    hs = sb("s_hs", [P, B, T])
    ps_t = ctx.enter_context(nc.psum_tensor("s_ps_t", [P, 2, T], F32))
    ps = ctx.enter_context(nc.psum_tensor("s_ps", [P, 4, 512], F32))
    norm = Norm(nc, ctx, keep, "s_", xn, xnT, [HT + 1] * B)
    stats = Stats(nc, ctx, keep, "s_")
    s = semaphores(nc, ctx, "scan", "driven taken moved merged projected added")
    block = ctx.enter_context(nc.Block())

    def moves():
        out = []
        for up in (True, False):
            for level in (range(LEVELS) if up else reversed(range(LEVELS - 1))):
                c = 2 << level
                m = T // c
                cols = m if up else m - 1
                per = min(B, 512 // (m if m <= 512 else 512))
                tree = hs[:, :, :].rearrange("p b (m c) -> p b m c", c=c)
                for b in range(0, B, per):
                    if up:
                        src, dst = tree[:, b:b + per, :, c // 2 - 1], tree[:, b:b + per, :, c - 1]
                    else:
                        src, dst = tree[:, b:b + per, 0:cols, c - 1], tree[:, b:b + per, 1:m, c // 2 - 1]
                    out.append((level, b, per, cols, src, dst))
        return out

    plan = moves()
    needs, last_of = [], [0] * B
    for n, (_, b, per, *_) in enumerate(plan):
        needs.append(max(last_of[b:b + per]))
        for i in range(b, b + per):
            last_of[i] = n + 1

    def result(n):
        _, _, per, cols, _, _ = plan[n]
        return ps[:, n % 4, 0:per * cols].rearrange("p (b m) -> p b m", b=per)

    @block.tensor
    def _(pe):
        def drive(b):
            for n in (2 * b, 2 * b + 1):
                pe.wait_ge(norm.s["xnT"], b + 1)
                if n >= 4:
                    pe.wait_ge(s["taken"], n - 3)
                nc.tensor.matmul(ps[:, n % 4, :], keep.b_T[:, :], xnT[:, n * 512:(n + 1) * 512], start=True, stop=True).then_inc(s["driven"], 1)

        for b in range(B):
            norm.tensor_turn(nc.tensor, ps_t[:, b % 2, :], b)
            if b:
                drive(b - 1)
        drive(B - 1)
        for n, (level, b, per, cols, src, _) in enumerate(plan):
            if n < 4:
                pe.wait_ge(s["taken"], B * T // 512 - 3 + n)
            need = max(needs[n], n - 3)
            if need > 0:
                pe.wait_ge(s["merged"], need)
            nc.tensor.matmul(result(n), keep.a_powT[:, level, :], src, start=True, stop=True).then_inc(s["moved"], 1)
        pe.wait_ge(s["merged"], len(plan))
        flat = hs[:, :, :].rearrange("p b t -> p (b t)")
        for g in range(TILES // GROUP):
            if g >= 4:
                pe.wait_ge(s["added"], g - 3)
            for t in range(GROUP):
                at = (g * GROUP + t) * P
                mm = nc.tensor.matmul(ps[:, g % 4, t * P:(t + 1) * P], flat[:, at:at + P], keep.c_T[:, :], start=True, stop=True)
            mm.then_inc(s["projected"], 1)

    @block.scalar
    def _(act):
        flat = hs[:, :, :].rearrange("p b t -> p (b t)")

        def take_driven(b):
            for n in (2 * b, 2 * b + 1):
                act.wait_ge(s["driven"], n + 1)
                nc.scalar.copy(flat[:, n * 512:(n + 1) * 512], ps[:, n % 4, :]).then_inc(s["taken"], 1)

        norm.scalar_scale(nc.scalar, 0)
        for b in range(B):
            if b + 1 < B:
                norm.scalar_scale(nc.scalar, b + 1)
            norm.scalar_copy(nc.scalar, ps_t[:, b % 2, :], b)
            if b:
                take_driven(b - 1)
        take_driven(B - 1)
        for b in range(B):
            stats.scalar_std(nc.scalar, b)

    @block.vector
    def _(dve):
        v = nc.vector
        for b in range(B):
            norm.vector_scale(v, b)
        for n, (*_, dst) in enumerate(plan):
            dve.wait_ge(s["moved"], n + 1)
            if needs[n] > 0:
                dve.wait_ge(s["merged"], needs[n])
            v.tensor_tensor(dst, result(n), dst, ALU.add).then_inc(s["merged"], 1)
        for g in range(TILES // GROUP):
            dve.wait_ge(s["projected"], g + 1)
            xs = keep.x[:, g * GROUP:(g + 1) * GROUP, :]
            v.tensor_tensor(xs, ps[:, g % 4, :].rearrange("p (t d) -> p t d", t=GROUP), xs, ALU.add).then_inc(s["added"], 1)
            if g % 2:
                dve.wait_ge(s["added"], g + 1)
                stats.vector_mean(v, g // 2)
                if g >= 2:
                    stats.vector_rstd(v, g // 2 - 1)
        stats.vector_rstd(v, B - 1)


def hybrid_kernel(nc, inp, out):
    dram = inp
    keep = Keep()
    with ExitStack() as ctx:
        def sb(name, shape, dt=F32):
            return ctx.enter_context(nc.sbuf_tensor(name, shape, dt))
        keep.x = sb("x", [P, TILES, D])
        keep.ident = sb("ident", [P, P])
        keep.ones = sb("ones", [P, P])
        keep.eps = sb("eps", [P, 1])
        keep.stats, keep.mv = sb("stats", [P, TILES, 6]), sb("mv", [P, TILES, 2])
        keep.std, keep.rstd, keep.shift = (sb(n, [P, TILES]) for n in ("std", "rstd", "shift"))
        keep.a_nat, keep.a_T = sb("a_nat", [P, P]), sb("a_T", [P, P])
        keep.b_T, keep.c_T = sb("b_T", [P, P]), sb("c_T", [P, P])
        keep.a_powT = sb("a_powT", [P, LEVELS, P])
        place_weights(nc, ctx, keep)
        slots = nc.dram_tensor("slots", [SLOTS, ROW], F32).ap()
        parted = nc.dram_tensor("parted", [B * T * TOPK + 2 * E * P, D], F32).ap()
        keep.stored = ctx.enter_context(nc.semaphore("stored"))
        keep.q_parts = nc.dram_tensor("q_parts", [PARTS, P, B * T], BF16).ap()
        keep.k_parts = nc.dram_tensor("k_parts", [PARTS, P, B * T], BF16).ap()
        with ExitStack() as attn_ctx:
            keep.v = attn_ctx.enter_context(nc.sbuf_tensor("v", [P, TILES, H, HD + 1], F32))
            keep.q_stack, keep.k_stack = ([attn_ctx.enter_context(nc.sbuf_tensor(f"{n}_stack0", [SROWS, G, T], BF16))] for n in "qk")
            with ExitStack() as c:
                load_and_project(nc, c, dram, keep)
            keep.attn = attn_ctx.enter_context(nc.sbuf_tensor("attn", [P, TILES, D], F32))
            with ExitStack() as c:
                attention(nc, c, dram, keep, slots)
            with ExitStack() as c:
                project_out(nc, c, dram, keep)
        with ExitStack() as c:
            feed_forward(nc, c, dram, keep, "f1", slots, parted)
        with ExitStack() as c:
            state_space(nc, c, dram, keep)
        with ExitStack() as c:
            feed_forward(nc, c, dram, keep, "f2", slots, parted, out)


NAMES = {
    "x": "L0_attn_a_x", "w_q": "L0_attn_a_W_q", "w_dkv": "L0_attn_a_W_dkv", "w_uk": "L0_attn_a_W_uk",
    "w_uv": "L0_attn_a_W_uv", "w_o": "L0_attn_a_W_o", "ln_gamma": "L0_attn_a_ln_gamma", "ln_beta": "L0_attn_a_ln_beta",
    "w_a": "L0_attn_b_W_A", "w_b": "L0_attn_b_W_B", "w_c": "L0_attn_b_W_C",
    "gate_w": "L0_ffn_gate_w", "gate_b": "L0_ffn_gate_b", "w1": "L0_ffn_w1", "b1": "L0_ffn_b1", "w3": "L0_ffn_w3",
    "b3": "L0_ffn_b3", "w2": "L0_ffn_w2", "b2": "L0_ffn_b2", "sw1": "L0_ffn_sw1", "sb1": "L0_ffn_sb1",
    "sw3": "L0_ffn_sw3", "sb3": "L0_ffn_sb3", "sw2": "L0_ffn_sw2", "sb2": "L0_ffn_sb2",
}


def shape_constants():
    f = np.float32
    inv_freq = (f(1.0) / f(10000.0) ** (np.arange(HALF, dtype=f) / f(HALF))).astype(f)
    angles = (np.arange(T, dtype=f)[:, None] * inv_freq[None, :]).astype(f)
    spare = 2 * E * P
    rows = np.zeros((spare, ROW), f)
    rows[:, D] = (np.arange(spare, dtype=np.int32) + B * T * TOPK).view(f)
    tokens = np.arange(TILES)[None, :] * P + np.arange(P)[:, None]
    token_id = np.ascontiguousarray(np.stack([tokens * TOPK + k for k in range(TOPK)], axis=1).astype(np.int32))
    return {
        "cos": np.ascontiguousarray(np.cos(angles).astype(f).reshape(NT, P, HALF).transpose(1, 0, 2)),
        "sin": np.ascontiguousarray(np.sin(angles).astype(f).reshape(NT, P, HALF).transpose(1, 0, 2)),
        "ident": np.eye(P, dtype=f),
        "before": np.triu(np.ones((P, P), f), 1),
        "expert_no": np.arange(E, dtype=f),
        "region": np.arange(E, dtype=f) * f(REGION),
        "tile_no": np.arange(SLOT_TILES, dtype=f),
        "token_id": token_id.view(f),
        "slot_rows": rows,
    }


def kernel(**inputs):
    import concourse.bacc as bacc
    from concourse.bass_utils import run_bass_kernel_spmd

    nc = bacc.Bacc("TRN2", target_bir_lowering=False, num_devices=1)
    arrays, inp = {}, {}
    held = {short: np.ascontiguousarray(inputs[name]) for short, name in NAMES.items()}
    for short, a in {**held, **shape_constants()}.items():
        arrays[f"in_{short}"] = a
        inp[short] = nc.dram_tensor(f"in_{short}", a.shape, mybir.dt.from_np(a.dtype), kind="ExternalInput").ap()
    out = nc.dram_tensor("out", (B, T, D), F32, kind="ExternalOutput").ap()
    hybrid_kernel(nc, inp, out)
    r = run_bass_kernel_spmd(nc, [arrays], core_ids=[0])
    return r.results[0]["out"]
```
